# Optimizing a Trainium2 kernel written in Bass

```python
import numpy as np
import jax
import jax.numpy as jnp

def _softmax(x, axis=-1):
    return jax.nn.softmax(x, axis=axis)

def _gelu(x):
    return jax.nn.gelu(x, approximate=True)

def _silu(x):
    return jax.nn.silu(x)

def _sigmoid(x):
    return jax.nn.sigmoid(x)

def _layernorm(x, axis=-1, eps=1e-05):
    m = jnp.mean(x, axis=axis, keepdims=True)
    v = jnp.var(x, axis=axis, keepdims=True)
    return (x - m) / jnp.sqrt(v + eps)

def _scatter_add(tgt, idx, src, axis=0):
    return tgt.at[idx].add(src)

def _segment_sum(src, seg, n):
    return jax.ops.segment_sum(src, seg, n)
kernel_name = 'mk_gnn_preln_d4_gnn_r64_04778d'

def setup_inputs(seed: int=0):
    np.random.seed(seed)
    _w = jnp.asarray

    def _rec_inputs():
        import jax
        import jax.numpy as jnp
        _gk = jax.random.key(seed)
        x = -7.329e-05 + 0.9999 * jax.random.normal(jax.random.fold_in(_gk, 1), (10000, 512), jnp.float32)
        src = jax.random.randint(jax.random.fold_in(_gk, 2), (2500,), 0, 10000, jnp.int32)
        dst = jax.random.randint(jax.random.fold_in(_gk, 3), (2500,), 0, 10000, jnp.int32)
        _o = jnp.argsort(dst, stable=True)
        src = src[_o]
        dst = dst[_o]
        edge_attr_64 = 0.000279952 + 1.00013 * jax.random.normal(jax.random.fold_in(_gk, 12), (2500, 64), jnp.float32)
        return (x, src, dst, edge_attr_64)
    x, src, dst, edge_attr_64 = _rec_inputs()

    def _L0_gnn_setup():
        import jax, jax.numpy as jnp
        import numpy as np
        N_NODES = 100000
        N_EDGES = 25000
        IN_CH = 512
        HID_CH = 128

        def _gcn_conv(x, edge_index, W_conv, b_conv):
            N = x.shape[0]
            loop = jnp.arange(N, dtype=edge_index.dtype)
            row = jnp.concatenate([edge_index[0], loop])
            col = jnp.concatenate([edge_index[1], loop])
            ones = jnp.ones(row.shape[0], dtype=x.dtype)
            deg = jax.ops.segment_sum(ones, col, num_segments=N)
            deg_inv_sqrt = jnp.where(deg > 0, jax.lax.rsqrt(deg), 0.0)
            norm = deg_inv_sqrt[row] * deg_inv_sqrt[col]
            h = x @ W_conv
            msg = h[row] * norm[:, None]
            out = jax.ops.segment_sum(msg, col, num_segments=N)
            return out + b_conv
        key = jax.random.key(seed)
        k1, k2, k3, k4, k5, k6 = jax.random.split(key, 6)
        x = jax.random.normal(k1, (N_NODES, IN_CH), dtype=jnp.float32)
        edge_index = jax.random.randint(k2, (2, N_EDGES), 0, N_NODES, dtype=jnp.int64)
        W_conv = jax.random.normal(k3, (IN_CH, HID_CH), dtype=jnp.float32) / np.sqrt(IN_CH)
        b_conv = jnp.zeros((HID_CH,), dtype=jnp.float32)
        W_lin = jax.random.normal(k4, (HID_CH, IN_CH), dtype=jnp.float32) / np.sqrt(HID_CH)
        b_lin = jnp.zeros((IN_CH,), dtype=jnp.float32)
        return {'x': x, 'edge_index': edge_index, 'W_conv': W_conv, 'b_conv': b_conv, 'W_lin': W_lin, 'b_lin': b_lin}
    _L0_gnn_all = _L0_gnn_setup()
    _L0_gnn_in = {k: v for k, v in _L0_gnn_all.items() if k in ('W_conv', 'b_conv', 'W_lin', 'b_lin')}
    del _L0_gnn_all

    def _L1_gnn_setup():
        import jax, jax.numpy as jnp
        import numpy as np
        N_NODES = 50000
        N_EDGES = 12500
        D = 512
        N_LAYERS = 3
        EPS = 1e-12
        key = jax.random.key(seed)
        ks = jax.random.split(key, 6)
        x = jax.random.normal(ks[0], (N_NODES, D), dtype=jnp.float32)
        src = jax.random.randint(ks[1], (N_EDGES,), 0, N_NODES, dtype=jnp.int64)
        dst = jax.random.randint(ks[2], (N_EDGES,), 0, N_NODES, dtype=jnp.int64)
        scale = 1.0 / np.sqrt(D)
        W_self = jax.random.normal(ks[3], (N_LAYERS, D, D), dtype=jnp.float32) * scale
        W_neigh = jax.random.normal(ks[4], (N_LAYERS, D, D), dtype=jnp.float32) * scale
        b = jax.random.normal(ks[5], (N_LAYERS, D), dtype=jnp.float32) * 0.01
        return {'x': x, 'src': src, 'dst': dst, 'W_self': W_self, 'W_neigh': W_neigh, 'b': b}
    _L1_gnn_all = _L1_gnn_setup()
    _L1_gnn_in = {k: v for k, v in _L1_gnn_all.items() if k in ('W_self', 'W_neigh', 'b')}
    del _L1_gnn_all

    def _L2_gnn_setup():
        import jax, jax.numpy as jnp
        import numpy as np
        N_NODES = 20000
        N_EDGES = 5000
        HIDDEN = 512
        EDGE_DIM = 64
        LN_EPS = 1e-05

        def mish(x):
            return x * jnp.tanh(jax.nn.softplus(x))
        key = jax.random.key(seed)
        ks = jax.random.split(key, 8)
        s = lambda fan_in: 1.0 / np.sqrt(fan_in)
        return {'x': jax.random.normal(ks[0], (N_NODES, HIDDEN), dtype=jnp.float32), 'edge_index': jax.random.randint(ks[1], (2, N_EDGES), 0, N_NODES, dtype=jnp.int64), 'edge_attr': jax.random.normal(ks[2], (N_EDGES, EDGE_DIM), dtype=jnp.float32), 'W1': jax.random.normal(ks[3], (2 * HIDDEN + EDGE_DIM, HIDDEN), dtype=jnp.float32) * s(2 * HIDDEN + EDGE_DIM), 'b1': jnp.zeros((HIDDEN,), dtype=jnp.float32), 'W2': jax.random.normal(ks[4], (HIDDEN, HIDDEN), dtype=jnp.float32) * s(HIDDEN), 'b2': jnp.zeros((HIDDEN,), dtype=jnp.float32), 'W3': jax.random.normal(ks[5], (2 * HIDDEN, HIDDEN), dtype=jnp.float32) * s(2 * HIDDEN), 'b3': jnp.zeros((HIDDEN,), dtype=jnp.float32), 'W4': jax.random.normal(ks[6], (HIDDEN, HIDDEN), dtype=jnp.float32) * s(HIDDEN), 'b4': jnp.zeros((HIDDEN,), dtype=jnp.float32), 'gamma': jnp.ones((HIDDEN,), dtype=jnp.float32), 'beta': jnp.zeros((HIDDEN,), dtype=jnp.float32)}
    _L2_gnn_all = _L2_gnn_setup()
    _L2_gnn_in = {k: v for k, v in _L2_gnn_all.items() if k in ('W1', 'b1', 'W2', 'b2', 'W3', 'b3', 'W4', 'b4', 'gamma', 'beta')}
    del _L2_gnn_all

    def _L3_gnn_setup():
        import jax, jax.numpy as jnp
        import numpy as np
        N = 100000
        E = 12500
        D_IN = 512
        D_OUT = 512
        EPS = 1e-05
        key = jax.random.key(seed)
        k = jax.random.split(key, 7)
        x = jax.random.normal(k[0], (N, D_IN), dtype=jnp.float32)
        edge_index = jax.random.randint(k[1], (2, E), 0, N, dtype=jnp.int64)
        W_l = jax.random.normal(k[2], (D_OUT, D_IN), dtype=jnp.float32) * 0.02
        b_l = jnp.zeros((D_OUT,), dtype=jnp.float32)
        W_r = jax.random.normal(k[3], (D_OUT, D_IN), dtype=jnp.float32) * 0.02
        gamma = jnp.ones((D_OUT,), dtype=jnp.float32)
        beta = jnp.zeros((D_OUT,), dtype=jnp.float32)
        return {'x': x, 'edge_index': edge_index, 'W_l': W_l, 'b_l': b_l, 'W_r': W_r, 'gamma': gamma, 'beta': beta}
    _L3_gnn_all = _L3_gnn_setup()
    _L3_gnn_in = {k: v for k, v in _L3_gnn_all.items() if k in ('W_l', 'b_l', 'W_r', 'gamma', 'beta')}
    del _L3_gnn_all
    return {'x': x, 'src': src, 'dst': dst, 'edge_attr_64': edge_attr_64, 'L0_gnn_W_conv': _L0_gnn_in['W_conv'], 'L0_gnn_b_conv': _L0_gnn_in['b_conv'], 'L0_gnn_W_lin': _L0_gnn_in['W_lin'], 'L0_gnn_b_lin': _L0_gnn_in['b_lin'], 'L1_gnn_W_self': _L1_gnn_in['W_self'], 'L1_gnn_W_neigh': _L1_gnn_in['W_neigh'], 'L1_gnn_b': _L1_gnn_in['b'], 'L2_gnn_W1': _L2_gnn_in['W1'], 'L2_gnn_b1': _L2_gnn_in['b1'], 'L2_gnn_W2': _L2_gnn_in['W2'], 'L2_gnn_b2': _L2_gnn_in['b2'], 'L2_gnn_W3': _L2_gnn_in['W3'], 'L2_gnn_b3': _L2_gnn_in['b3'], 'L2_gnn_W4': _L2_gnn_in['W4'], 'L2_gnn_b4': _L2_gnn_in['b4'], 'L2_gnn_gamma': _L2_gnn_in['gamma'], 'L2_gnn_beta': _L2_gnn_in['beta'], 'L3_gnn_W_l': _L3_gnn_in['W_l'], 'L3_gnn_b_l': _L3_gnn_in['b_l'], 'L3_gnn_W_r': _L3_gnn_in['W_r'], 'L3_gnn_gamma': _L3_gnn_in['gamma'], 'L3_gnn_beta': _L3_gnn_in['beta']}

def reference(x, src, dst, edge_attr_64, L0_gnn_W_conv, L0_gnn_b_conv, L0_gnn_W_lin, L0_gnn_b_lin, L1_gnn_W_self, L1_gnn_W_neigh, L1_gnn_b, L2_gnn_W1, L2_gnn_b1, L2_gnn_W2, L2_gnn_b2, L2_gnn_W3, L2_gnn_b3, L2_gnn_W4, L2_gnn_b4, L2_gnn_gamma, L2_gnn_beta, L3_gnn_W_l, L3_gnn_b_l, L3_gnn_W_r, L3_gnn_gamma, L3_gnn_beta):
    import jax
    import jax.numpy as jnp

    def _L0_gnn_ref(x, edge_index, W_conv, b_conv, W_lin, b_lin):
        import jax, jax.numpy as jnp
        import numpy as np
        N_NODES = 100000
        N_EDGES = 25000
        IN_CH = 512
        HID_CH = 128

        def _gcn_conv(x, edge_index, W_conv, b_conv):
            N = x.shape[0]
            loop = jnp.arange(N, dtype=edge_index.dtype)
            row = jnp.concatenate([edge_index[0], loop])
            col = jnp.concatenate([edge_index[1], loop])
            ones = jnp.ones(row.shape[0], dtype=x.dtype)
            deg = jax.ops.segment_sum(ones, col, num_segments=N)
            deg_inv_sqrt = jnp.where(deg > 0, jax.lax.rsqrt(deg), 0.0)
            norm = deg_inv_sqrt[row] * deg_inv_sqrt[col]
            h = x @ W_conv
            msg = h[row] * norm[:, None]
            out = jax.ops.segment_sum(msg, col, num_segments=N)
            return out + b_conv
        h = _gcn_conv(x, edge_index, W_conv, b_conv)
        return h @ W_lin + b_lin

    def _L1_gnn_ref(x, src, dst, W_self, W_neigh, b):
        import jax, jax.numpy as jnp
        import numpy as np
        N_NODES = 50000
        N_EDGES = 12500
        D = 512
        N_LAYERS = 3
        EPS = 1e-12
        n = x.shape[0]
        deg = jax.ops.segment_sum(jnp.ones_like(dst, dtype=x.dtype), dst, num_segments=n)
        deg = jnp.maximum(deg, 1.0)[:, None]
        h = x
        for l in range(N_LAYERS):
            h_neigh = jax.ops.segment_sum(h[src], dst, num_segments=n) / deg
            rst = h @ W_self[l] + h_neigh @ W_neigh[l] + b[l]
            rst = jax.nn.relu(rst)
            nrm = jnp.sqrt(jnp.sum(rst * rst, axis=-1, keepdims=True))
            h = rst / jnp.maximum(nrm, EPS)
        return h

    def _L2_gnn_ref(x, edge_index, edge_attr, W1, b1, W2, b2, W3, b3, W4, b4, gamma, beta):
        import jax, jax.numpy as jnp
        import numpy as np
        N_NODES = 20000
        N_EDGES = 5000
        HIDDEN = 512
        EDGE_DIM = 64
        LN_EPS = 1e-05

        def mish(x):
            return x * jnp.tanh(jax.nn.softplus(x))
        src, dst = (edge_index[0], edge_index[1])
        edge_feat = jnp.concatenate([x[src], x[dst], edge_attr], axis=-1)
        h = mish(edge_feat @ W1 + b1)
        messages = mish(h @ W2 + b2)
        agg = jax.ops.segment_sum(messages, dst, num_segments=x.shape[0])
        u = mish(jnp.concatenate([x, agg], axis=-1) @ W3 + b3)
        out = u @ W4 + b4
        y = x + out
        mu = jnp.mean(y, axis=-1, keepdims=True)
        var = jnp.mean(jnp.square(y - mu), axis=-1, keepdims=True)
        return (y - mu) * jax.lax.rsqrt(var + LN_EPS) * gamma + beta

    def _L3_gnn_ref(x, edge_index, W_l, b_l, W_r, gamma, beta):
        import jax, jax.numpy as jnp
        import numpy as np
        N = 100000
        E = 12500
        D_IN = 512
        D_OUT = 512
        EPS = 1e-05
        n = x.shape[0]
        src, dst = (edge_index[0], edge_index[1])
        summed = jax.ops.segment_sum(x[src], dst, num_segments=n)
        cnt = jax.ops.segment_sum(jnp.ones((src.shape[0],), x.dtype), dst, num_segments=n)
        aggr = summed / jnp.maximum(cnt, 1.0)[:, None]
        h = aggr @ W_l.T + b_l + x @ W_r.T
        mu = jnp.mean(h, axis=0)
        var = jnp.mean(jnp.square(h - mu), axis=0)
        h_norm = (h - mu) * jax.lax.rsqrt(var + EPS) * gamma + beta
        return jax.nn.relu(h_norm)
    edge_index = jnp.stack([src, dst])
    h = jnp.maximum(_layernorm(x, axis=-1), 0.0)
    x = x + _L0_gnn_ref(h, edge_index, L0_gnn_W_conv, L0_gnn_b_conv, L0_gnn_W_lin, L0_gnn_b_lin)
    h = jnp.maximum(_layernorm(x, axis=-1), 0.0)
    x = x + _L1_gnn_ref(h, src, dst, L1_gnn_W_self, L1_gnn_W_neigh, L1_gnn_b)
    h = jnp.maximum(_layernorm(x, axis=-1), 0.0)
    x = x + _L2_gnn_ref(h, edge_index, edge_attr_64, L2_gnn_W1, L2_gnn_b1, L2_gnn_W2, L2_gnn_b2, L2_gnn_W3, L2_gnn_b3, L2_gnn_W4, L2_gnn_b4, L2_gnn_gamma, L2_gnn_beta)
    h = jnp.maximum(_layernorm(x, axis=-1), 0.0)
    x = x + _L3_gnn_ref(h, edge_index, L3_gnn_W_l, L3_gnn_b_l, L3_gnn_W_r, L3_gnn_gamma, L3_gnn_beta)
    return x

_drawn_inputs = setup_inputs


def setup_inputs(seed=0):
    import zlib

    import numpy as np

    out = dict(_drawn_inputs(seed))
    spreads = {'L0_gnn_b_conv': (0.0, 0.1),
     'L0_gnn_b_lin': (0.0, 0.1),
     'L2_gnn_b1': (0.0, 0.8),
     'L2_gnn_b2': (0.0, 0.707),
     'L2_gnn_b3': (0.0, 0.1),
     'L2_gnn_b4': (0.0, 0.1),
     'L2_gnn_gamma': (1.0, 0.2),
     'L2_gnn_beta': (0.0, 0.1),
     'L3_gnn_b_l': (0.0, 0.8),
     'L3_gnn_gamma': (1.0, 0.2),
     'L3_gnn_beta': (0.0, 0.1)}
    factors = {'edge_attr_64': 3.319, 'L1_gnn_W_neigh': 4.264, 'L1_gnn_b': 5.299}
    for name, (base, spread) in spreads.items():
        noise = np.random.default_rng([zlib.crc32(name.encode()), seed]).standard_normal(out[name].shape)
        drawn = base * np.exp(spread * noise) if base else spread * noise
        out[name] = jnp.asarray(drawn.astype(out[name].dtype))
    for name, factor in factors.items():
        out[name] = (out[name] * factor).astype(out[name].dtype)
    return out
```

```python
from contextlib import ExitStack

import concourse.bass as bass
from concourse import mybir

P = 128
F32 = mybir.dt.float32
F16 = mybir.dt.float16
I32 = mybir.dt.int32
ALU = mybir.AluOpType
ACT = mybir.ActivationFunctionType
AX = mybir.AxisListType
ADD, SUB, MUL, MAX, MIN, POW = ALU.add, ALU.subtract, ALU.mult, ALU.max, ALU.min, ALU.pow

N, D, E, ED, HID = 10000, 512, 2500, 64, 128
C = D // P
NT = -(-N // P)
TAIL = N - (NT - 1) * P
NPAD = NT * P
EPT = P - 1
ET = -(-E // EPT)
EQ = 20
EP = E // EQ
assert EP * EQ == E and EP <= P
NOWHERE = 2 * N
LN_EPS, NORM_EPS, BN_EPS = 1e-5, 1e-12, 1e-5
PEEL = 6
SCALE_LN = 2.0 ** 11
SCALE_UNIT = 2.0 ** 15
MISH_CAP = 20.0


def wait_count(eng, sem, n):
    if not isinstance(n, int) or n > 0:
        eng.wait_ge(sem, n)


def each_tile(eng, n, body):
    for t in range(PEEL):
        body(t, t // 2, t % 2)
    with eng.Fori(PEEL // 2, n // 2) as i:
        body(2 * i, i, 0)
        body(2 * i + 1, i, 1)
    if n % 2:
        body(n - 1, n // 2, 0)


def ago(n, t, k, b):
    for _ in range(n):
        t, k, b = t - 1, (k if b else k - 1), 1 - b
    return t, k, b


def started(n, t):
    return not isinstance(t, int) or t >= n


def last(n, lag):
    return [(t, t // 2, t % 2) for t in range(n - lag, n)]


def gnn_program(nc, x, src, dst, edge_attr, Wc, bc, Wlin, blin, Wself, Wneigh, bsage, W1, b1, W2, b2,
                W3, b3, W4, b4, gamma2, beta2, WlT, bl, WrT, gamma3, beta3, out):
    top = ExitStack()

    def dram(name, shape, dt=F32):
        return nc.dram_tensor(name, shape, dt, kind="Internal").ap()

    hw_d = dram("hw_rows", [NPAD, HID])
    gcn_d = dram("gcn_sums", [NPAD, HID])
    agg_d = dram("neighbour_rows", [NPAD, D])
    x1_d = dram("x1_rows", [NPAD, D])
    x2_d = dram("x2_rows", [NPAD, D])
    x3_d = dram("x3_rows", [NPAD, D])
    h_d = dram("sage_rows", [NPAD, D])
    msg_d = dram("message_rows", [ET * P, D])
    rec_d = dram("edge_records", [ET * P, 8])
    cnt_d = dram("in_degree", [NPAD, 1])
    sel_d = dram("selections", [P, ET * 2 * P])

    units = {"conv": (Wc, 1), **{f"self{l}": (Wself[l], 1) for l in range(3)},
             **{f"neigh{l}": (Wneigh[l], 1) for l in range(3)},
             "edge": (W1[0:2 * D, :], 2), "update": (W3[0:D, :], 1), "aggr": (WlT, 1), "root": (WrT, 1)}
    unit_no = {name: n for n, name in enumerate(units)}
    cols = {name: w.shape[0] // P * w.shape[1] for name, (w, _) in units.items()}
    split_d = {name: dram(f"split_{name}", [P, 2 * cols[name]], F16) for name in units}
    NU = len(units)

    def sb(ctx, name, shape, dt=F32):
        return ctx.enter_context(nc.sbuf_tensor(name, shape, dt))

    def ps(ctx, name, shape=(P, D)):
        return ctx.enter_context(nc.psum_tensor(name, list(shape), F32))

    taken = []

    def sem(name):
        taken.append(nc.alloc_semaphore(name))
        return taken[-1]

    def sems(phase, names):
        return [sem(f"{phase}_{n}") for n in names.split()]

    def pair(phase, name):
        return [sem(f"{phase}_{name}{b}") for b in range(2)]

    def recycle_semaphores():
        nc.clear_and_free_semaphores(taken)
        taken.clear()
        nc.all_engine_barrier()

    slots = sb(top, "slots", [P, NT * D])
    ident = sb(top, "ident", [P, P])
    dis = sb(top, "dis", [P, NT])
    src_i = sb(top, "src_i", [P, ET], I32)
    dst_i = sb(top, "dst_i", [P, ET], I32)
    put_i = sb(top, "put_i", [P, ET], I32)
    edge_i = sb(top, "edge_i", [P, ET], I32)
    up = sb(top, "up", [P, NU])
    down = sb(top, "down", [P, NU])
    eps_col = sb(top, "eps_col", [P, 1])
    minus_half = sb(top, "minus_half", [P, 1])
    minus_one = sb(top, "minus_one", [P, 1])
    slots16 = slots[:, :].bitcast(F16)

    def slot(t):
        return slots[:, bass.ds(t * D, D)]

    def slot_hi(t):
        return slots16[:, bass.ds(t * 2 * D, D)]

    def slot_lo(t):
        return slots16[:, bass.ds(t * 2 * D + D, D)]

    def rows_of(t):
        return TAIL if isinstance(t, int) and t == NT - 1 else P

    def rows(ap, t):
        return ap[bass.ds(t * P, rows_of(t)), :]

    def wide(vec):
        return vec.rearrange("(o d) -> o d", o=1).to_broadcast([P, vec.shape[0]])

    def product(pe, out_ap, hi, lo, w, n, nchunks=C, first=True, stop=True):
        size = nchunks * n
        ins = None
        for c in range(nchunks):
            for m, (a, part) in enumerate(((hi, 0), (hi, 1), (lo, 0))):
                ins = nc.tensor.matmul(out_ap, a(c), w[:, part * size + c * n:part * size + (c + 1) * n],
                                       start=first and c == 0 and m == 0,
                                       stop=stop and c == nchunks - 1 and m == 2)
        return ins

    def transposes(pe, out_ap, in_ap):
        for c in range(C):
            ins = nc.tensor.transpose(out_ap[:, c * P:(c + 1) * P], in_ap[:, c * P:(c + 1) * P], ident[:, :])
        return ins

    def prepare_weights():
        with ExitStack() as ctx:
            mx = sb(ctx, "w_mx", [P, NU])
            mxa = sb(ctx, "w_mxa", [P, NU])
            ex = sb(ctx, "w_ex", [P, NU], I32)
            fld = sb(ctx, "w_fld", [P, NU], I32)
            inv = sb(ctx, "w_inv", [P, NU], I32)
            parts = [sb(ctx, f"w_parts{b}", [P, 2 * 2 * C * D], F16) for b in range(2)]
            zid, made, s_max, s_all, s_exp, s_up, s_hi, s_lo = sems("w", "zid made max all exp up hi lo")
            loaded = [sem(f"w_in{n}") for n in range(NU)]
            stored = pair("w", "out")
            base, at = {}, 0
            for name in units:
                base[name] = at
                at += cols[name]
            assert at <= NT * D
            block = ctx.enter_context(nc.Block())

            def raw(name):
                return slots[:, base[name]:base[name] + cols[name]]

            @block.sync
            def _(sp):
                for n, (name, (w, _)) in enumerate(units.items()):
                    sp.dma_start(raw(name).rearrange("p (c m) -> p c m", m=w.shape[1]),
                                 w.rearrange("(c p) m -> p c m", p=P)).then_inc(loaded[n], 16)
                for n, name in enumerate(units):
                    sp.wait_ge(s_lo, n + 1)
                    sp.dma_start(split_d[name][:, :], parts[n % 2][:, 0:2 * cols[name]]).then_inc(
                        stored[n % 2], 16)
                for b in range(2):
                    sp.wait_ge(stored[b], 16 * ((NU + 1 - b) // 2))

            @block.gpsimd
            def _(pool):
                nc.gpsimd.memset(ident[:, :], 0.0).then_inc(zid, 1)
                nc.gpsimd.memset(eps_col[:, :], LN_EPS)
                nc.gpsimd.memset(minus_half[:, :], -0.5)
                nc.gpsimd.memset(minus_one[:, :], -1.0)
                pool.wait_ge(zid, 1)
                nc.gpsimd.affine_select(out=ident[:, :], in_=ident[:, :], compare_op=ALU.not_equal, fill=1.0,
                                        base=0, pattern=[[-1, P]], channel_multiplier=1).then_inc(made, 1)
                pool.wait_ge(s_max, NU)
                nc.gpsimd.partition_all_reduce(mxa[:, :], mx[:, :], P, bass.bass_isa.ReduceOp.max).then_inc(s_all, 1)
                pool.wait_ge(made, 1)

            @block.vector
            def _(dve):
                for n, name in enumerate(units):
                    dve.wait_ge(loaded[n], 16)
                    nc.vector.tensor_reduce(out=mx[:, n:n + 1], in_=raw(name), op=MAX, axis=AX.X,
                                            apply_absolute_value=True).then_inc(s_max, 1)
                dve.wait_ge(s_all, 1)
                nc.vector.tensor_scalar(out=ex[:, :], in0=mxa[:, :].bitcast(I32), scalar1=23, scalar2=None,
                                        op0=ALU.logical_shift_right).then_inc(s_exp, 1)
                dve.wait_ge(s_exp, 1)
                nc.vector.tensor_scalar(out=fld[:, :], in0=ex[:, :], scalar1=-1.0, scalar2=268.0,
                                        op0=MUL, op1=ADD).then_inc(s_exp, 1)
                dve.wait_ge(s_exp, 2)
                nc.vector.tensor_scalar(out=ex[:, :], in0=fld[:, :], scalar1=253.0, scalar2=1.0,
                                        op0=MIN, op1=MAX).then_inc(s_exp, 1)
                dve.wait_ge(s_exp, 3)
                nc.vector.tensor_scalar(out=inv[:, :], in0=ex[:, :], scalar1=-1.0, scalar2=254.0,
                                        op0=MUL, op1=ADD).then_inc(s_exp, 1)
                nc.vector.tensor_scalar(out=up[:, :].bitcast(I32), in0=ex[:, :], scalar1=23, scalar2=None,
                                        op0=ALU.logical_shift_left).then_inc(s_up, 1)
                dve.wait_ge(s_exp, 4)
                nc.vector.tensor_scalar(out=down[:, :].bitcast(I32), in0=inv[:, :], scalar1=23, scalar2=None,
                                        op0=ALU.logical_shift_left).then_inc(s_up, 1)
                dve.wait_ge(s_up, 2)
                for n, name in enumerate(units):
                    dve.wait_ge(s_hi, n + 1)
                    m = cols[name]
                    nc.vector.scalar_tensor_tensor(out=parts[n % 2][:, m:2 * m], in0=raw(name),
                                                   scalar=up[:, n:n + 1], in1=parts[n % 2][:, 0:m],
                                                   op0=MUL, op1=SUB).then_inc(s_lo, 1)

            @block.scalar
            def _(act):
                act.wait_ge(s_up, 2)
                for n, name in enumerate(units):
                    wait_count(act, stored[n % 2], 16 * (n // 2))
                    nc.scalar.activation(parts[n % 2][:, 0:cols[name]], raw(name), ACT.Copy,
                                         scale=up[:, n:n + 1]).then_inc(s_hi, 1)

    def prepare_graph():
        with ExitStack() as ctx:
            ZW = NT * D // 8
            zeros = sb(ctx, "g_zeros", [P, ZW])
            row_i = sb(ctx, "g_row_i", [P, E], I32)
            row_f = slots[:, 0:E]
            number = slots[:, E:2 * E]
            same = slots[:, 2 * E:3 * E]
            junk = slots[:, 3 * E:4 * E]
            junk2 = slots[:, 4 * E:5 * E]
            col_i = sb(ctx, "g_col_i", [P, EQ], I32)
            scol_i = sb(ctx, "g_scol_i", [P, EQ], I32)
            col_f = sb(ctx, "g_col_f", [P, EQ])
            neg_f = sb(ctx, "g_neg_f", [P, EQ])
            mine = sb(ctx, "g_mine", [P, EQ])
            sign = sb(ctx, "g_sign", [P, EQ])
            equal = sb(ctx, "g_equal", [P, EQ])
            before = sb(ctx, "g_before", [P, EQ])
            start = sb(ctx, "g_start", [P, EQ])
            rank = sb(ctx, "g_rank", [P, EQ])
            whole = [sb(ctx, f"g_whole{b}", [P, EQ]) for b in range(2)]
            put_f = sb(ctx, "g_put_f", [P, EQ])
            is_last = sb(ctx, "g_is_last", [P, EQ])
            put_u = sb(ctx, "g_put_u", [P, EQ], I32)
            pos_u = sb(ctx, "g_pos_u", [P, EQ], I32)
            rec = sb(ctx, "g_rec", [P, EQ, 8])
            blank = sb(ctx, "g_blank", [P, ET, 8])
            recs = sb(ctx, "g_recs", [P, ET, 8])
            offs = sb(ctx, "g_offs", [P, ET])
            first_j = sb(ctx, "g_first_j", [P, ET])
            jrow = sb(ctx, "g_jrow", [P, P])
            tri = sb(ctx, "g_tri", [P, P])
            selT = [sb(ctx, f"g_selT{b}", [P, 2 * P]) for b in range(2)]
            sel = slots[:, 5 * E:5 * E + ET * 2 * P]
            cnt = sb(ctx, "g_cnt", [P, P])
            deg = sb(ctx, "g_deg", [P, NT])
            half = sb(ctx, "g_half", [P, NT])
            ps_sel = [ps(ctx, f"g_ps_sel{b}") for b in range(2)]
            ps_cnt = ps(ctx, "g_ps_cnt")
            (s_in, s_zero, s_made, s_cast, s_eq, s_sign, s_bef, s_col, s_ready, s_blank, s_rec, s_cntin,
             s_recs, s_put, s_selT, s_turn, s_sel, s_selout, s_cload, s_cT, s_deg, s_dis) = sems(
                "g", "in zero made cast eq sign bef col ready blank rec cntin recs put selT turn sel "
                "selout cload cT deg dis")
            block = ctx.enter_context(nc.Block())

            @block.sync
            def _(sp):
                sp.dma_start(row_i[:, :], wide(dst)).then_inc(s_in, 16)
                sp.dma_start(col_i[0:EP, :], dst.rearrange("(p q) -> p q", q=EQ)).then_inc(s_in, 16)
                sp.dma_start(scol_i[0:EP, :], src.rearrange("(p q) -> p q", q=EQ)).then_inc(s_in, 16)
                sp.wait_ge(s_made, 1)
                agg_v = agg_d.rearrange("(p a) d -> p (a d)", p=P)
                gcn_v = gcn_d.rearrange("(p a) d -> p (a d)", p=P)
                for q in range(8):
                    sp.dma_start(agg_v[:, q * ZW:(q + 1) * ZW], zeros[:, :]).then_inc(s_zero, 16)
                for q in range(2):
                    sp.dma_start(gcn_v[:, q * ZW:(q + 1) * ZW], zeros[:, :]).then_inc(s_zero, 16)
                sp.dma_start(cnt_d.rearrange("(p a) o -> p (a o)", p=P), zeros[:, 0:NT]).then_inc(s_blank, 16)
                sp.dma_start(rec_d.rearrange("(p a) f -> p a f", p=P), blank[:, :, :]).then_inc(s_blank, 16)
                sp.wait_ge(s_rec, 16 * EQ)
                sp.dma_start(recs[:, :, :], rec_d.rearrange("(t p) f -> p t f", p=P)).then_inc(s_recs, 16)
                sp.wait_ge(s_cntin, 16 * EQ)
                sp.dma_start(cnt[0:NT, :], cnt_d.rearrange("(t p) o -> t (p o)", p=P)).then_inc(s_cload, 16)
                sp.wait_ge(s_sel, ET)
                sp.dma_start(sel_d[:, :], sel).then_inc(s_selout, 16)
                sp.wait_ge(s_selout, 16)
                sp.wait_ge(s_zero, 160)

            @block.gpsimd
            def _(pool):
                nc.gpsimd.iota(number, pattern=[[1, E]], base=0, channel_multiplier=0,
                               allow_small_or_imprecise_dtypes=True).then_inc(s_col, 1)
                nc.gpsimd.iota(mine[:, :], pattern=[[1, EQ]], base=0, channel_multiplier=EQ,
                               allow_small_or_imprecise_dtypes=True).then_inc(s_col, 1)
                nc.gpsimd.iota(offs[:, :], pattern=[[EPT, ET]], base=-1, channel_multiplier=0,
                               allow_small_or_imprecise_dtypes=True).then_inc(s_col, 1)
                nc.gpsimd.iota(jrow[:, :], pattern=[[1, P]], base=0, channel_multiplier=0,
                               allow_small_or_imprecise_dtypes=True).then_inc(s_col, 1)
                nc.gpsimd.memset(tri[:, :], 1.0).then_inc(s_col, 1)
                nc.gpsimd.memset(half[:, :], -0.5).then_inc(s_col, 1)
                pool.wait_ge(s_col, 6)
                nc.gpsimd.affine_select(out=tri[:, :], in_=tri[:, :], compare_op=ALU.is_ge, fill=0.0, base=0,
                                        pattern=[[-1, P]], channel_multiplier=1).then_inc(s_col, 1)
                pool.wait_ge(s_blank, 32)
                pool.wait_ge(s_ready, 1)
                for q in range(EQ):
                    nc.gpsimd.indirect_dma_start(
                        rec_d[:, :], bass.IndirectOffsetOnAxis(ap=pos_u[0:EP, q:q + 1], axis=0),
                        rec[0:EP, q, :], None).then_inc(s_rec, 16)
                for q in range(EQ):
                    nc.gpsimd.indirect_dma_start(
                        cnt_d[:, :], bass.IndirectOffsetOnAxis(ap=put_u[0:EP, q:q + 1], axis=0),
                        equal[0:EP, q:q + 1], None, bounds_check=N - 1, oob_is_err=False).then_inc(s_cntin, 16)
                pool.wait_ge(s_deg, 1)
                nc.gpsimd.tensor_tensor(out=dis[:, :], in0=deg[:, :], in1=half[:, :], op=POW).then_inc(s_dis, 1)
                pool.wait_ge(s_dis, 1)

            @block.scalar
            def _(act):
                act.wait_ge(s_cast, 4)
                for q in range(EQ):
                    nc.scalar.activation(junk2[0:EP, :], row_f[0:EP, :], ACT.Sign, bias=neg_f[0:EP, q:q + 1],
                                         accum_out=sign[0:EP, q:q + 1]).then_inc(s_sign, 1)
                    act.wait_ge(s_sign, q + 1)
                for t in range(ET):
                    act.wait_ge(s_turn, t + 1)
                    nc.scalar.activation(sel[:, t * 2 * P:(t + 1) * 2 * P], ps_sel[t % 2][:, 0:2 * P],
                                         ACT.Copy).then_inc(s_sel, 1)

            @block.vector
            def _(dve):
                chain = s_put
                links = [0]

                def link(ins):
                    links[0] += 1
                    ins.then_inc(chain, 1)
                    dve.wait_ge(chain, links[0])

                nc.vector.memset(zeros[:, :], 0.0)
                nc.vector.memset(slot(NT - 1), 0.0)
                link(nc.vector.memset(blank[:, :, :], 0.0))
                nc.vector.memset(blank[:, :, 2], float(NOWHERE))
                nc.vector.memset(blank[:, :, 3], 1e6)
                link(nc.vector.memset(rec[:, :, :], 0.0))
                nc.vector.memset(cnt[:, :], 0.0).then_inc(s_made, 1)
                dve.wait_ge(s_in, 48)
                nc.vector.tensor_copy(row_f, row_i[:, :]).then_inc(s_cast, 1)
                nc.vector.tensor_copy(col_f[0:EP, :], col_i[0:EP, :]).then_inc(s_cast, 1)
                nc.vector.tensor_copy(rec[0:EP, :, 0], scol_i[0:EP, :]).then_inc(s_cast, 1)
                dve.wait_ge(s_cast, 3)
                nc.vector.tensor_scalar(out=neg_f[0:EP, :], in0=col_f[0:EP, :], scalar1=-1.0, scalar2=None,
                                        op0=MUL).then_inc(s_cast, 1)
                dve.wait_ge(s_col, 2)
                for q in range(EQ):
                    link(nc.vector.tensor_scalar(out=same[0:EP, :], in0=row_f[0:EP, :],
                                                 scalar1=col_f[0:EP, q:q + 1], scalar2=0.0, op0=ALU.is_equal,
                                                 op1=ADD, accum_out=equal[0:EP, q:q + 1]))
                    link(nc.vector.scalar_tensor_tensor(out=junk[0:EP, :], in0=number[0:EP, :],
                                                        scalar=mine[0:EP, q:q + 1], in1=same[0:EP, :],
                                                        op0=ALU.is_lt, op1=MUL,
                                                        accum_out=before[0:EP, q:q + 1]))
                dve.wait_ge(s_sign, EQ)
                a = slice(0, EP)
                link(nc.vector.tensor_tensor(out=start[a, :], in0=equal[a, :], in1=sign[a, :], op=ADD))
                link(nc.vector.tensor_scalar(out=start[a, :], in0=start[a, :], scalar1=-0.5, scalar2=0.5 * E,
                                             op0=MUL, op1=ADD))
                link(nc.vector.tensor_tensor(out=rank[a, :], in0=start[a, :], in1=before[a, :], op=ADD))
                link(nc.vector.tensor_scalar(out=whole[0][a, :], in0=rank[a, :], scalar1=1.0, scalar2=None, op0=ADD))
                for n in range(1, ET):
                    link(nc.vector.scalar_tensor_tensor(out=whole[n % 2][a, :], in0=rank[a, :],
                                                        scalar=float(n * EPT), in1=whole[(n - 1) % 2][a, :],
                                                        op0=ALU.is_ge, op1=ADD))
                link(nc.vector.tensor_copy(pos_u[a, :], whole[(ET - 1) % 2][a, :]))
                link(nc.vector.tensor_tensor(out=is_last[a, :], in0=equal[a, :], in1=before[a, :], op=SUB))
                link(nc.vector.tensor_scalar(out=is_last[a, :], in0=is_last[a, :], scalar1=1.0, scalar2=None,
                                             op0=ALU.is_equal))
                link(nc.vector.scalar_tensor_tensor(out=put_f[a, :], in0=col_f[a, :], scalar=-float(NOWHERE),
                                                    in1=is_last[a, :], op0=ADD, op1=MUL))
                link(nc.vector.tensor_scalar(out=rec[a, :, 2], in0=put_f[a, :], scalar1=float(NOWHERE),
                                             scalar2=None, op0=ADD))
                link(nc.vector.tensor_copy(put_u[a, :], rec[a, :, 2]))
                link(nc.vector.tensor_copy(rec[a, :, 1], col_f[a, :]))
                link(nc.vector.tensor_copy(rec[a, :, 3], start[a, :]))
                link(nc.vector.reciprocal(rec[a, :, 4], equal[a, :]))
                nc.vector.tensor_copy(rec[a, :, 5], mine[a, :]).then_inc(s_ready, 1)
                dve.wait_ge(s_recs, 16)
                nc.vector.tensor_copy(src_i[:, :], recs[:, :, 0])
                nc.vector.tensor_copy(dst_i[:, :], recs[:, :, 1])
                nc.vector.tensor_copy(put_i[:, :], recs[:, :, 2])
                nc.vector.tensor_copy(edge_i[:, :], recs[:, :, 5])
                dve.wait_ge(s_col, 7)
                link(nc.vector.tensor_tensor(out=first_j[:, :], in0=recs[:, :, 3], in1=offs[:, :], op=SUB))
                for t in range(ET):
                    wait_count(dve, s_turn, t - 1)
                    link(nc.vector.scalar_tensor_tensor(out=selT[t % 2][:, 0:P], in0=jrow[:, :],
                                                        scalar=first_j[:, t:t + 1], in1=tri[:, :],
                                                        op0=ALU.is_ge, op1=MUL))
                    nc.vector.tensor_scalar(out=selT[t % 2][:, P:2 * P], in0=selT[t % 2][:, 0:P],
                                            scalar1=recs[:, t, 4:5], scalar2=None, op0=MUL).then_inc(s_selT, 1)
                dve.wait_ge(s_cT, 1)
                nc.vector.tensor_scalar(out=deg[:, :], in0=ps_cnt[:, 0:NT], scalar1=1.0, scalar2=None,
                                        op0=ADD).then_inc(s_deg, 1)

            @block.tensor
            def _(pe):
                for t in range(ET):
                    pe.wait_ge(s_selT, t + 1)
                    wait_count(pe, s_sel, t - 1)
                    nc.tensor.transpose(ps_sel[t % 2][:, 0:P], selT[t % 2][:, 0:P], ident[:, :])
                    nc.tensor.transpose(ps_sel[t % 2][:, P:2 * P], selT[t % 2][:, P:2 * P],
                                        ident[:, :]).then_inc(s_turn, 1)
                pe.wait_ge(s_cload, 16)
                nc.tensor.transpose(ps_cnt[:, 0:P], cnt[:, :], ident[:, :]).then_inc(s_cT, 1)

    class Norm:
        def __init__(self, ctx, name):
            self.stats = [sb(ctx, f"{name}_st{b}", [P, 6]) for b in range(2)]
            self.mv = [sb(ctx, f"{name}_mv{b}", [P, 2]) for b in range(2)]
            self.ve = [sb(ctx, f"{name}_ve{b}", [P, 1]) for b in range(2)]
            self.rstd = [sb(ctx, f"{name}_rs{b}", [P, 1]) for b in range(2)]
            self.shift = [sb(ctx, f"{name}_sh{b}", [P, 1]) for b in range(2)]
            self.pause = sb(ctx, f"{name}_pause", [P, 1])
            self.nm = [sb(ctx, f"{name}_nm{b}", [P, 1]) for b in range(2)]
            self.s_stats, self.s_mv, self.s_ve, self.s_rstd, self.s_ready = sems(
                name, "stats mv ve rstd ready")

        def on_vector(self, dve, in_ap, t, b):
            nc.vector.bn_stats(self.stats[b][:, :], in_ap).then_inc(self.s_stats, 1)
            dve.wait_ge(self.s_stats, t + 1)
            wait_count(dve, self.s_ready, t - 1)
            nc.vector.memset(self.pause[:, :], 0.0)
            nc.vector.bn_aggr(self.mv[b][:, :], self.stats[b][:, :]).then_inc(self.s_mv, 1)

        def on_pool(self, pool, t, b, free=()):
            pool.wait_ge(self.s_mv, t + 1)
            nc.gpsimd.tensor_tensor(out=self.nm[b][:, :], in0=self.mv[b][:, 0:1], in1=minus_one[:, :], op=MUL)
            nc.gpsimd.tensor_tensor(out=self.ve[b][:, :], in0=self.mv[b][:, 1:2], in1=eps_col[:, :],
                                    op=ADD).then_inc(self.s_ve, 1)
            pool.wait_ge(self.s_ve, t + 1)
            for s, n in free:
                wait_count(pool, s, n)
            nc.gpsimd.tensor_tensor(out=self.rstd[b][:, :], in0=self.ve[b][:, :], in1=minus_half[:, :],
                                    op=POW).then_inc(self.s_rstd, 1)
            pool.wait_ge(self.s_rstd, t + 1)
            nc.gpsimd.tensor_tensor(out=self.shift[b][:, :], in0=self.nm[b][:, :], in1=self.rstd[b][:, :],
                                    op=MUL).then_inc(self.s_ready, 1)

    def gcn_project():
        with ExitStack() as ctx:
            w = sb(ctx, "p_w", [P, 2 * cols["conv"]], F16)
            h = [sb(ctx, f"p_h{b}", [P, D]) for b in range(2)]
            hT = [sb(ctx, f"p_hT{b}", [P, 2 * D], F16) for b in range(2)]
            hw = [sb(ctx, f"p_hw{b}", [P, HID]) for b in range(2)]
            f = sb(ctx, "p_f", [P, 1])
            dcol = [sb(ctx, f"p_dcol{b}", [P, 1]) for b in range(2)]
            ps_t = [ps(ctx, f"p_ps_t{b}") for b in range(2)]
            ps_h = [ps(ctx, f"p_ps_h{b}") for b in range(2)]
            s_w, s_f, s_h, s_turn, s_hi, s_lo, s_mm, s_dcol, s_hw = sems(
                "p", "w f h turn hi lo mm dcol hw")
            x_in, hw_out = pair("p", "xin"), pair("p", "hwout")
            norm = Norm(ctx, "p_norm")
            block = ctx.enter_context(nc.Block())

            @block.sync
            def _(sp):
                sp.dma_start(w[:, :], split_d["conv"][:, :]).then_inc(s_w, 16)

                def store(t, k, b):
                    sp.wait_ge(s_hw, t + 1)
                    sp.dma_start(rows(hw_d, t), hw[b][0:rows_of(t), :]).then_inc(hw_out[b], 16)

                def body(t, k, b):
                    wait_count(sp, norm.s_stats, t - 1)
                    r = rows_of(t)
                    sp.dma_start(slot(t)[0:r, :], rows(x, t)).then_inc(x_in[b], 16)
                    if started(3, t):
                        store(*ago(3, t, k, b))
                each_tile(sp, NT, body)
                for tile in last(NT, 3):
                    store(*tile)
                sp.wait_ge(hw_out[0], 16 * ((NT + 1) // 2))
                sp.wait_ge(hw_out[1], 16 * (NT // 2))

            @block.vector
            def _(dve):
                nc.vector.tensor_scalar(out=f[:, :], in0=down[:, unit_no["conv"]:unit_no["conv"] + 1],
                                        scalar1=1.0 / SCALE_LN, scalar2=None, op0=MUL).then_inc(s_f, 1)
                dve.wait_ge(s_f, 1)

                def rest(t, k, b):
                    dve.wait_ge(s_turn, t + 1)
                    dve.wait_ge(s_hi, t + 1)
                    nc.vector.scalar_tensor_tensor(out=hT[b][:, D:2 * D], in0=ps_t[b][:, :], scalar=SCALE_LN,
                                                   in1=hT[b][:, 0:D], op0=MUL, op1=SUB).then_inc(s_lo, 1)
                    wait_count(dve, s_hw, t - 1)
                    nc.vector.tensor_copy(dcol[b][:, :], dis[:, bass.ds(t, 1)]).then_inc(s_dcol, 1)
                    dve.wait_ge(s_dcol, t + 1)
                    dve.wait_ge(s_mm, t + 1)
                    wait_count(dve, hw_out[b], 16 * k)
                    nc.vector.tensor_scalar(out=hw[b][:, :], in0=ps_h[b][:, 0:HID], scalar1=f[:, 0:1],
                                            scalar2=dcol[b][:, 0:1], op0=MUL, op1=MUL).then_inc(s_hw, 1)

                def body(t, k, b):
                    dve.wait_ge(x_in[b], 16 * (k + 1))
                    norm.on_vector(dve, slot(t), t, b)
                    if started(2, t):
                        rest(*ago(2, t, k, b))
                each_tile(dve, NT, body)
                for tile in last(NT, 2):
                    rest(*tile)

            @block.gpsimd
            def _(pool):
                each_tile(pool, NT, lambda t, k, b: norm.on_pool(pool, t, b, [(s_h, t - 1)]))

            @block.scalar
            def _(act):
                def hi(t, k, b):
                    act.wait_ge(s_turn, t + 1)
                    wait_count(act, s_mm, t - 1)
                    nc.scalar.activation(hT[b][:, 0:D], ps_t[b][:, :], ACT.Copy, scale=SCALE_LN).then_inc(s_hi, 1)

                def body(t, k, b):
                    if started(1, t):
                        hi(*ago(1, t, k, b))
                    act.wait_ge(norm.s_ready, t + 1)
                    wait_count(act, s_turn, t - 1)
                    nc.scalar.activation(h[b][:, :], slot(t), ACT.Relu, scale=norm.rstd[b][:, 0:1],
                                         bias=norm.shift[b][:, 0:1]).then_inc(s_h, 1)
                each_tile(act, NT, body)
                for tile in last(NT, 1):
                    hi(*tile)

            @block.tensor
            def _(pe):
                pe.wait_ge(s_w, 16)

                def mm(t, k, b):
                    pe.wait_ge(s_lo, t + 1)
                    wait_count(pe, s_hw, t - 1)
                    product(pe, ps_h[b][:, 0:HID], lambda c: hT[b][:, c * P:(c + 1) * P],
                            lambda c: hT[b][:, D + c * P:D + (c + 1) * P], w, HID).then_inc(s_mm, 1)

                def body(t, k, b):
                    pe.wait_ge(s_h, t + 1)
                    wait_count(pe, s_lo, t - 1)
                    transposes(pe, ps_t[b], h[b]).then_inc(s_turn, 1)
                    if started(1, t):
                        mm(*ago(1, t, k, b))
                each_tile(pe, NT, body)
                for tile in last(NT, 1):
                    mm(*tile)

    def edge_sums_gcn():
        with ExitStack() as ctx:
            m = [sb(ctx, f"q_m{b}", [P, HID]) for b in range(2)]
            sl = [sb(ctx, f"q_sel{b}", [P, 2 * P]) for b in range(2)]
            tot = [sb(ctx, f"q_tot{b}", [P, HID]) for b in range(2)]
            ps_c = ps(ctx, "q_ps_c")
            ps_s = [ps(ctx, f"q_ps_s{b}") for b in range(2)]
            s_carry, s_carried, s_sum, s_tot = sems("q", "carry carried sum tot")
            m_in, sel_in, t_out = pair("q", "min"), pair("q", "selin"), pair("q", "tout")
            block = ctx.enter_context(nc.Block())

            @block.sync
            def _(sp):
                for t in range(ET):
                    wait_count(sp, s_sum, t - 1)
                    sp.dma_start(sl[t % 2][:, :], sel_d[:, t * 2 * P:(t + 1) * 2 * P]).then_inc(sel_in[t % 2], 16)

            @block.gpsimd
            def _(pool):
                def scatter(t):
                    pool.wait_ge(s_tot, t + 1)
                    nc.gpsimd.indirect_dma_start(
                        gcn_d[:, :], bass.IndirectOffsetOnAxis(ap=put_i[:, t:t + 1], axis=0), tot[t % 2][:, :],
                        None, bounds_check=N - 1, oob_is_err=False).then_inc(t_out[t % 2], 16)

                for t in range(ET):
                    wait_count(pool, s_sum, t - 1)
                    nc.gpsimd.indirect_dma_start(
                        m[t % 2][:, :], None, hw_d[0:N, :],
                        bass.IndirectOffsetOnAxis(ap=src_i[:, t:t + 1], axis=0)).then_inc(m_in[t % 2], 16)
                    if t >= 1:
                        scatter(t - 1)
                scatter(ET - 1)
                for b in range(2):
                    pool.wait_ge(t_out[b], 16 * (ET // 2))

            @block.vector
            def _(dve):
                for t in range(ET):
                    b, k = t % 2, t // 2
                    if t:
                        dve.wait_ge(m_in[b], 16 * (k + 1))
                        dve.wait_ge(s_carry, t)
                        nc.vector.tensor_copy(m[b][0:1, :], ps_c[0:1, 0:HID]).then_inc(s_carried, 1)
                    dve.wait_ge(s_sum, t + 1)
                    wait_count(dve, t_out[b], 16 * k)
                    nc.vector.tensor_copy(tot[b][:, :], ps_s[b][:, 0:HID]).then_inc(s_tot, 1)

            @block.tensor
            def _(pe):
                for t in range(ET):
                    b, k = t % 2, t // 2
                    pe.wait_ge(sel_in[b], 16 * (k + 1))
                    pe.wait_ge(m_in[b], 16 * (k + 1))
                    wait_count(pe, s_carried, t)
                    nc.tensor.matmul(ps_c[0:1, 0:HID], sl[b][:, P - 1:P], m[b][:, :], start=True,
                                     stop=True).then_inc(s_carry, 1)
                    wait_count(pe, s_tot, t - 1)
                    nc.tensor.matmul(ps_s[b][:, 0:HID], sl[b][:, 0:P], m[b][:, :], start=True,
                                     stop=True).then_inc(s_sum, 1)

    def gcn_finish():
        with ExitStack() as ctx:
            w = sb(ctx, "r_w", [P, D])
            bias_c = sb(ctx, "r_bias_c", [P, HID])
            bias_l = sb(ctx, "r_bias_l", [P, D])
            hw = [sb(ctx, f"r_hw{b}", [P, HID]) for b in range(2)]
            gs = [sb(ctx, f"r_gs{b}", [P, HID]) for b in range(2)]
            cv = [sb(ctx, f"r_cv{b}", [P, HID]) for b in range(2)]
            cT = [sb(ctx, f"r_cT{b}", [P, HID]) for b in range(2)]
            x1 = [sb(ctx, f"r_x1{b}", [P, D]) for b in range(2)]
            xb = [sb(ctx, f"r_xb{b}", [P, D]) for b in range(2)]
            h = [sb(ctx, f"r_h{b}", [P, D]) for b in range(2)]
            dcol = [sb(ctx, f"r_dcol{b}", [P, 1]) for b in range(2)]
            ps_c = [ps(ctx, f"r_ps_c{b}") for b in range(2)]
            ps_x = [ps(ctx, f"r_ps_x{b}") for b in range(2)]
            ps_t = [ps(ctx, f"r_ps_t{b}") for b in range(2)]
            s_w, s_cv0, s_dcol, s_cv, s_ct, s_cT, s_mm, s_xb, s_x1, s_h, s_turn, s_hi, s_lo = sems(
                "r", "w cv0 dcol cv ct cT mm xb x1 h turn hi lo")
            g_in, x_out = pair("r", "gin"), pair("r", "xout")
            norm = Norm(ctx, "r_norm")
            block = ctx.enter_context(nc.Block())

            @block.sync
            def _(sp):
                sp.dma_start(w[:, :], Wlin[:, :]).then_inc(s_w, 16)
                sp.dma_start(bias_c[:, :], wide(bc)).then_inc(s_w, 16)
                sp.dma_start(bias_l[:, :], wide(blin)).then_inc(s_w, 16)

                def store(t, k, b):
                    sp.wait_ge(s_x1, t + 1)
                    sp.dma_start(rows(x1_d, t), x1[b][0:rows_of(t), :]).then_inc(x_out[b], 16)

                def body(t, k, b):
                    wait_count(sp, s_cv, t - 1)
                    r = rows_of(t)
                    sp.dma_start(hw[b][0:r, :], rows(hw_d, t)).then_inc(g_in[b], 16)
                    sp.dma_start(gs[b][0:r, :], rows(gcn_d, t)).then_inc(g_in[b], 16)
                    if started(1, t):
                        store(*ago(1, t, k, b))
                each_tile(sp, NT, body)
                for tile in last(NT, 1):
                    store(*tile)
                sp.wait_ge(x_out[0], 16 * ((NT + 1) // 2))
                sp.wait_ge(x_out[1], 16 * (NT // 2))

            @block.gpsimd
            def _(pool):
                pool.wait_ge(s_w, 48)

                def body(t, k, b):
                    wait_count(pool, s_x1, t - 1)
                    nc.gpsimd.tensor_tensor(out=xb[b][:, :], in0=slot(t), in1=bias_l[:, :], op=ADD)\
                        .then_inc(s_xb, 1)
                    if started(1, t):
                        u, _, ub = ago(1, t, k, b)
                        norm.on_pool(pool, u, ub, [(s_h, u - 1)])
                each_tile(pool, NT, body)
                for t, _, b in last(NT, 1):
                    norm.on_pool(pool, t, b, [(s_h, t - 1)])

            @block.vector
            def _(dve):
                dve.wait_ge(s_w, 48)

                def conv(t, k, b):
                    dve.wait_ge(g_in[b], 32 * (k + 1))
                    nc.vector.tensor_copy(dcol[b][:, :], dis[:, bass.ds(t, 1)]).then_inc(s_dcol, 1)
                    wait_count(dve, s_ct, t - 1)
                    nc.vector.tensor_tensor(out=cv[b][:, :], in0=hw[b][:, :], in1=gs[b][:, :], op=ADD)\
                        .then_inc(s_cv0, 1)
                    dve.wait_ge(s_dcol, t + 1)
                    dve.wait_ge(s_cv0, t + 1)
                    nc.vector.scalar_tensor_tensor(out=cv[b][:, :], in0=cv[b][:, :], scalar=dcol[b][:, 0:1],
                                                   in1=bias_c[:, :], op0=MUL, op1=ADD).then_inc(s_cv, 1)

                def residual(t, k, b):
                    dve.wait_ge(s_mm, t + 1)
                    dve.wait_ge(s_xb, t + 1)
                    wait_count(dve, x_out[b], 16 * k)
                    wait_count(dve, s_h, t - 1)
                    nc.vector.tensor_tensor(out=x1[b][:, :], in0=ps_x[b][:, :], in1=xb[b][:, :], op=ADD)\
                        .then_inc(s_x1, 1)
                    dve.wait_ge(s_x1, t + 1)
                    norm.on_vector(dve, x1[b][:, :], t, b)

                def lo(t, k, b):
                    dve.wait_ge(s_hi, t + 1)
                    nc.vector.scalar_tensor_tensor(out=slot_lo(t), in0=ps_t[b][:, :], scalar=SCALE_LN,
                                                   in1=slot_hi(t), op0=MUL, op1=SUB).then_inc(s_lo, 1)

                def body(t, k, b):
                    conv(t, k, b)
                    if started(1, t):
                        residual(*ago(1, t, k, b))
                    if started(3, t):
                        lo(*ago(3, t, k, b))
                each_tile(dve, NT, body)
                residual(*last(NT, 1)[0])
                for tile in last(NT, 3):
                    lo(*tile)

            @block.scalar
            def _(act):
                def body(t, k, b):
                    act.wait_ge(s_ct, t + 1)
                    wait_count(act, s_mm, t - 1)
                    nc.scalar.activation(cT[b][:, :], ps_c[b][:, 0:HID], ACT.Copy).then_inc(s_cT, 1)
                    if started(3, t):
                        hi(*ago(3, t, k, b))
                    if started(2, t):
                        normed(*ago(2, t, k, b))

                def normed(t, k, b):
                    act.wait_ge(norm.s_ready, t + 1)
                    wait_count(act, s_turn, t - 1)
                    nc.scalar.activation(h[b][:, :], x1[b][:, :], ACT.Relu, scale=norm.rstd[b][:, 0:1],
                                         bias=norm.shift[b][:, 0:1]).then_inc(s_h, 1)

                def hi(t, k, b):
                    act.wait_ge(s_turn, t + 1)
                    act.wait_ge(s_x1, t + 1)
                    nc.scalar.activation(slot_hi(t), ps_t[b][:, :], ACT.Copy, scale=SCALE_LN).then_inc(s_hi, 1)
                each_tile(act, NT, body)
                hi(*last(NT, 3)[0])
                normed(*last(NT, 2)[0])
                hi(*last(NT, 2)[0])
                normed(*last(NT, 1)[0])
                hi(*last(NT, 1)[0])

            @block.tensor
            def _(pe):
                pe.wait_ge(s_w, 48)

                def linear(t, k, b):
                    pe.wait_ge(s_cT, t + 1)
                    wait_count(pe, s_x1, t - 1)
                    nc.tensor.matmul(ps_x[b][:, :], cT[b][:, :], w[:, :], start=True, stop=True).then_inc(s_mm, 1)

                def turn(t, k, b):
                    pe.wait_ge(s_h, t + 1)
                    wait_count(pe, s_lo, t - 1)
                    transposes(pe, ps_t[b], h[b]).then_inc(s_turn, 1)

                def body(t, k, b):
                    pe.wait_ge(s_cv, t + 1)
                    wait_count(pe, s_cT, t - 1)
                    nc.tensor.transpose(ps_c[b][:, 0:P], cv[b][:, :], ident[:, :]).then_inc(s_ct, 1)
                    if started(3, t):
                        turn(*ago(3, t, k, b))
                    linear(t, k, b)
                each_tile(pe, NT, body)
                for tile in last(NT, 3):
                    turn(*tile)

    def edge_products(phase, source, gather, normed, mean, scale, unit, weight=None):
        with ExitStack() as ctx:
            if unit:
                w = sb(ctx, f"{phase}_w", [P, 2 * cols[unit]], F16)
            else:
                w = sb(ctx, f"{phase}_w", [P, C * D])
            m = [sb(ctx, f"{phase}_m{b}", [P, D]) for b in range(2)]
            sl = [sb(ctx, f"{phase}_sel{b}", [P, 2 * P]) for b in range(2)]
            aT = [sb(ctx, f"{phase}_aT{b}", [P, D]) for b in range(2)]
            tot = [sb(ctx, f"{phase}_tot{b}", [P, D]) for b in range(2)]
            f = sb(ctx, f"{phase}_f", [P, 1])
            ps_c = ps(ctx, f"{phase}_ps_c")
            ps_a = [ps(ctx, f"{phase}_ps_a{b}") for b in range(2)]
            ps_g = [ps(ctx, f"{phase}_ps_g{b}") for b in range(2)]
            s_w, s_f, s_row, s_carry, s_carried, s_sum, s_hi, s_lo, s_mm, s_tot = sems(
                phase, "w f row carry carried sum hi lo mm tot")
            m_in, sel_in, t_out = pair(phase, "min"), pair(phase, "selin"), pair(phase, "tout")
            norm = Norm(ctx, f"{phase}_norm") if normed else None
            aT16 = [a[:, :].bitcast(F16) for a in aT]
            block = ctx.enter_context(nc.Block())

            @block.sync
            def _(sp):
                if unit:
                    sp.dma_start(w[:, :], split_d[unit][:, :]).then_inc(s_w, 16)
                else:
                    sp.dma_start(w[:, :].rearrange("p (c n) -> p c n", c=C),
                                 weight.rearrange("(c p) n -> p c n", p=P)).then_inc(s_w, 16)

                def body(t, k, b):
                    wait_count(sp, s_sum, t - 1)
                    sp.dma_start(sl[b][:, :], sel_d[:, bass.ds(t * 2 * P, 2 * P)]).then_inc(sel_in[b], 16)
                    if not gather:
                        sp.dma_start(m[b][:, :], source[bass.ds(t * P, P), :]).then_inc(m_in[b], 16)
                each_tile(sp, ET, body)

            @block.gpsimd
            def _(pool):
                def scatter(t, k, b):
                    pool.wait_ge(s_tot, t + 1)
                    nc.gpsimd.indirect_dma_start(
                        agg_d[:, :], bass.IndirectOffsetOnAxis(ap=put_i[:, t:t + 1], axis=0), tot[b][:, :],
                        None, bounds_check=N - 1, oob_is_err=False).then_inc(t_out[b], 16)

                for t in range(ET):
                    b, k = t % 2, t // 2
                    if gather:
                        wait_count(pool, s_sum, t - 1)
                        nc.gpsimd.indirect_dma_start(
                            m[b][:, :], None, source[0:N, :],
                            bass.IndirectOffsetOnAxis(ap=src_i[:, t:t + 1], axis=0)).then_inc(m_in[b], 16)
                    if normed and t >= 1:
                        norm.on_pool(pool, t - 1, 1 - b, [(s_row, t - 2)])
                    if t >= 3:
                        scatter(*ago(3, t, k, b))
                if normed:
                    norm.on_pool(pool, ET - 1, (ET - 1) % 2, [(s_row, ET - 2)])
                for tile in last(ET, 3):
                    scatter(*tile)
                for b in range(2):
                    pool.wait_ge(t_out[b], 16 * (ET // 2))

            @block.vector
            def _(dve):
                if unit:
                    nc.vector.tensor_scalar(out=f[:, :], in0=down[:, unit_no[unit]:unit_no[unit] + 1],
                                            scalar1=1.0 / scale, scalar2=None, op0=MUL).then_inc(s_f, 1)
                else:
                    nc.vector.memset(f[:, :], 1.0).then_inc(s_f, 1)
                dve.wait_ge(s_f, 1)

                def carry(t, k, b):
                    if normed:
                        dve.wait_ge(s_row, t + 1)
                    else:
                        dve.wait_ge(m_in[b], 16 * (k + 1))
                    dve.wait_ge(s_carry, t)
                    nc.vector.tensor_copy(m[b][0:1, :], ps_c[0:1, :]).then_inc(s_carried, 1)

                def lo(t, k, b):
                    dve.wait_ge(s_hi, t + 1)
                    nc.vector.scalar_tensor_tensor(out=aT16[b][:, D:2 * D], in0=ps_a[b][:, :], scalar=scale,
                                                   in1=aT16[b][:, 0:D], op0=MUL, op1=SUB).then_inc(s_lo, 1)

                def totals(t, k, b):
                    dve.wait_ge(s_mm, t + 1)
                    wait_count(dve, t_out[b], 16 * k)
                    nc.vector.tensor_scalar(out=tot[b][:, :], in0=ps_g[b][:, :], scalar1=f[:, 0:1],
                                            scalar2=None, op0=MUL).then_inc(s_tot, 1)

                def rest(t, k, b):
                    if started(1, t):
                        carry(t, k, b)
                    if unit:
                        lo(t, k, b)

                def body(t, k, b):
                    if normed:
                        dve.wait_ge(m_in[b], 16 * (k + 1))
                        norm.on_vector(dve, m[b][:, :], t, b)
                    if started(1, t):
                        rest(*ago(1, t, k, b))
                    if started(2, t):
                        totals(*ago(2, t, k, b))
                each_tile(dve, ET, body)
                rest(*last(ET, 1)[0])
                for tile in last(ET, 2):
                    totals(*tile)

            @block.scalar
            def _(act):
                def hi(t, k, b):
                    act.wait_ge(s_sum, t + 1)
                    wait_count(act, s_mm, t - 1)
                    if unit:
                        nc.scalar.activation(aT16[b][:, 0:D], ps_a[b][:, :], ACT.Copy, scale=scale).then_inc(s_hi, 1)
                    else:
                        nc.scalar.activation(aT[b][:, :], ps_a[b][:, :], ACT.Copy).then_inc(s_hi, 1)

                def body(t, k, b):
                    if normed:
                        act.wait_ge(norm.s_ready, t + 1)
                        nc.scalar.activation(m[b][:, :], m[b][:, :], ACT.Relu, scale=norm.rstd[b][:, 0:1],
                                             bias=norm.shift[b][:, 0:1]).then_inc(s_row, 1)
                    if started(1, t):
                        hi(*ago(1, t, k, b))
                each_tile(act, ET, body)
                hi(*last(ET, 1)[0])

            @block.tensor
            def _(pe):
                pe.wait_ge(s_w, 16)

                def sums(t, k, b):
                    pe.wait_ge(sel_in[b], 16 * (k + 1))
                    if normed:
                        pe.wait_ge(s_row, t + 1)
                    else:
                        pe.wait_ge(m_in[b], 16 * (k + 1))
                    wait_count(pe, s_carried, t)
                    nc.tensor.matmul(ps_c[0:1, :], sl[b][:, P - 1:P], m[b][:, :], start=True,
                                     stop=True).then_inc(s_carry, 1)
                    wait_count(pe, s_lo if unit else s_hi, t - 1)
                    half = P if mean else 0
                    for c in range(C):
                        ins = nc.tensor.matmul(ps_a[b][:, c * P:(c + 1) * P], m[b][:, c * P:(c + 1) * P],
                                               sl[b][:, half:half + P], start=True, stop=True)
                    ins.then_inc(s_sum, 1)

                def mm(t, k, b):
                    pe.wait_ge(s_lo if unit else s_hi, t + 1)
                    wait_count(pe, s_tot, t - 1)
                    if unit:
                        product(pe, ps_g[b][:, :], lambda c: aT16[b][:, c * P:(c + 1) * P],
                                lambda c: aT16[b][:, D + c * P:D + (c + 1) * P], w, D).then_inc(s_mm, 1)
                    else:
                        for c in range(C):
                            ins = nc.tensor.matmul(ps_g[b][:, :], aT[b][:, c * P:(c + 1) * P],
                                                   w[:, c * D:(c + 1) * D], start=c == 0, stop=c == C - 1)
                        ins.then_inc(s_mm, 1)

                def body(t, k, b):
                    sums(t, k, b)
                    if started(1, t):
                        mm(*ago(1, t, k, b))
                each_tile(pe, ET, body)
                mm(*last(ET, 1)[0])

    def sage_layer(l):
        final = l == 2
        phase = f"s{l}"
        scale_in = SCALE_LN if l == 0 else SCALE_UNIT
        scale_out = SCALE_LN if final else SCALE_UNIT
        unit = f"self{l}"
        with ExitStack() as ctx:
            w = sb(ctx, f"{phase}_w", [P, 2 * cols[unit]], F16)
            bias = sb(ctx, f"{phase}_bias", [P, D])
            g = [sb(ctx, f"{phase}_g{b}", [P, D]) for b in range(2)]
            r = [sb(ctx, f"{phase}_r{b}", [P, D]) for b in range(2)]
            junk = sb(ctx, f"{phase}_junk", [P, D])
            h = [sb(ctx, f"{phase}_h{b}", [P, D]) for b in range(2)]
            en = [sb(ctx, f"{phase}_en{b}", [P, 1]) for b in range(2)]
            em = [sb(ctx, f"{phase}_em{b}", [P, 1]) for b in range(2)]
            rn = [sb(ctx, f"{phase}_rn{b}", [P, 1]) for b in range(2)]
            f = sb(ctx, f"{phase}_f", [P, 1])
            least = sb(ctx, f"{phase}_least", [P, 1])
            if final:
                x1 = [sb(ctx, f"{phase}_x1{b}", [P, D]) for b in range(2)]
                h3 = [sb(ctx, f"{phase}_h3{b}", [P, D]) for b in range(2)]
            ps_z = [ps(ctx, f"{phase}_ps_z{b}") for b in range(2)]
            ps_t = [ps(ctx, f"{phase}_ps_t{b}") for b in range(2)]
            s_w, s_f, s_mm, s_bias, s_r, s_en, s_em, s_rn, s_h, s_turn, s_hi, s_lo, s_x2, s_h3 = sems(
                phase, "w f mm bias r en em rn h turn hi lo x2 h3")
            g_in, h_out = pair(phase, "gin"), pair(phase, "hout")
            x_in = pair(phase, "xin") if final else None
            norm = Norm(ctx, f"{phase}_norm") if final else None
            turned = h3 if final else h
            s_turned = s_h3 if final else s_h
            lag = 3 if final else 2
            block = ctx.enter_context(nc.Block())

            @block.sync
            def _(sp):
                sp.dma_start(w[:, :], split_d[unit][:, :]).then_inc(s_w, 16)
                sp.dma_start(bias[:, :], wide(bsage[l])).then_inc(s_w, 16)

                def store(t, k, b):
                    n = rows_of(t)
                    if final:
                        sp.wait_ge(s_x2, t + 1)
                        sp.dma_start(rows(x2_d, t), x1[b][0:n, :]).then_inc(h_out[b], 16)
                    else:
                        sp.wait_ge(s_h, t + 1)
                        sp.dma_start(rows(h_d, t), h[b][0:n, :]).then_inc(h_out[b], 16)

                def body(t, k, b):
                    wait_count(sp, s_r, t - 1)
                    n = rows_of(t)
                    sp.dma_start(g[b][0:n, :], rows(agg_d, t)).then_inc(g_in[b], 16)
                    if final:
                        if started(2, t):
                            store(*ago(2, t, k, b))
                        wait_count(sp, h_out[b], 16 * k)
                        wait_count(sp, s_h3, t - 1)
                        sp.dma_start(x1[b][0:n, :], rows(x1_d, t)).then_inc(x_in[b], 16)
                    elif started(1, t):
                        store(*ago(1, t, k, b))
                each_tile(sp, NT, body)
                for tile in last(NT, 2 if final else 1):
                    store(*tile)
                sp.wait_ge(h_out[0], 16 * ((NT + 1) // 2))
                sp.wait_ge(h_out[1], 16 * (NT // 2))

            @block.gpsimd
            def _(pool):
                nc.gpsimd.memset(least[:, :], NORM_EPS * NORM_EPS)
                pool.wait_ge(s_w, 32)

                def body(t, k, b):
                    pool.wait_ge(g_in[b], 16 * (k + 1))
                    nc.gpsimd.tensor_tensor(out=g[b][:, :], in0=g[b][:, :], in1=bias[:, :], op=ADD)\
                        .then_inc(s_bias, 1)
                    if started(1, t):
                        factor(*ago(1, t, k, b))
                    if final and started(2, t):
                        u, _, ub = ago(2, t, k, b)
                        norm.on_pool(pool, u, ub, [(s_h3, u - 1)])

                def factor(t, k, b):
                    pool.wait_ge(s_em, t + 1)
                    wait_count(pool, s_h, t - 1)
                    nc.gpsimd.tensor_tensor(out=rn[b][:, :], in0=em[b][:, :], in1=minus_half[:, :],
                                            op=POW).then_inc(s_rn, 1)
                each_tile(pool, NT, body)
                t, k, b = last(NT, 1)[0]
                if final:
                    norm.on_pool(pool, t - 1, 1 - b, [(s_h3, t - 2)])
                factor(t, k, b)
                if final:
                    norm.on_pool(pool, t, b, [(s_h3, t - 1)])

            @block.vector
            def _(dve):
                nc.vector.tensor_scalar(out=f[:, :], in0=down[:, unit_no[unit]:unit_no[unit] + 1],
                                        scalar1=1.0 / scale_in, scalar2=None, op0=MUL).then_inc(s_f, 1)
                dve.wait_ge(s_f, 1)

                def lo(t, k, b):
                    dve.wait_ge(s_hi, t + 1)
                    nc.vector.scalar_tensor_tensor(out=slot_lo(t), in0=ps_t[b][:, :], scalar=scale_out,
                                                   in1=slot_hi(t), op0=MUL, op1=SUB).then_inc(s_lo, 1)

                def residual(t, k, b):
                    dve.wait_ge(s_h, t + 1)
                    dve.wait_ge(x_in[b], 16 * (k + 1))
                    nc.vector.tensor_tensor(out=x1[b][:, :], in0=x1[b][:, :], in1=h[b][:, :], op=ADD)\
                        .then_inc(s_x2, 1)
                    dve.wait_ge(s_x2, t + 1)
                    norm.on_vector(dve, x1[b][:, :], t, b)

                def body(t, k, b):
                    dve.wait_ge(s_mm, t + 1)
                    dve.wait_ge(s_bias, t + 1)
                    wait_count(dve, s_h, t - 1)
                    nc.vector.scalar_tensor_tensor(out=r[b][:, :], in0=ps_z[b][:, :], scalar=f[:, 0:1],
                                                   in1=g[b][:, :], op0=MUL, op1=ADD).then_inc(s_r, 1)
                    dve.wait_ge(s_r, t + 1)
                    wait_count(dve, s_em, t)
                    nc.vector.scalar_tensor_tensor(out=junk[:, :], in0=r[b][:, :], scalar=0.0, in1=r[b][:, :],
                                                   op0=MAX, op1=MUL, accum_out=en[b][:, 0:1]).then_inc(s_en, 1)
                    dve.wait_ge(s_en, t + 1)
                    wait_count(dve, s_rn, t - 1)
                    nc.vector.tensor_scalar(out=em[b][:, :], in0=en[b][:, :], scalar1=NORM_EPS * NORM_EPS,
                                            scalar2=None, op0=MAX).then_inc(s_em, 1)
                    if final and started(1, t):
                        residual(*ago(1, t, k, b))
                    if started(lag, t):
                        lo(*ago(lag, t, k, b))
                each_tile(dve, NT, body)
                if final:
                    residual(*last(NT, 1)[0])
                for tile in last(NT, lag):
                    lo(*tile)

            @block.scalar
            def _(act):
                def hi(t, k, b):
                    act.wait_ge(s_turn, t + 1)
                    nc.scalar.activation(slot_hi(t), ps_t[b][:, :], ACT.Copy, scale=scale_out).then_inc(s_hi, 1)

                def normed(t, k, b):
                    act.wait_ge(norm.s_ready, t + 1)
                    wait_count(act, s_turn, t - 1)
                    nc.scalar.activation(h3[b][:, :], x1[b][:, :], ACT.Relu, scale=norm.rstd[b][:, 0:1],
                                         bias=norm.shift[b][:, 0:1]).then_inc(s_h3, 1)

                def body(t, k, b):
                    if started(lag, t):
                        hi(*ago(lag, t, k, b))
                    if final and started(2, t):
                        normed(*ago(2, t, k, b))
                    act.wait_ge(s_rn, t + 1)
                    if final:
                        wait_count(act, s_x2, t - 1)
                    else:
                        wait_count(act, s_turn, t - 1)
                        wait_count(act, h_out[b], 16 * k)
                    nc.scalar.activation(h[b][:, :], r[b][:, :], ACT.Relu, scale=rn[b][:, 0:1]).then_inc(s_h, 1)
                each_tile(act, NT, body)
                if final:
                    a3, a2, a1 = last(NT, 3)
                    hi(*a3)
                    normed(*a2)
                    hi(*a2)
                    normed(*a1)
                    hi(*a1)
                else:
                    for tile in last(NT, lag):
                        hi(*tile)

            @block.tensor
            def _(pe):
                pe.wait_ge(s_w, 32)

                def turn(t, k, b):
                    pe.wait_ge(s_turned, t + 1)
                    wait_count(pe, s_lo, t - 1)
                    transposes(pe, ps_t[b], turned[b]).then_inc(s_turn, 1)

                def body(t, k, b):
                    wait_count(pe, s_r, t - 1)
                    product(pe, ps_z[b][:, :], lambda c: slots16[:, bass.ds(t * 2 * D + c * P, P)],
                            lambda c: slots16[:, bass.ds(t * 2 * D + D + c * P, P)], w, D).then_inc(s_mm, 1)
                    if started(lag, t):
                        turn(*ago(lag, t, k, b))
                each_tile(pe, NT, body)
                for tile in last(NT, lag):
                    turn(*tile)

    class Mish:
        def __init__(self, ctx, name):
            self.c = sb(ctx, f"{name}_c", [P, D])
            self.e = sb(ctx, f"{name}_e", [P, D])
            self.w = sb(ctx, f"{name}_w", [P, D])
            self.q = self.e
            self.s_c, self.s_e, self.s_w, self.s_q, self.s_rq, self.s_rw, self.s_u = sems(
                name, "c e w q rq rw u")

        def on_vector(self, dve, r, out_ap, n):
            nc.vector.tensor_scalar(out=self.c[:, :], in0=r, scalar1=MISH_CAP, scalar2=None,
                                    op0=MIN).then_inc(self.s_c, 1)
            dve.wait_ge(self.s_e, n + 1)
            nc.vector.scalar_tensor_tensor(out=self.w[:, :], in0=self.e[:, :], scalar=2.0, in1=self.e[:, :],
                                           op0=ADD, op1=MUL).then_inc(self.s_w, 1)
            dve.wait_ge(self.s_w, n + 1)
            nc.vector.tensor_scalar(out=self.q[:, :], in0=self.w[:, :], scalar1=2.0, scalar2=None,
                                    op0=ADD).then_inc(self.s_q, 1)
            dve.wait_ge(self.s_q, n + 1)
            nc.vector.reciprocal(self.q[:, :], self.q[:, :]).then_inc(self.s_rq, 1)
            dve.wait_ge(self.s_rq, n + 1)
            dve.wait_ge(self.s_rw, n + 1)
            nc.vector.tensor_tensor(out=out_ap, in0=self.c[:, :], in1=self.q[:, :], op=MUL).then_inc(self.s_u, 1)

        def on_scalar(self, act, n):
            act.wait_ge(self.s_c, n + 1)
            nc.scalar.activation(self.e[:, :], self.c[:, :], ACT.Exp).then_inc(self.s_e, 1)

        def on_pool(self, pool, r, n):
            pool.wait_ge(self.s_w, n + 1)
            nc.gpsimd.tensor_tensor(out=self.c[:, :], in0=r, in1=self.w[:, :], op=MUL).then_inc(self.s_rw, 1)

    def edge_network():
        with ExitStack() as ctx:
            w1 = sb(ctx, "e_w1", [P, 2 * cols["edge"]], F16)
            w1c = sb(ctx, "e_w1c", [ED, D])
            w2 = sb(ctx, "e_w2", [P, C * D])
            bias1 = sb(ctx, "e_bias1", [P, D])
            bias2 = sb(ctx, "e_bias2", [P, D])
            m = [sb(ctx, f"e_m{s}", [P, D]) for s in range(2)]
            ea = sb(ctx, "e_ea", [P, ED])
            eaT = sb(ctx, "e_eaT", [ED, P])
            hT = [sb(ctx, f"e_hT{s}", [P, 2 * D], F16) for s in range(2)]
            r = sb(ctx, "e_r", [P, D])
            mT = hT[0][:, :].bitcast(F32)
            m1 = r
            f = sb(ctx, "e_f", [P, 1])
            ps_t = [ps(ctx, f"e_ps_t{s}") for s in range(2)]
            ps_e = ps(ctx, "e_ps_e")
            ps_1, ps_2, ps_m = ps(ctx, "e_ps_1"), ps(ctx, "e_ps_2"), ps(ctx, "e_ps_m")
            (s_w, s_f, s_wc, s_row, s_turn, s_hi, s_lo, s_et, s_eT, s_mm1, s_r, s_mt, s_mT, s_mm2,
             s_out, s_ea) = sems("e", "w f wc row turn hi lo et eT mm1 r mt mT mm2 out ea")
            m_in = pair("e", "min")
            norm = Norm(ctx, "e_norm")
            mish = Mish(ctx, "e_mish")
            msg = mish.w
            u_edge = unit_no["edge"]
            block = ctx.enter_context(nc.Block())

            def first_no(t):
                return 0 if isinstance(t, int) and t == 0 else 2 * t - 1

            def next_of(t):
                return ET if isinstance(t, int) and t == ET - 1 else t + 2

            def second_no(t):
                return 2 * ET - 1 if isinstance(t, int) and t == ET - 1 else 2 * t + 2

            @block.sync
            def _(sp):
                sp.dma_start(w1[:, :], split_d["edge"][:, :]).then_inc(s_w, 16)
                sp.dma_start(w1c[:, :], W1[2 * D:2 * D + ED, :]).then_inc(s_w, 16)
                sp.dma_start(w2[:, :].rearrange("p (c n) -> p c n", c=C),
                             W2.rearrange("(c p) n -> p c n", p=P)).then_inc(s_w, 16)
                sp.dma_start(bias1[:, :], wide(b1)).then_inc(s_w, 16)
                sp.dma_start(bias2[:, :], wide(b2)).then_inc(s_w, 16)

                def body(t, k, b):
                    sp.wait_ge(mish.s_u, second_no(t) + 1)
                    sp.dma_start(msg_d[bass.ds(t * P, P), :], msg[:, :]).then_inc(s_out, 16)
                each_tile(sp, ET - 1, body)
                body(ET - 1, 0, 0)
                sp.wait_ge(s_out, 16 * ET)

            @block.gpsimd
            def _(pool):
                pool.wait_ge(s_w, 80)
                for t in range(ET):
                    for s, idx in enumerate((src_i, dst_i)):
                        wait_count(pool, s_turn, 2 * (t - 1) + s + 1)
                        nc.gpsimd.indirect_dma_start(
                            m[s][:, :], None, x2_d[0:N, :],
                            bass.IndirectOffsetOnAxis(ap=idx[:, t:t + 1], axis=0)).then_inc(m_in[s], 16)
                    wait_count(pool, s_et, t)
                    nc.gpsimd.indirect_dma_start(
                        ea[:, :], None, edge_attr[:, :],
                        bass.IndirectOffsetOnAxis(ap=edge_i[:, t:t + 1], axis=0)).then_inc(s_ea, 16)
                    for s in range(2):
                        v = 2 * t + s
                        norm.on_pool(pool, v, s, [(s_row, v - 1)])
                    mish.on_pool(pool, r[:, :], first_no(t))
                    if t >= 1:
                        mish.on_pool(pool, r[:, :], second_no(t - 1))
                mish.on_pool(pool, r[:, :], second_no(ET - 1))

            @block.vector
            def _(dve):
                dve.wait_ge(s_w, 80)
                nc.vector.tensor_scalar(out=f[:, :], in0=down[:, u_edge:u_edge + 1], scalar1=1.0 / SCALE_LN,
                                        scalar2=None, op0=MUL).then_inc(s_f, 1)
                nc.vector.tensor_scalar(out=w1c[:, :], in0=w1c[:, :], scalar1=up[0:ED, u_edge:u_edge + 1],
                                        scalar2=SCALE_LN, op0=MUL, op1=MUL).then_inc(s_wc, 1)
                dve.wait_ge(s_f, 1)

                def load_stage(t, k, b):
                    for s in range(2):
                        dve.wait_ge(m_in[s], 16 * (t + 1))
                        norm.on_vector(dve, m[s][:, :], 2 * t + s, s)

                def split(t, k, b):
                    dve.wait_ge(s_et, t + 1)
                    wait_count(dve, s_mm1, t)
                    nc.vector.tensor_copy(eaT[:, :], ps_e[0:ED, 0:P]).then_inc(s_eT, 1)
                    for s in range(2):
                        dve.wait_ge(s_hi, 2 * t + s + 1)
                        nc.vector.scalar_tensor_tensor(out=hT[s][:, D:2 * D], in0=ps_t[s][:, :],
                                                       scalar=SCALE_LN, in1=hT[s][:, 0:D], op0=MUL,
                                                       op1=SUB).then_inc(s_lo, 1)

                def first(t, k, b):
                    dve.wait_ge(s_mm1, t + 1)
                    if started(2, t):
                        dve.wait_ge(s_out, 16 * (t - 1))
                    nc.vector.scalar_tensor_tensor(out=r[:, :], in0=ps_1[:, :], scalar=f[:, 0:1],
                                                   in1=bias1[:, :], op0=MUL, op1=ADD).then_inc(s_r, 1)
                    dve.wait_ge(s_r, first_no(t) + 1)
                    mish.on_vector(dve, r[:, :], m1[:, :], first_no(t))

                def second(t, k, b):
                    dve.wait_ge(s_mm2, t + 1)
                    dve.wait_ge(s_mt, next_of(t))
                    nc.vector.tensor_tensor(out=r[:, :], in0=ps_2[:, :], in1=bias2[:, :], op=ADD).then_inc(s_r, 1)
                    dve.wait_ge(s_r, second_no(t) + 1)
                    mish.on_vector(dve, r[:, :], msg[:, :], second_no(t))

                def body(t, k, b):
                    load_stage(t, k, b)
                    split(t, k, b)
                    first(t, k, b)
                    if started(1, t):
                        second(*ago(1, t, k, b))
                each_tile(dve, ET, body)
                dve.wait_ge(s_out, 16 * (ET - 1))
                second(*last(ET, 1)[0])

            @block.scalar
            def _(act):
                def body(t, k, b):
                    for s in range(2):
                        act.wait_ge(norm.s_ready, 2 * t + s + 1)
                        nc.scalar.activation(m[s][:, :], m[s][:, :], ACT.Relu, scale=norm.rstd[s][:, 0:1],
                                             bias=norm.shift[s][:, 0:1]).then_inc(s_row, 1)
                    for s in range(2):
                        act.wait_ge(s_turn, 2 * t + s + 1)
                        wait_count(act, s_mm2, t)
                        nc.scalar.activation(hT[s][:, 0:D], ps_t[s][:, :], ACT.Copy, scale=SCALE_LN)\
                            .then_inc(s_hi, 1)
                    mish.on_scalar(act, first_no(t))
                    if started(1, t):
                        mish.on_scalar(act, second_no(ago(1, t, k, b)[0]))
                    act.wait_ge(s_mt, t + 1)
                    wait_count(act, s_mm2, t)
                    nc.scalar.activation(mT[:, :], ps_m[:, :], ACT.Copy).then_inc(s_mT, 1)
                each_tile(act, ET, body)
                mish.on_scalar(act, second_no(ET - 1))

            @block.tensor
            def _(pe):
                pe.wait_ge(s_w, 80)
                pe.wait_ge(s_wc, 1)

                def hidden(t, k, b):
                    pe.wait_ge(s_lo, 2 * t + 2)
                    pe.wait_ge(s_eT, t + 1)
                    wait_count(pe, s_r, first_no(t))
                    nc.tensor.matmul(ps_1[:, :], eaT[:, :], w1c[:, :], start=True, stop=False)
                    product(pe, ps_1[:, :], lambda c: hT[c // C][:, (c % C) * P:(c % C + 1) * P],
                            lambda c: hT[c // C][:, D + (c % C) * P:D + (c % C + 1) * P], w1, D,
                            nchunks=2 * C, first=False).then_inc(s_mm1, 1)

                def output(t, k, b):
                    pe.wait_ge(s_mT, t + 1)
                    if started(1, t):
                        pe.wait_ge(s_r, 2 * t + 1)
                    for c in range(C):
                        ins = nc.tensor.matmul(ps_2[:, :], mT[:, c * P:(c + 1) * P],
                                               w2[:, c * D:(c + 1) * D], start=c == 0, stop=c == C - 1)
                    ins.then_inc(s_mm2, 1)

                def body(t, k, b):
                    for s in range(2):
                        pe.wait_ge(s_row, 2 * t + s + 1)
                        wait_count(pe, s_lo, 2 * (t - 1) + s + 1)
                        transposes(pe, ps_t[s], m[s]).then_inc(s_turn, 1)
                    pe.wait_ge(s_ea, 16 * (t + 1))
                    wait_count(pe, s_eT, t)
                    nc.tensor.matmul(ps_e[0:ED, 0:P], ea[:, :], ident[:, :], start=True, stop=True)\
                        .then_inc(s_et, 1)
                    hidden(t, k, b)
                    pe.wait_ge(mish.s_u, first_no(t) + 1)
                    wait_count(pe, s_mT, t)
                    transposes(pe, ps_m, m1).then_inc(s_mt, 1)
                    output(t, k, b)
                each_tile(pe, ET, body)

    def node_update():
        with ExitStack() as ctx:
            w3 = sb(ctx, "u_w3", [P, 2 * cols["update"]], F16)
            w4 = sb(ctx, "u_w4", [P, C * D])
            bias3, bias4, gam, bet = (sb(ctx, f"u_{n}", [P, D]) for n in ("bias3", "bias4", "gam", "bet"))
            g = sb(ctx, "u_g", [P, D])
            x2 = sb(ctx, "u_x2", [P, D])
            r = sb(ctx, "u_r", [P, D])
            u = sb(ctx, "u_u", [P, D])
            uT = sb(ctx, "u_uT", [P, D])
            h3 = sb(ctx, "u_h3", [P, D])
            f = sb(ctx, "u_f", [P, 1])
            ps_z = [ps(ctx, f"u_ps_z{b}") for b in range(2)]
            ps_u, ps_o = ps(ctx, "u_ps_u"), ps(ctx, "u_ps_o")
            ps_t = [ps(ctx, f"u_ps_t{b}") for b in range(2)]
            (s_w, s_f, s_mm, s_bias, s_r, s_ut, s_uT, s_mm4, s_h3, s_h3b, s_y, s_yn, s_xb, s_yg, s_x3,
             s_h4, s_turn, s_hi, s_lo, s_gin, s_xin, s_xout) = sems(
                "u", "w f mm bias r ut uT mm4 h3 h3b y yn xb yg x3 h4 turn hi lo gin xin xout")
            norm2, normy, norm3 = Norm(ctx, "u_n2"), Norm(ctx, "u_ny"), Norm(ctx, "u_n3")
            mish = Mish(ctx, "u_mish")
            u_no = unit_no["update"]
            block = ctx.enter_context(nc.Block())

            @block.sync
            def _(sp):
                sp.dma_start(w3[:, :], split_d["update"][:, :]).then_inc(s_w, 16)
                sp.dma_start(w4[:, :].rearrange("p (c n) -> p c n", c=C),
                             W4.rearrange("(c p) n -> p c n", p=P)).then_inc(s_w, 16)
                for tile, vec in ((bias3, b3), (bias4, b4), (gam, gamma2), (bet, beta2)):
                    sp.dma_start(tile[:, :], wide(vec)).then_inc(s_w, 16)

                def body(t, k, b):
                    n = rows_of(t)
                    wait_count(sp, s_r, t)
                    sp.dma_start(g[0:n, :], rows(agg_d, t)).then_inc(s_gin, 16)
                    if started(1, t):
                        store(*ago(1, t, k, b))
                    wait_count(sp, s_xout, 16 * t)
                    wait_count(sp, s_h4, t)
                    sp.dma_start(x2[0:n, :], rows(x2_d, t)).then_inc(s_xin, 16)

                def store(t, k, b):
                    sp.wait_ge(s_x3, t + 1)
                    sp.dma_start(rows(x3_d, t), x2[0:rows_of(t), :]).then_inc(s_xout, 16)
                each_tile(sp, NT, body)
                store(*last(NT, 1)[0])
                sp.wait_ge(s_xout, 16 * NT)

            @block.gpsimd
            def _(pool):
                pool.wait_ge(s_w, 96)

                def body(t, k, b):
                    pool.wait_ge(s_gin, 16 * (t + 1))
                    nc.gpsimd.tensor_tensor(out=g[:, :], in0=g[:, :], in1=bias3[:, :], op=ADD).then_inc(s_bias, 1)
                    norm2.on_pool(pool, t, b, [(s_h3, t - 1)])
                    mish.on_pool(pool, r[:, :], t)
                    pool.wait_ge(s_h3, t + 1)
                    nc.gpsimd.tensor_tensor(out=h3[:, :], in0=h3[:, :], in1=bias4[:, :], op=ADD).then_inc(s_h3b, 1)
                    nc.gpsimd.tensor_tensor(out=x2[:, :], in0=x2[:, :], in1=bet[:, :], op=ADD).then_inc(s_xb, 1)
                    normy.on_pool(pool, t, b, [(s_yn, t - 1)])
                    pool.wait_ge(s_yn, t + 1)
                    nc.gpsimd.tensor_tensor(out=h3[:, :], in0=h3[:, :], in1=gam[:, :], op=MUL).then_inc(s_yg, 1)
                    norm3.on_pool(pool, t, b, [(s_h4, t - 1)])
                each_tile(pool, NT, body)

            @block.vector
            def _(dve):
                nc.vector.tensor_scalar(out=f[:, :], in0=down[:, u_no:u_no + 1], scalar1=1.0 / SCALE_LN,
                                        scalar2=None, op0=MUL).then_inc(s_f, 1)
                dve.wait_ge(s_f, 1)

                def body(t, k, b):
                    dve.wait_ge(s_xin, 16 * (t + 1))
                    norm2.on_vector(dve, x2[:, :], t, b)
                    dve.wait_ge(s_mm, t + 1)
                    dve.wait_ge(s_bias, t + 1)
                    nc.vector.scalar_tensor_tensor(out=r[:, :], in0=ps_z[b][:, :], scalar=f[:, 0:1],
                                                   in1=g[:, :], op0=MUL, op1=ADD).then_inc(s_r, 1)
                    dve.wait_ge(s_r, t + 1)
                    wait_count(dve, s_ut, t)
                    mish.on_vector(dve, r[:, :], u[:, :], t)
                    if started(1, t):
                        lo(*ago(1, t, k, b))
                    dve.wait_ge(s_mm4, t + 1)
                    dve.wait_ge(s_h3b, t + 1)
                    nc.vector.tensor_tensor(out=h3[:, :], in0=ps_o[:, :], in1=h3[:, :], op=ADD).then_inc(s_y, 1)
                    dve.wait_ge(s_y, t + 1)
                    normy.on_vector(dve, h3[:, :], t, b)
                    dve.wait_ge(s_yg, t + 1)
                    dve.wait_ge(s_xb, t + 1)
                    nc.vector.tensor_tensor(out=x2[:, :], in0=x2[:, :], in1=h3[:, :], op=ADD).then_inc(s_x3, 1)
                    dve.wait_ge(s_x3, t + 1)
                    norm3.on_vector(dve, x2[:, :], t, b)

                def lo(t, k, b):
                    dve.wait_ge(s_hi, t + 1)
                    nc.vector.scalar_tensor_tensor(out=slot_lo(t), in0=ps_t[b][:, :], scalar=SCALE_LN,
                                                   in1=slot_hi(t), op0=MUL, op1=SUB).then_inc(s_lo, 1)
                each_tile(dve, NT, body)
                lo(*last(NT, 1)[0])

            @block.scalar
            def _(act):
                def hi(t, k, b):
                    act.wait_ge(s_turn, t + 1)
                    nc.scalar.activation(slot_hi(t), ps_t[b][:, :], ACT.Copy, scale=SCALE_LN).then_inc(s_hi, 1)

                def body(t, k, b):
                    act.wait_ge(norm2.s_ready, t + 1)
                    wait_count(act, s_x3, t)
                    nc.scalar.activation(h3[:, :], x2[:, :], ACT.Relu, scale=norm2.rstd[b][:, 0:1],
                                         bias=norm2.shift[b][:, 0:1]).then_inc(s_h3, 1)
                    mish.on_scalar(act, t)
                    if started(1, t):
                        hi(*ago(1, t, k, b))
                    act.wait_ge(s_ut, t + 1)
                    wait_count(act, s_mm4, t)
                    nc.scalar.activation(uT[:, :], ps_u[:, :], ACT.Copy).then_inc(s_uT, 1)
                    act.wait_ge(normy.s_ready, t + 1)
                    nc.scalar.activation(h3[:, :], h3[:, :], ACT.Identity, scale=normy.rstd[b][:, 0:1],
                                         bias=normy.shift[b][:, 0:1]).then_inc(s_yn, 1)
                    act.wait_ge(norm3.s_ready, t + 1)
                    nc.scalar.activation(r[:, :], x2[:, :], ACT.Relu, scale=norm3.rstd[b][:, 0:1],
                                         bias=norm3.shift[b][:, 0:1]).then_inc(s_h4, 1)
                each_tile(act, NT, body)
                hi(*last(NT, 1)[0])

            @block.tensor
            def _(pe):
                pe.wait_ge(s_w, 96)

                def update(t, b):
                    wait_count(pe, s_r, t - 1)
                    product(pe, ps_z[b][:, :], lambda c: slots16[:, bass.ds(t * 2 * D + c * P, P)],
                            lambda c: slots16[:, bass.ds(t * 2 * D + D + c * P, P)], w3, D).then_inc(s_mm, 1)

                def body(t, k, b):
                    update(t, b)
                    pe.wait_ge(mish.s_u, t + 1)
                    wait_count(pe, s_uT, t)
                    transposes(pe, ps_u, u).then_inc(s_ut, 1)
                    pe.wait_ge(s_uT, t + 1)
                    wait_count(pe, s_y, t)
                    for c in range(C):
                        ins = nc.tensor.matmul(ps_o[:, :], uT[:, c * P:(c + 1) * P],
                                               w4[:, c * D:(c + 1) * D], start=c == 0, stop=c == C - 1)
                    ins.then_inc(s_mm4, 1)
                    pe.wait_ge(s_h4, t + 1)
                    wait_count(pe, s_lo, t - 1)
                    transposes(pe, ps_t[b], r).then_inc(s_turn, 1)
                each_tile(pe, NT, body)

    def batch_rows(pilot, shiftb, sum1, sum2):
        phase = "zp" if pilot else "z"
        with ExitStack() as ctx:
            w = sb(ctx, f"{phase}_w", [P, 2 * cols["root"]], F16)
            g = [sb(ctx, f"{phase}_g{b}", [P, D]) for b in range(2)]
            sq = [sb(ctx, f"{phase}_sq{b}", [P, D]) for b in range(2)]
            ones = sb(ctx, f"{phase}_ones", [P, P])
            f = sb(ctx, f"{phase}_f", [P, 1])
            ps_z = [ps(ctx, f"{phase}_ps_z{b}") for b in range(2)]
            ps_m = ps(ctx, f"{phase}_ps_m")
            s_w, s_f, s_mm, s_bias, s_z, s_sq, s_s1, s_s2, s_mean = sems(
                phase, "w f mm bias z sq s1 s2 mean")
            g_in = pair(phase, "gin")
            nt = 1 if pilot else NT
            u_no = unit_no["root"]
            zrow = (lambda t: sq[0][:, :]) if pilot else slot
            block = ctx.enter_context(nc.Block())

            @block.sync
            def _(sp):
                sp.dma_start(w[:, :], split_d["root"][:, :]).then_inc(s_w, 16)
                if pilot:
                    sp.dma_start(shiftb[:, :], wide(bl)).then_inc(s_w, 16)
                    sp.dma_start(g[0][:, :], rows(agg_d, 0)).then_inc(g_in[0], 16)
                    return

                def body(t, k, b):
                    wait_count(sp, s_z, t - 1)
                    sp.dma_start(g[b][0:rows_of(t), :], rows(agg_d, t)).then_inc(g_in[b], 16)
                each_tile(sp, NT, body)

            @block.gpsimd
            def _(pool):
                if pilot:
                    nc.gpsimd.memset(ones[:, :], 1.0 / P).then_inc(s_mean, 1)
                    pool.wait_ge(s_w, 32)
                    pool.wait_ge(g_in[0], 16)
                    nc.gpsimd.tensor_tensor(out=g[0][:, :], in0=g[0][:, :], in1=shiftb[:, :], op=ADD)\
                        .then_inc(s_bias, 1)
                    return

                def body(t, k, b):
                    pool.wait_ge(g_in[b], 16 * (k + 1))
                    nc.gpsimd.tensor_tensor(out=g[b][:, :], in0=g[b][:, :], in1=shiftb[:, :], op=ADD)\
                        .then_inc(s_bias, 1)
                each_tile(pool, NT, body)

            @block.vector
            def _(dve):
                nc.vector.tensor_scalar(out=f[:, :], in0=down[:, u_no:u_no + 1], scalar1=1.0 / SCALE_LN,
                                        scalar2=None, op0=MUL).then_inc(s_f, 1)
                dve.wait_ge(s_f, 1)

                def z_of(t, k, b):
                    dve.wait_ge(s_mm, t + 1)
                    dve.wait_ge(s_bias, t + 1)
                    nc.vector.scalar_tensor_tensor(out=zrow(t), in0=ps_z[b][:, :], scalar=f[:, 0:1],
                                                   in1=g[b][:, :], op0=MUL, op1=ADD).then_inc(s_z, 1)
                if pilot:
                    z_of(0, 0, 0)
                    dve.wait_ge(s_mean, 2)
                    nc.vector.tensor_tensor(out=shiftb[:, :], in0=shiftb[:, :], in1=ps_m[:, :], op=SUB)\
                        .then_inc(s_s1, 1)
                    dve.wait_ge(s_s1, 1)
                    return
                nc.vector.memset(sum1[:, :], 0.0)
                nc.vector.memset(sum2[:, :], 0.0).then_inc(s_f, 1)
                dve.wait_ge(s_f, 2)

                def squares(t, k, b):
                    n = rows_of(t)
                    dve.wait_ge(s_sq, t + 1)
                    wait_count(dve, s_s2, t)
                    nc.vector.tensor_tensor(out=sum2[0:n, :], in0=sum2[0:n, :], in1=sq[b][0:n, :], op=ADD)\
                        .then_inc(s_s2, 1)

                def body(t, k, b):
                    n = rows_of(t)
                    z_of(t, k, b)
                    if started(1, t):
                        squares(*ago(1, t, k, b))
                    dve.wait_ge(s_z, t + 1)
                    wait_count(dve, s_s1, t)
                    nc.vector.tensor_tensor(out=sum1[0:n, :], in0=sum1[0:n, :], in1=slot(t)[0:n, :], op=ADD)\
                        .then_inc(s_s1, 1)
                each_tile(dve, NT, body)
                squares(*last(NT, 1)[0])

            @block.scalar
            def _(act):
                if pilot:
                    return

                def body(t, k, b):
                    act.wait_ge(s_z, t + 1)
                    wait_count(act, s_s2, t - 1)
                    nc.scalar.activation(sq[b][:, :], slot(t), ACT.Square).then_inc(s_sq, 1)
                each_tile(act, NT, body)

            @block.tensor
            def _(pe):
                pe.wait_ge(s_w, 32 if pilot else 16)

                def body(t, k, b):
                    wait_count(pe, s_z, t - 1)
                    product(pe, ps_z[b][:, :], lambda c: slots16[:, bass.ds(t * 2 * D + c * P, P)],
                            lambda c: slots16[:, bass.ds(t * 2 * D + D + c * P, P)], w, D).then_inc(s_mm, 1)
                if pilot:
                    body(0, 0, 0)
                    pe.wait_ge(s_z, 1)
                    pe.wait_ge(s_mean, 1)
                    nc.tensor.matmul(ps_m[:, :], ones[:, :], sq[0][:, :], start=True, stop=True).then_inc(s_mean, 1)
                else:
                    each_tile(pe, NT, body)

    def finish(sum1, sum2):
        with ExitStack() as ctx:
            ones = sb(ctx, "f_ones", [P, P])
            gam, bet, mean, var, a_row, b_row, half = (
                sb(ctx, f"f_{n}", [P, D]) for n in ("gam", "bet", "mean", "var", "a", "b", "half"))
            x3 = [sb(ctx, f"f_x{b}", [P, D]) for b in range(4)]
            ps_1, ps_2 = ps(ctx, "f_ps_1"), ps(ctx, "f_ps_2")
            s_w, s_mm, s_v, s_p, s_coef, s_za, s_zb, s_o, s_mem = sems("f", "w mm v p coef za zb o mem")
            x_in = [sem(f"f_in{b}") for b in range(4)]
            o_out = [sem(f"f_out{b}") for b in range(4)]
            block = ctx.enter_context(nc.Block())
            whole = NT // 4 * 4

            def by_four(eng, body):
                for t in range(4):
                    body(t, 0, t)
                with eng.Fori(1, NT // 4) as i:
                    for b in range(4):
                        body(4 * i + b, i, b)
                for t in range(whole, NT):
                    body(t, t // 4, t % 4)

            @block.sync
            def _(sp):
                sp.dma_start(gam[:, :], wide(gamma3)).then_inc(s_w, 16)
                sp.dma_start(bet[:, :], wide(beta3)).then_inc(s_w, 16)

                def body(t, k, b):
                    wait_count(sp, o_out[b], 16 * k)
                    sp.dma_start(x3[b][0:rows_of(t), :], rows(x3_d, t)).then_inc(x_in[b], 16)
                by_four(sp, body)

            @block.scalar
            def _(act):
                def body(t, k, b):
                    act.wait_ge(s_o, t + 1)
                    act.dma_start(rows(out, t), x3[b][0:rows_of(t), :]).then_inc(o_out[b], 16)
                by_four(act, body)
                for b in range(4):
                    act.wait_ge(o_out[b], 16 * ((NT - b + 3) // 4))

            @block.tensor
            def _(pe):
                pe.wait_ge(s_mem, 2)
                nc.tensor.matmul(ps_1[:, :], ones[:, :], sum1[:, :], start=True, stop=True)
                nc.tensor.matmul(ps_2[:, :], ones[:, :], sum2[:, :], start=True, stop=True).then_inc(s_mm, 1)

            @block.gpsimd
            def _(pool):
                nc.gpsimd.memset(ones[:, :], 1.0).then_inc(s_mem, 1)
                nc.gpsimd.memset(half[:, :], -0.5).then_inc(s_mem, 1)
                pool.wait_ge(s_mem, 2)
                pool.wait_ge(s_v, 4)
                nc.gpsimd.tensor_tensor(out=a_row[:, :], in0=var[:, :], in1=half[:, :], op=POW).then_inc(s_p, 1)
                pool.wait_ge(s_coef, 2)

                def body(t, k, b):
                    nc.gpsimd.tensor_tensor(out=slot(t), in0=slot(t), in1=a_row[:, :], op=MUL).then_inc(s_za, 1)
                by_four(pool, body)

            @block.vector
            def _(dve):
                dve.wait_ge(s_mm, 1)
                dve.wait_ge(s_w, 32)
                nc.vector.tensor_scalar(out=mean[:, :], in0=ps_1[:, :], scalar1=1.0 / N, scalar2=None,
                                        op0=MUL).then_inc(s_v, 1)
                dve.wait_ge(s_v, 1)
                nc.vector.tensor_tensor(out=b_row[:, :], in0=mean[:, :], in1=mean[:, :], op=MUL).then_inc(s_v, 1)
                dve.wait_ge(s_v, 2)
                nc.vector.scalar_tensor_tensor(out=var[:, :], in0=ps_2[:, :], scalar=1.0 / N, in1=b_row[:, :],
                                               op0=MUL, op1=SUB).then_inc(s_v, 1)
                dve.wait_ge(s_v, 3)
                nc.vector.tensor_scalar(out=var[:, :], in0=var[:, :], scalar1=0.0, scalar2=BN_EPS,
                                        op0=MAX, op1=ADD).then_inc(s_v, 1)
                dve.wait_ge(s_p, 1)
                nc.vector.tensor_tensor(out=a_row[:, :], in0=a_row[:, :], in1=gam[:, :], op=MUL).then_inc(s_coef, 1)
                dve.wait_ge(s_coef, 1)
                nc.vector.tensor_tensor(out=b_row[:, :], in0=mean[:, :], in1=a_row[:, :], op=MUL).then_inc(s_v, 1)
                dve.wait_ge(s_v, 5)
                nc.vector.tensor_tensor(out=b_row[:, :], in0=bet[:, :], in1=b_row[:, :], op=SUB).then_inc(s_coef, 1)
                dve.wait_ge(s_coef, 2)

                def body(t, k, b):
                    dve.wait_ge(s_za, t + 1)
                    nc.vector.tensor_tensor(out=slot(t), in0=slot(t), in1=b_row[:, :], op=ADD).then_inc(s_zb, 1)
                    dve.wait_ge(s_zb, t + 1)
                    dve.wait_ge(x_in[b], 16 * (k + 1))
                    nc.vector.scalar_tensor_tensor(out=x3[b][:, :], in0=slot(t), scalar=0.0, in1=x3[b][:, :],
                                                   op0=MAX, op1=ADD).then_inc(s_o, 1)
                by_four(dve, body)

    prepare_weights()
    prepare_graph()
    gcn_project()
    edge_sums_gcn()
    gcn_finish()
    recycle_semaphores()
    edge_products("a0", x1_d, True, True, True, SCALE_LN, "neigh0")
    sage_layer(0)
    edge_products("a1", h_d, True, False, True, SCALE_UNIT, "neigh1")
    sage_layer(1)
    edge_products("a2", h_d, True, False, True, SCALE_UNIT, "neigh2")
    sage_layer(2)
    recycle_semaphores()
    edge_network()
    edge_products("a3", msg_d, False, False, False, None, None, W3[D:2 * D, :])
    node_update()
    recycle_semaphores()
    edge_products("a4", x3_d, True, True, True, SCALE_LN, "aggr")
    shiftb, sum1, sum2 = (sb(top, n, [P, D]) for n in ("shiftb", "sum1", "sum2"))
    batch_rows(True, shiftb, sum1, sum2)
    batch_rows(False, shiftb, sum1, sum2)
    finish(sum1, sum2)
    top.close()


_INS = ["x", "src", "dst", "edge_attr_64", "L0_gnn_W_conv", "L0_gnn_b_conv", "L0_gnn_W_lin", "L0_gnn_b_lin",
        "L1_gnn_W_self", "L1_gnn_W_neigh", "L1_gnn_b", "L2_gnn_W1", "L2_gnn_b1", "L2_gnn_W2", "L2_gnn_b2",
        "L2_gnn_W3", "L2_gnn_b3", "L2_gnn_W4", "L2_gnn_b4", "L2_gnn_gamma", "L2_gnn_beta",
        "L3_gnn_W_l", "L3_gnn_b_l", "L3_gnn_W_r", "L3_gnn_gamma", "L3_gnn_beta"]


def kernel(**inputs):
    import numpy as _np
    import concourse.bacc as _bacc
    from concourse import mybir as _mybir
    from concourse.bass_utils import run_bass_kernel_spmd as _run

    nc = _bacc.Bacc("TRN2", target_bir_lowering=False, num_devices=1)
    arrays, args = {}, []
    for name in _INS:
        a = _np.asarray(inputs[name])
        if name in ("L3_gnn_W_l", "L3_gnn_W_r"):
            a = a.T
        a = _np.ascontiguousarray(a)
        arrays[f"in_{name}"] = a
        args.append(nc.dram_tensor(f"in_{name}", a.shape, _mybir.dt.from_np(a.dtype), kind="ExternalInput").ap())
    out = nc.dram_tensor("out_rows", (N, D), F32, kind="ExternalOutput").ap()
    gnn_program(nc, *args, out)
    r = _run(nc, [arrays], core_ids=[0])
    return r.results[0]["out_rows"]
```

```python
from contextlib import ExitStack

import concourse.bass as bass
from concourse import mybir

P = 128
F32 = mybir.dt.float32
F16 = mybir.dt.float16
BF16 = mybir.dt.bfloat16
I32 = mybir.dt.int32
ALU = mybir.AluOpType
ACT = mybir.ActivationFunctionType
AX = mybir.AxisListType
ADD, SUB, MUL, MAX, MIN, POW = ALU.add, ALU.subtract, ALU.mult, ALU.max, ALU.min, ALU.pow

N, D, E, ED, HID = 10000, 512, 2500, 64, 128
C = D // P
NT = -(-N // P)
TAIL = N - (NT - 1) * P
NPAD = NT * P
EPT = P - 1
ET = -(-E // EPT)
EQ = 20
EP = E // EQ
assert EP * EQ == E and EP <= P
NOWHERE = 2 * N
LN_EPS, NORM_EPS, BN_EPS = 1e-5, 1e-12, 1e-5
PEEL = 6
SCALE_LN = 2.0 ** 11
SCALE_UNIT = 2.0 ** 15
MISH_CAP = 10.0


def wait_count(eng, sem, n):
    if not isinstance(n, int) or n > 0:
        eng.wait_ge(sem, n)


def each_tile(eng, n, body):
    for t in range(PEEL):
        body(t, t // 2, t % 2)
    with eng.Fori(PEEL // 2, n // 2) as i:
        body(2 * i, i, 0)
        body(2 * i + 1, i, 1)
    if n % 2:
        body(n - 1, n // 2, 0)


def ago(n, t, k, b):
    for _ in range(n):
        t, k, b = t - 1, (k if b else k - 1), 1 - b
    return t, k, b


def started(n, t):
    return not isinstance(t, int) or t >= n


def last(n, lag):
    return [(t, t // 2, t % 2) for t in range(n - lag, n)]


class Tile:

    def __init__(self, i, j):
        self.i, self.j = (i + j // 4 if j // 4 else i), j % 4
        self.t = 4 * self.i + self.j

    def buf(self, n):
        return self.j % n

    def uses(self, n):
        if n == 1:
            return self.t
        return self.i if n == 4 else 2 * self.i + self.j // 2

    def later(self, n):
        return Tile(self.i, self.j + n)


def pipeline(eng, n, *stages, peel=12):
    def step(t):
        for lag, stage in stages:
            tile = t.later(-lag)
            if not isinstance(tile.i, int) or 0 <= tile.t < n:
                stage(tile)

    for t in range(min(peel, n)):
        step(Tile(t // 4, t % 4))
    whole = max(n // 4 * 4, peel)
    if whole > peel:
        with eng.Fori(peel // 4, whole // 4) as i:
            for j in range(4):
                step(Tile(i, j))
    for t in range(min(whole, n) if n < peel else whole, n + max(lag for lag, _ in stages)):
        step(Tile(t // 4, t % 4))


def gnn_program(nc, x, src, dst, edge_attr, Wc, bc, Wlin, blin, Wself, Wneigh, bsage, W1, b1, W2, b2,
                W3, b3, W4, b4, gamma2, beta2, WlT, bl, WrT, gamma3, beta3, out):
    top = ExitStack()

    def dram(name, shape, dt=F32):
        return nc.dram_tensor(name, shape, dt, kind="Internal").ap()

    hw_d = dram("hw_rows", [NPAD, HID])
    gcn_d = dram("gcn_sums", [NPAD, HID])
    agg_d = dram("neighbour_rows", [NPAD, D])
    x1_d = dram("x1_rows", [NPAD, D])
    x2_d = dram("x2_rows", [NPAD, D])
    x3_d = dram("x3_rows", [NPAD, D])
    h_d = dram("sage_rows", [NPAD, D])
    msg_d = dram("message_rows", [ET * P, D])
    rec_d = dram("edge_records", [ET * P, 8])
    cnt_d = dram("in_degree", [NPAD, 1])
    sel_d = dram("selections", [P, ET * 2 * P])

    units = {"conv": (Wc, 1), **{f"self{l}": (Wself[l], 1) for l in range(3)},
             **{f"neigh{l}": (Wneigh[l], 1) for l in range(3)},
             "edge": (W1[0:2 * D, :], 2), "update": (W3[0:D, :], 1), "aggr": (WlT, 1), "root": (WrT, 1)}
    unit_no = {name: n for n, name in enumerate(units)}
    cols = {name: w.shape[0] // P * w.shape[1] for name, (w, _) in units.items()}
    split_d = {name: dram(f"split_{name}", [P, 2 * cols[name]], F16) for name in units}
    NU = len(units)

    def sb(ctx, name, shape, dt=F32):
        return ctx.enter_context(nc.sbuf_tensor(name, shape, dt))

    def ps(ctx, name, shape=(P, D)):
        return ctx.enter_context(nc.psum_tensor(name, list(shape), F32))

    taken = []

    def sem(name):
        taken.append(nc.alloc_semaphore(name))
        return taken[-1]

    def sems(phase, names):
        return [sem(f"{phase}_{n}") for n in names.split()]

    def pair(phase, name, n=2):
        return [sem(f"{phase}_{name}{b}") for b in range(n)]

    def recycle_semaphores():
        nc.clear_and_free_semaphores(taken)
        taken.clear()
        nc.all_engine_barrier()

    slots = sb(top, "slots", [P, NT * D])
    ident = sb(top, "ident", [P, P])
    dis = sb(top, "dis", [P, NT])
    src_i = sb(top, "src_i", [P, ET], I32)
    dst_i = sb(top, "dst_i", [P, ET], I32)
    put_i = sb(top, "put_i", [P, ET], I32)
    edge_i = sb(top, "edge_i", [P, ET], I32)
    up = sb(top, "up", [P, NU])
    down = sb(top, "down", [P, NU])
    eps_col = sb(top, "eps_col", [P, 1])
    minus_half = sb(top, "minus_half", [P, 1])
    minus_one = sb(top, "minus_one", [P, 1])
    two_col = sb(top, "two_col", [P, 1])
    unscale = sb(top, "unscale", [P, P], F16)
    slots16 = slots[:, :].bitcast(F16)

    def slot(t):
        return slots[:, bass.ds(t * D, D)]

    def slot_hi(t):
        return slots16[:, bass.ds(t * 2 * D, D)]

    def slot_lo(t):
        return slots16[:, bass.ds(t * 2 * D + D, D)]

    def rows_of(t):
        return TAIL if isinstance(t, int) and t == NT - 1 else P

    def rows(ap, t):
        return ap[bass.ds(t * P, rows_of(t)), :]

    def wide(vec):
        return vec.rearrange("(o d) -> o d", o=1).to_broadcast([P, vec.shape[0]])

    def product(pe, out_ap, hi, lo, w, n, nchunks=C, first=True, stop=True):
        size = nchunks * n
        ins = None
        for c in range(nchunks):
            for m, (a, part) in enumerate(((hi, 0), (hi, 1), (lo, 0))):
                ins = nc.tensor.matmul(out_ap, a(c), w[:, part * size + c * n:part * size + (c + 1) * n],
                                       start=first and c == 0 and m == 0,
                                       stop=stop and c == nchunks - 1 and m == 2)
        return ins

    def transposes(pe, out_ap, in_ap):
        for c in range(C):
            ins = nc.tensor.transpose(out_ap[:, c * P:(c + 1) * P], in_ap[:, c * P:(c + 1) * P], ident[:, :])
        return ins

    def prepare_weights():
        with ExitStack() as ctx:
            mx = sb(ctx, "w_mx", [P, NU])
            mxa = sb(ctx, "w_mxa", [P, NU])
            ex = sb(ctx, "w_ex", [P, NU], I32)
            fld = sb(ctx, "w_fld", [P, NU], I32)
            inv = sb(ctx, "w_inv", [P, NU], I32)
            parts = [sb(ctx, f"w_parts{b}", [P, 2 * 2 * C * D], F16) for b in range(2)]
            zid, made, s_max, s_all, s_exp, s_up, s_hi, s_lo = sems("w", "zid made max all exp up hi lo")
            loaded = [sem(f"w_in{n}") for n in range(NU)]
            stored = pair("w", "out")
            base, at = {}, 0
            for name in units:
                base[name] = at
                at += cols[name]
            assert at <= NT * D
            block = ctx.enter_context(nc.Block())

            def raw(name):
                return slots[:, base[name]:base[name] + cols[name]]

            @block.sync
            def _(sp):
                for n, (name, (w, _)) in enumerate(units.items()):
                    sp.dma_start(raw(name).rearrange("p (c m) -> p c m", m=w.shape[1]),
                                 w.rearrange("(c p) m -> p c m", p=P)).then_inc(loaded[n], 16)
                for n, name in enumerate(units):
                    sp.wait_ge(s_lo, n + 1)
                    sp.dma_start(split_d[name][:, :], parts[n % 2][:, 0:2 * cols[name]]).then_inc(
                        stored[n % 2], 16)
                for b in range(2):
                    sp.wait_ge(stored[b], 16 * ((NU + 1 - b) // 2))

            @block.gpsimd
            def _(pool):
                nc.gpsimd.memset(ident[:, :], 0.0).then_inc(zid, 1)
                nc.gpsimd.memset(eps_col[:, :], LN_EPS)
                nc.gpsimd.memset(minus_half[:, :], -0.5)
                nc.gpsimd.memset(minus_one[:, :], -1.0)
                nc.gpsimd.memset(two_col[:, :], 2.0)
                pool.wait_ge(zid, 1)
                nc.gpsimd.affine_select(out=ident[:, :], in_=ident[:, :], compare_op=ALU.not_equal, fill=1.0,
                                        base=0, pattern=[[-1, P]], channel_multiplier=1).then_inc(made, 1)
                nc.gpsimd.memset(unscale[:, :], 0.0).then_inc(zid, 1)
                pool.wait_ge(zid, 2)
                nc.gpsimd.affine_select(out=unscale[:, :], in_=unscale[:, :], compare_op=ALU.not_equal,
                                        fill=1.0 / SCALE_LN, base=0, pattern=[[-1, P]],
                                        channel_multiplier=1).then_inc(made, 1)
                pool.wait_ge(s_max, NU)
                nc.gpsimd.partition_all_reduce(mxa[:, :], mx[:, :], P, bass.bass_isa.ReduceOp.max).then_inc(s_all, 1)
                pool.wait_ge(made, 2)

            @block.vector
            def _(dve):
                for n, name in enumerate(units):
                    dve.wait_ge(loaded[n], 16)
                    nc.vector.tensor_reduce(out=mx[:, n:n + 1], in_=raw(name), op=MAX, axis=AX.X,
                                            apply_absolute_value=True).then_inc(s_max, 1)
                dve.wait_ge(s_all, 1)
                nc.vector.tensor_scalar(out=ex[:, :], in0=mxa[:, :].bitcast(I32), scalar1=23, scalar2=None,
                                        op0=ALU.logical_shift_right).then_inc(s_exp, 1)
                dve.wait_ge(s_exp, 1)
                nc.vector.tensor_scalar(out=fld[:, :], in0=ex[:, :], scalar1=-1.0, scalar2=268.0,
                                        op0=MUL, op1=ADD).then_inc(s_exp, 1)
                dve.wait_ge(s_exp, 2)
                nc.vector.tensor_scalar(out=ex[:, :], in0=fld[:, :], scalar1=253.0, scalar2=1.0,
                                        op0=MIN, op1=MAX).then_inc(s_exp, 1)
                dve.wait_ge(s_exp, 3)
                nc.vector.tensor_scalar(out=inv[:, :], in0=ex[:, :], scalar1=-1.0, scalar2=254.0,
                                        op0=MUL, op1=ADD).then_inc(s_exp, 1)
                nc.vector.tensor_scalar(out=up[:, :].bitcast(I32), in0=ex[:, :], scalar1=23, scalar2=None,
                                        op0=ALU.logical_shift_left).then_inc(s_up, 1)
                dve.wait_ge(s_exp, 4)
                nc.vector.tensor_scalar(out=down[:, :].bitcast(I32), in0=inv[:, :], scalar1=23, scalar2=None,
                                        op0=ALU.logical_shift_left).then_inc(s_up, 1)
                dve.wait_ge(s_up, 2)
                for n, name in enumerate(units):
                    dve.wait_ge(s_hi, n + 1)
                    m = cols[name]
                    nc.vector.scalar_tensor_tensor(out=parts[n % 2][:, m:2 * m], in0=raw(name),
                                                   scalar=up[:, n:n + 1], in1=parts[n % 2][:, 0:m],
                                                   op0=MUL, op1=SUB).then_inc(s_lo, 1)

            @block.scalar
            def _(act):
                act.wait_ge(s_up, 2)
                for n, name in enumerate(units):
                    wait_count(act, stored[n % 2], 16 * (n // 2))
                    nc.scalar.activation(parts[n % 2][:, 0:cols[name]], raw(name), ACT.Copy,
                                         scale=up[:, n:n + 1]).then_inc(s_hi, 1)

    def prepare_graph():
        with ExitStack() as ctx:
            ZW = NT * D // 8
            zeros = sb(ctx, "g_zeros", [P, ZW])
            row_i = sb(ctx, "g_row_i", [P, E], I32)
            row_f = slots[:, 0:E]
            number = slots[:, E:2 * E]
            same = slots[:, 2 * E:3 * E]
            junk = slots[:, 3 * E:4 * E]
            junk2 = slots[:, 4 * E:5 * E]
            col_i = sb(ctx, "g_col_i", [P, EQ], I32)
            scol_i = sb(ctx, "g_scol_i", [P, EQ], I32)
            col_f = sb(ctx, "g_col_f", [P, EQ])
            neg_f = sb(ctx, "g_neg_f", [P, EQ])
            mine = sb(ctx, "g_mine", [P, EQ])
            sign = sb(ctx, "g_sign", [P, EQ])
            equal = sb(ctx, "g_equal", [P, EQ])
            before = sb(ctx, "g_before", [P, EQ])
            start = sb(ctx, "g_start", [P, EQ])
            rank = sb(ctx, "g_rank", [P, EQ])
            whole = [sb(ctx, f"g_whole{b}", [P, EQ]) for b in range(2)]
            put_f = sb(ctx, "g_put_f", [P, EQ])
            is_last = sb(ctx, "g_is_last", [P, EQ])
            put_u = sb(ctx, "g_put_u", [P, EQ], I32)
            pos_u = sb(ctx, "g_pos_u", [P, EQ], I32)
            rec = sb(ctx, "g_rec", [P, EQ, 8])
            blank = sb(ctx, "g_blank", [P, ET, 8])
            recs = sb(ctx, "g_recs", [P, ET, 8])
            offs = sb(ctx, "g_offs", [P, ET])
            first_j = sb(ctx, "g_first_j", [P, ET])
            jrow = sb(ctx, "g_jrow", [P, P])
            tri = sb(ctx, "g_tri", [P, P])
            selT = [sb(ctx, f"g_selT{b}", [P, 2 * P]) for b in range(2)]
            sel = slots[:, 5 * E:5 * E + ET * 2 * P]
            cnt = sb(ctx, "g_cnt", [P, P])
            deg = sb(ctx, "g_deg", [P, NT])
            half = sb(ctx, "g_half", [P, NT])
            ps_sel = [ps(ctx, f"g_ps_sel{b}") for b in range(2)]
            ps_cnt = ps(ctx, "g_ps_cnt")
            (s_in, s_zero, s_made, s_cast, s_eq, s_sign, s_bef, s_col, s_ready, s_blank, s_rec, s_cntin,
             s_recs, s_put, s_selT, s_turn, s_sel, s_selout, s_cload, s_cT, s_deg, s_dis) = sems(
                "g", "in zero made cast eq sign bef col ready blank rec cntin recs put selT turn sel "
                "selout cload cT deg dis")
            block = ctx.enter_context(nc.Block())

            @block.sync
            def _(sp):
                sp.dma_start(row_i[:, :], wide(dst)).then_inc(s_in, 16)
                sp.dma_start(col_i[0:EP, :], dst.rearrange("(p q) -> p q", q=EQ)).then_inc(s_in, 16)
                sp.dma_start(scol_i[0:EP, :], src.rearrange("(p q) -> p q", q=EQ)).then_inc(s_in, 16)
                sp.wait_ge(s_made, 1)
                agg_v = agg_d.rearrange("(p a) d -> p (a d)", p=P)
                gcn_v = gcn_d.rearrange("(p a) d -> p (a d)", p=P)
                for q in range(8):
                    sp.dma_start(agg_v[:, q * ZW:(q + 1) * ZW], zeros[:, :]).then_inc(s_zero, 16)
                for q in range(2):
                    sp.dma_start(gcn_v[:, q * ZW:(q + 1) * ZW], zeros[:, :]).then_inc(s_zero, 16)
                sp.dma_start(cnt_d.rearrange("(p a) o -> p (a o)", p=P), zeros[:, 0:NT]).then_inc(s_blank, 16)
                sp.dma_start(rec_d.rearrange("(p a) f -> p a f", p=P), blank[:, :, :]).then_inc(s_blank, 16)
                sp.wait_ge(s_rec, 16 * EQ)
                sp.dma_start(recs[:, :, :], rec_d.rearrange("(t p) f -> p t f", p=P)).then_inc(s_recs, 16)
                sp.wait_ge(s_cntin, 16 * EQ)
                sp.dma_start(cnt[0:NT, :], cnt_d.rearrange("(t p) o -> t (p o)", p=P)).then_inc(s_cload, 16)
                sp.wait_ge(s_sel, ET)
                sp.dma_start(sel_d[:, :], sel).then_inc(s_selout, 16)
                sp.wait_ge(s_selout, 16)
                sp.wait_ge(s_zero, 160)

            @block.gpsimd
            def _(pool):
                nc.gpsimd.iota(number, pattern=[[1, E]], base=0, channel_multiplier=0,
                               allow_small_or_imprecise_dtypes=True).then_inc(s_col, 1)
                nc.gpsimd.iota(mine[:, :], pattern=[[1, EQ]], base=0, channel_multiplier=EQ,
                               allow_small_or_imprecise_dtypes=True).then_inc(s_col, 1)
                nc.gpsimd.iota(offs[:, :], pattern=[[EPT, ET]], base=-1, channel_multiplier=0,
                               allow_small_or_imprecise_dtypes=True).then_inc(s_col, 1)
                nc.gpsimd.iota(jrow[:, :], pattern=[[1, P]], base=0, channel_multiplier=0,
                               allow_small_or_imprecise_dtypes=True).then_inc(s_col, 1)
                nc.gpsimd.memset(tri[:, :], 1.0).then_inc(s_col, 1)
                nc.gpsimd.memset(half[:, :], -0.5).then_inc(s_col, 1)
                pool.wait_ge(s_col, 6)
                nc.gpsimd.affine_select(out=tri[:, :], in_=tri[:, :], compare_op=ALU.is_ge, fill=0.0, base=0,
                                        pattern=[[-1, P]], channel_multiplier=1).then_inc(s_col, 1)
                pool.wait_ge(s_blank, 32)
                pool.wait_ge(s_ready, 1)
                for q in range(EQ):
                    nc.gpsimd.indirect_dma_start(
                        rec_d[:, :], bass.IndirectOffsetOnAxis(ap=pos_u[0:EP, q:q + 1], axis=0),
                        rec[0:EP, q, :], None).then_inc(s_rec, 16)
                for q in range(EQ):
                    nc.gpsimd.indirect_dma_start(
                        cnt_d[:, :], bass.IndirectOffsetOnAxis(ap=put_u[0:EP, q:q + 1], axis=0),
                        equal[0:EP, q:q + 1], None, bounds_check=N - 1, oob_is_err=False).then_inc(s_cntin, 16)
                pool.wait_ge(s_deg, 1)
                nc.gpsimd.tensor_tensor(out=dis[:, :], in0=deg[:, :], in1=half[:, :], op=POW).then_inc(s_dis, 1)
                pool.wait_ge(s_dis, 1)

            @block.scalar
            def _(act):
                act.wait_ge(s_cast, 4)
                for q in range(EQ):
                    nc.scalar.activation(junk2[0:EP, :], row_f[0:EP, :], ACT.Sign, bias=neg_f[0:EP, q:q + 1],
                                         accum_out=sign[0:EP, q:q + 1]).then_inc(s_sign, 1)
                    act.wait_ge(s_sign, q + 1)
                for t in range(ET):
                    act.wait_ge(s_turn, t + 1)
                    nc.scalar.activation(sel[:, t * 2 * P:(t + 1) * 2 * P], ps_sel[t % 2][:, 0:2 * P],
                                         ACT.Copy).then_inc(s_sel, 1)

            @block.vector
            def _(dve):
                chain = s_put
                links = [0]

                def link(ins):
                    links[0] += 1
                    ins.then_inc(chain, 1)
                    dve.wait_ge(chain, links[0])

                nc.vector.memset(zeros[:, :], 0.0)
                nc.vector.memset(slot(NT - 1), 0.0)
                link(nc.vector.memset(blank[:, :, :], 0.0))
                nc.vector.memset(blank[:, :, 2], float(NOWHERE))
                nc.vector.memset(blank[:, :, 3], 1e6)
                link(nc.vector.memset(rec[:, :, :], 0.0))
                nc.vector.memset(cnt[:, :], 0.0).then_inc(s_made, 1)
                dve.wait_ge(s_in, 48)
                nc.vector.tensor_copy(row_f, row_i[:, :]).then_inc(s_cast, 1)
                nc.vector.tensor_copy(col_f[0:EP, :], col_i[0:EP, :]).then_inc(s_cast, 1)
                nc.vector.tensor_copy(rec[0:EP, :, 0], scol_i[0:EP, :]).then_inc(s_cast, 1)
                dve.wait_ge(s_cast, 3)
                nc.vector.tensor_scalar(out=neg_f[0:EP, :], in0=col_f[0:EP, :], scalar1=-1.0, scalar2=None,
                                        op0=MUL).then_inc(s_cast, 1)
                dve.wait_ge(s_col, 2)
                for q in range(EQ):
                    link(nc.vector.tensor_scalar(out=same[0:EP, :], in0=row_f[0:EP, :],
                                                 scalar1=col_f[0:EP, q:q + 1], scalar2=0.0, op0=ALU.is_equal,
                                                 op1=ADD, accum_out=equal[0:EP, q:q + 1]))
                    link(nc.vector.scalar_tensor_tensor(out=junk[0:EP, :], in0=number[0:EP, :],
                                                        scalar=mine[0:EP, q:q + 1], in1=same[0:EP, :],
                                                        op0=ALU.is_lt, op1=MUL,
                                                        accum_out=before[0:EP, q:q + 1]))
                dve.wait_ge(s_sign, EQ)
                a = slice(0, EP)
                link(nc.vector.tensor_tensor(out=start[a, :], in0=equal[a, :], in1=sign[a, :], op=ADD))
                link(nc.vector.tensor_scalar(out=start[a, :], in0=start[a, :], scalar1=-0.5, scalar2=0.5 * E,
                                             op0=MUL, op1=ADD))
                link(nc.vector.tensor_tensor(out=rank[a, :], in0=start[a, :], in1=before[a, :], op=ADD))
                link(nc.vector.tensor_scalar(out=whole[0][a, :], in0=rank[a, :], scalar1=1.0, scalar2=None, op0=ADD))
                for n in range(1, ET):
                    link(nc.vector.scalar_tensor_tensor(out=whole[n % 2][a, :], in0=rank[a, :],
                                                        scalar=float(n * EPT), in1=whole[(n - 1) % 2][a, :],
                                                        op0=ALU.is_ge, op1=ADD))
                link(nc.vector.tensor_copy(pos_u[a, :], whole[(ET - 1) % 2][a, :]))
                link(nc.vector.tensor_tensor(out=is_last[a, :], in0=equal[a, :], in1=before[a, :], op=SUB))
                link(nc.vector.tensor_scalar(out=is_last[a, :], in0=is_last[a, :], scalar1=1.0, scalar2=None,
                                             op0=ALU.is_equal))
                link(nc.vector.scalar_tensor_tensor(out=put_f[a, :], in0=col_f[a, :], scalar=-float(NOWHERE),
                                                    in1=is_last[a, :], op0=ADD, op1=MUL))
                link(nc.vector.tensor_scalar(out=rec[a, :, 2], in0=put_f[a, :], scalar1=float(NOWHERE),
                                             scalar2=None, op0=ADD))
                link(nc.vector.tensor_copy(put_u[a, :], rec[a, :, 2]))
                link(nc.vector.tensor_copy(rec[a, :, 1], col_f[a, :]))
                link(nc.vector.tensor_copy(rec[a, :, 3], start[a, :]))
                link(nc.vector.reciprocal(rec[a, :, 4], equal[a, :]))
                nc.vector.tensor_copy(rec[a, :, 5], mine[a, :]).then_inc(s_ready, 1)
                dve.wait_ge(s_recs, 16)
                nc.vector.tensor_copy(src_i[:, :], recs[:, :, 0])
                nc.vector.tensor_copy(dst_i[:, :], recs[:, :, 1])
                nc.vector.tensor_copy(put_i[:, :], recs[:, :, 2])
                nc.vector.tensor_copy(edge_i[:, :], recs[:, :, 5])
                dve.wait_ge(s_col, 7)
                link(nc.vector.tensor_tensor(out=first_j[:, :], in0=recs[:, :, 3], in1=offs[:, :], op=SUB))
                for t in range(ET):
                    wait_count(dve, s_turn, t - 1)
                    link(nc.vector.scalar_tensor_tensor(out=selT[t % 2][:, 0:P], in0=jrow[:, :],
                                                        scalar=first_j[:, t:t + 1], in1=tri[:, :],
                                                        op0=ALU.is_ge, op1=MUL))
                    nc.vector.tensor_scalar(out=selT[t % 2][:, P:2 * P], in0=selT[t % 2][:, 0:P],
                                            scalar1=recs[:, t, 4:5], scalar2=None, op0=MUL).then_inc(s_selT, 1)
                dve.wait_ge(s_cT, 1)
                nc.vector.tensor_scalar(out=deg[:, :], in0=ps_cnt[:, 0:NT], scalar1=1.0, scalar2=None,
                                        op0=ADD).then_inc(s_deg, 1)

            @block.tensor
            def _(pe):
                for t in range(ET):
                    pe.wait_ge(s_selT, t + 1)
                    wait_count(pe, s_sel, t - 1)
                    nc.tensor.transpose(ps_sel[t % 2][:, 0:P], selT[t % 2][:, 0:P], ident[:, :])
                    nc.tensor.transpose(ps_sel[t % 2][:, P:2 * P], selT[t % 2][:, P:2 * P],
                                        ident[:, :]).then_inc(s_turn, 1)
                pe.wait_ge(s_cload, 16)
                nc.tensor.transpose(ps_cnt[:, 0:P], cnt[:, :], ident[:, :]).then_inc(s_cT, 1)

    class Norm:
        def __init__(self, ctx, name):
            self.stats = [sb(ctx, f"{name}_st{b}", [P, 6]) for b in range(2)]
            self.mv = [sb(ctx, f"{name}_mv{b}", [P, 2]) for b in range(2)]
            self.ve = [sb(ctx, f"{name}_ve{b}", [P, 1]) for b in range(2)]
            self.rstd = [sb(ctx, f"{name}_rs{b}", [P, 1]) for b in range(2)]
            self.shift = [sb(ctx, f"{name}_sh{b}", [P, 1]) for b in range(2)]
            self.pause = sb(ctx, f"{name}_pause", [P, 1])
            self.nm = [sb(ctx, f"{name}_nm{b}", [P, 1]) for b in range(2)]
            self.s_stats, self.s_mv, self.s_ve, self.s_rstd, self.s_ready = sems(
                name, "stats mv ve rstd ready")

        def on_vector(self, dve, in_ap, t, b):
            nc.vector.bn_stats(self.stats[b][:, :], in_ap).then_inc(self.s_stats, 1)
            dve.wait_ge(self.s_stats, t + 1)
            wait_count(dve, self.s_ready, t - 1)
            nc.vector.memset(self.pause[:, :], 0.0)
            nc.vector.bn_aggr(self.mv[b][:, :], self.stats[b][:, :]).then_inc(self.s_mv, 1)

        def on_pool(self, pool, t, b, free=()):
            pool.wait_ge(self.s_mv, t + 1)
            nc.gpsimd.tensor_tensor(out=self.nm[b][:, :], in0=self.mv[b][:, 0:1], in1=minus_one[:, :], op=MUL)
            nc.gpsimd.tensor_tensor(out=self.ve[b][:, :], in0=self.mv[b][:, 1:2], in1=eps_col[:, :],
                                    op=ADD).then_inc(self.s_ve, 1)
            pool.wait_ge(self.s_ve, t + 1)
            for s, n in free:
                wait_count(pool, s, n)
            nc.gpsimd.tensor_tensor(out=self.rstd[b][:, :], in0=self.ve[b][:, :], in1=minus_half[:, :],
                                    op=POW).then_inc(self.s_rstd, 1)
            pool.wait_ge(self.s_rstd, t + 1)
            nc.gpsimd.tensor_tensor(out=self.shift[b][:, :], in0=self.nm[b][:, :], in1=self.rstd[b][:, :],
                                    op=MUL).then_inc(self.s_ready, 1)

        def stats_of(self, dve, in_ap, v):
            self.on_vector(dve, in_ap, v.t, v.buf(2))

        def factors(self, pool, v, s_used):
            self.on_pool(pool, v.t, v.buf(2), [(s_used, v.t - 1)])

    def gcn_project():
        with ExitStack() as ctx:
            w = sb(ctx, "p_w", [P, 2 * cols["conv"]], F16)
            h = [sb(ctx, f"p_h{b}", [P, D]) for b in range(2)]
            hT = [sb(ctx, f"p_hT{b}", [P, 2 * D], F16) for b in range(2)]
            hw = [sb(ctx, f"p_hw{b}", [P, HID]) for b in range(2)]
            f = sb(ctx, "p_f", [P, 1])
            dcol = [sb(ctx, f"p_dcol{b}", [P, 1]) for b in range(2)]
            ps_t = [ps(ctx, f"p_ps_t{b}") for b in range(2)]
            ps_h = [ps(ctx, f"p_ps_h{b}") for b in range(2)]
            s_w, s_f, s_h, s_turn, s_hi, s_lo, s_mm, s_dcol, s_hw = sems(
                "p", "w f h turn hi lo mm dcol hw")
            x_in, hw_out = pair("p", "xin"), pair("p", "hwout")
            norm = Norm(ctx, "p_norm")
            block = ctx.enter_context(nc.Block())

            @block.sync
            def _(sp):
                sp.dma_start(w[:, :], split_d["conv"][:, :]).then_inc(s_w, 16)

                def store(t, k, b):
                    sp.wait_ge(s_hw, t + 1)
                    sp.dma_start(rows(hw_d, t), hw[b][0:rows_of(t), :]).then_inc(hw_out[b], 16)

                def body(t, k, b):
                    wait_count(sp, norm.s_stats, t - 1)
                    r = rows_of(t)
                    sp.dma_start(slot(t)[0:r, :], rows(x, t)).then_inc(x_in[b], 16)
                    if started(3, t):
                        store(*ago(3, t, k, b))
                each_tile(sp, NT, body)
                for tile in last(NT, 3):
                    store(*tile)
                sp.wait_ge(hw_out[0], 16 * ((NT + 1) // 2))
                sp.wait_ge(hw_out[1], 16 * (NT // 2))

            @block.vector
            def _(dve):
                nc.vector.tensor_scalar(out=f[:, :], in0=down[:, unit_no["conv"]:unit_no["conv"] + 1],
                                        scalar1=1.0 / SCALE_LN, scalar2=None, op0=MUL).then_inc(s_f, 1)
                dve.wait_ge(s_f, 1)

                def rest(t, k, b):
                    dve.wait_ge(s_turn, t + 1)
                    dve.wait_ge(s_hi, t + 1)
                    nc.vector.scalar_tensor_tensor(out=hT[b][:, D:2 * D], in0=ps_t[b][:, :], scalar=SCALE_LN,
                                                   in1=hT[b][:, 0:D], op0=MUL, op1=SUB).then_inc(s_lo, 1)
                    wait_count(dve, s_hw, t - 1)
                    nc.vector.tensor_copy(dcol[b][:, :], dis[:, bass.ds(t, 1)]).then_inc(s_dcol, 1)
                    dve.wait_ge(s_dcol, t + 1)
                    dve.wait_ge(s_mm, t + 1)
                    wait_count(dve, hw_out[b], 16 * k)
                    nc.vector.tensor_scalar(out=hw[b][:, :], in0=ps_h[b][:, 0:HID], scalar1=f[:, 0:1],
                                            scalar2=dcol[b][:, 0:1], op0=MUL, op1=MUL).then_inc(s_hw, 1)

                def body(t, k, b):
                    dve.wait_ge(x_in[b], 16 * (k + 1))
                    norm.on_vector(dve, slot(t), t, b)
                    if started(2, t):
                        rest(*ago(2, t, k, b))
                each_tile(dve, NT, body)
                for tile in last(NT, 2):
                    rest(*tile)

            @block.gpsimd
            def _(pool):
                each_tile(pool, NT, lambda t, k, b: norm.on_pool(pool, t, b, [(s_h, t - 1)]))

            @block.scalar
            def _(act):
                def hi(t, k, b):
                    act.wait_ge(s_turn, t + 1)
                    wait_count(act, s_mm, t - 1)
                    nc.scalar.activation(hT[b][:, 0:D], ps_t[b][:, :], ACT.Copy, scale=SCALE_LN).then_inc(s_hi, 1)

                def body(t, k, b):
                    if started(1, t):
                        hi(*ago(1, t, k, b))
                    act.wait_ge(norm.s_ready, t + 1)
                    wait_count(act, s_turn, t - 1)
                    nc.scalar.activation(h[b][:, :], slot(t), ACT.Relu, scale=norm.rstd[b][:, 0:1],
                                         bias=norm.shift[b][:, 0:1]).then_inc(s_h, 1)
                each_tile(act, NT, body)
                for tile in last(NT, 1):
                    hi(*tile)

            @block.tensor
            def _(pe):
                pe.wait_ge(s_w, 16)

                def mm(t, k, b):
                    pe.wait_ge(s_lo, t + 1)
                    wait_count(pe, s_hw, t - 1)
                    product(pe, ps_h[b][:, 0:HID], lambda c: hT[b][:, c * P:(c + 1) * P],
                            lambda c: hT[b][:, D + c * P:D + (c + 1) * P], w, HID).then_inc(s_mm, 1)

                def body(t, k, b):
                    pe.wait_ge(s_h, t + 1)
                    wait_count(pe, s_lo, t - 1)
                    transposes(pe, ps_t[b], h[b]).then_inc(s_turn, 1)
                    if started(1, t):
                        mm(*ago(1, t, k, b))
                each_tile(pe, NT, body)
                for tile in last(NT, 1):
                    mm(*tile)

    def edge_sums_gcn():
        with ExitStack() as ctx:
            m = [sb(ctx, f"q_m{b}", [P, HID]) for b in range(2)]
            sl = [sb(ctx, f"q_sel{b}", [P, 2 * P]) for b in range(2)]
            tot = [sb(ctx, f"q_tot{b}", [P, HID]) for b in range(2)]
            ps_c = ps(ctx, "q_ps_c")
            ps_s = [ps(ctx, f"q_ps_s{b}") for b in range(2)]
            s_carry, s_carried, s_sum, s_tot = sems("q", "carry carried sum tot")
            m_in, sel_in, t_out = pair("q", "min"), pair("q", "selin"), pair("q", "tout")
            block = ctx.enter_context(nc.Block())

            @block.sync
            def _(sp):
                for t in range(ET):
                    wait_count(sp, s_sum, t - 1)
                    sp.dma_start(sl[t % 2][:, :], sel_d[:, t * 2 * P:(t + 1) * 2 * P]).then_inc(sel_in[t % 2], 16)

            @block.gpsimd
            def _(pool):
                def scatter(t):
                    pool.wait_ge(s_tot, t + 1)
                    nc.gpsimd.indirect_dma_start(
                        gcn_d[:, :], bass.IndirectOffsetOnAxis(ap=put_i[:, t:t + 1], axis=0), tot[t % 2][:, :],
                        None, bounds_check=N - 1, oob_is_err=False).then_inc(t_out[t % 2], 16)

                for t in range(ET):
                    wait_count(pool, s_sum, t - 1)
                    nc.gpsimd.indirect_dma_start(
                        m[t % 2][:, :], None, hw_d[0:N, :],
                        bass.IndirectOffsetOnAxis(ap=src_i[:, t:t + 1], axis=0)).then_inc(m_in[t % 2], 16)
                    if t >= 1:
                        scatter(t - 1)
                scatter(ET - 1)
                for b in range(2):
                    pool.wait_ge(t_out[b], 16 * (ET // 2))

            @block.vector
            def _(dve):
                for t in range(ET):
                    b, k = t % 2, t // 2
                    if t:
                        dve.wait_ge(m_in[b], 16 * (k + 1))
                        dve.wait_ge(s_carry, t)
                        nc.vector.tensor_copy(m[b][0:1, :], ps_c[0:1, 0:HID]).then_inc(s_carried, 1)
                    dve.wait_ge(s_sum, t + 1)
                    wait_count(dve, t_out[b], 16 * k)
                    nc.vector.tensor_copy(tot[b][:, :], ps_s[b][:, 0:HID]).then_inc(s_tot, 1)

            @block.tensor
            def _(pe):
                for t in range(ET):
                    b, k = t % 2, t // 2
                    pe.wait_ge(sel_in[b], 16 * (k + 1))
                    pe.wait_ge(m_in[b], 16 * (k + 1))
                    wait_count(pe, s_carried, t)
                    nc.tensor.matmul(ps_c[0:1, 0:HID], sl[b][:, P - 1:P], m[b][:, :], start=True,
                                     stop=True).then_inc(s_carry, 1)
                    wait_count(pe, s_tot, t - 1)
                    nc.tensor.matmul(ps_s[b][:, 0:HID], sl[b][:, 0:P], m[b][:, :], start=True,
                                     stop=True).then_inc(s_sum, 1)

    def gcn_finish():
        with ExitStack() as ctx:
            w = sb(ctx, "r_w", [P, D])
            bias_c = sb(ctx, "r_bias_c", [P, HID])
            bias_l = sb(ctx, "r_bias_l", [P, D])
            hw = [sb(ctx, f"r_hw{b}", [P, HID]) for b in range(2)]
            gs = [sb(ctx, f"r_gs{b}", [P, HID]) for b in range(2)]
            cv = [sb(ctx, f"r_cv{b}", [P, HID]) for b in range(2)]
            cT = [sb(ctx, f"r_cT{b}", [P, HID]) for b in range(2)]
            x1 = [sb(ctx, f"r_x1{b}", [P, D]) for b in range(2)]
            xb = [sb(ctx, f"r_xb{b}", [P, D]) for b in range(2)]
            h = [sb(ctx, f"r_h{b}", [P, D]) for b in range(2)]
            dcol = [sb(ctx, f"r_dcol{b}", [P, 1]) for b in range(2)]
            ps_c = [ps(ctx, f"r_ps_c{b}") for b in range(2)]
            ps_x = [ps(ctx, f"r_ps_x{b}") for b in range(2)]
            ps_t = [ps(ctx, f"r_ps_t{b}") for b in range(2)]
            s_w, s_cv0, s_dcol, s_cv, s_ct, s_cT, s_mm, s_xb, s_x1, s_h, s_turn, s_hi, s_lo = sems(
                "r", "w cv0 dcol cv ct cT mm xb x1 h turn hi lo")
            g_in, x_out = pair("r", "gin"), pair("r", "xout")
            norm = Norm(ctx, "r_norm")
            block = ctx.enter_context(nc.Block())

            @block.sync
            def _(sp):
                sp.dma_start(w[:, :], Wlin[:, :]).then_inc(s_w, 16)
                sp.dma_start(bias_c[:, :], wide(bc)).then_inc(s_w, 16)
                sp.dma_start(bias_l[:, :], wide(blin)).then_inc(s_w, 16)

                def store(t, k, b):
                    sp.wait_ge(s_x1, t + 1)
                    sp.dma_start(rows(x1_d, t), x1[b][0:rows_of(t), :]).then_inc(x_out[b], 16)

                def body(t, k, b):
                    wait_count(sp, s_cv, t - 1)
                    r = rows_of(t)
                    sp.dma_start(hw[b][0:r, :], rows(hw_d, t)).then_inc(g_in[b], 16)
                    sp.dma_start(gs[b][0:r, :], rows(gcn_d, t)).then_inc(g_in[b], 16)
                    if started(1, t):
                        store(*ago(1, t, k, b))
                each_tile(sp, NT, body)
                for tile in last(NT, 1):
                    store(*tile)
                sp.wait_ge(x_out[0], 16 * ((NT + 1) // 2))
                sp.wait_ge(x_out[1], 16 * (NT // 2))

            @block.gpsimd
            def _(pool):
                pool.wait_ge(s_w, 48)

                def body(t, k, b):
                    wait_count(pool, s_x1, t - 1)
                    nc.gpsimd.tensor_tensor(out=xb[b][:, :], in0=slot(t), in1=bias_l[:, :], op=ADD)\
                        .then_inc(s_xb, 1)
                    if started(1, t):
                        u, _, ub = ago(1, t, k, b)
                        norm.on_pool(pool, u, ub, [(s_h, u - 1)])
                each_tile(pool, NT, body)
                for t, _, b in last(NT, 1):
                    norm.on_pool(pool, t, b, [(s_h, t - 1)])

            @block.vector
            def _(dve):
                dve.wait_ge(s_w, 48)

                def conv(t, k, b):
                    dve.wait_ge(g_in[b], 32 * (k + 1))
                    nc.vector.tensor_copy(dcol[b][:, :], dis[:, bass.ds(t, 1)]).then_inc(s_dcol, 1)
                    wait_count(dve, s_ct, t - 1)
                    nc.vector.tensor_tensor(out=cv[b][:, :], in0=hw[b][:, :], in1=gs[b][:, :], op=ADD)\
                        .then_inc(s_cv0, 1)
                    dve.wait_ge(s_dcol, t + 1)
                    dve.wait_ge(s_cv0, t + 1)
                    nc.vector.scalar_tensor_tensor(out=cv[b][:, :], in0=cv[b][:, :], scalar=dcol[b][:, 0:1],
                                                   in1=bias_c[:, :], op0=MUL, op1=ADD).then_inc(s_cv, 1)

                def residual(t, k, b):
                    dve.wait_ge(s_mm, t + 1)
                    dve.wait_ge(s_xb, t + 1)
                    wait_count(dve, x_out[b], 16 * k)
                    wait_count(dve, s_h, t - 1)
                    nc.vector.tensor_tensor(out=x1[b][:, :], in0=ps_x[b][:, :], in1=xb[b][:, :], op=ADD)\
                        .then_inc(s_x1, 1)
                    dve.wait_ge(s_x1, t + 1)
                    norm.on_vector(dve, x1[b][:, :], t, b)

                def lo(t, k, b):
                    dve.wait_ge(s_hi, t + 1)
                    nc.vector.scalar_tensor_tensor(out=slot_lo(t), in0=ps_t[b][:, :], scalar=SCALE_LN,
                                                   in1=slot_hi(t), op0=MUL, op1=SUB).then_inc(s_lo, 1)

                def body(t, k, b):
                    conv(t, k, b)
                    if started(1, t):
                        residual(*ago(1, t, k, b))
                    if started(3, t):
                        lo(*ago(3, t, k, b))
                each_tile(dve, NT, body)
                residual(*last(NT, 1)[0])
                for tile in last(NT, 3):
                    lo(*tile)

            @block.scalar
            def _(act):
                def body(t, k, b):
                    act.wait_ge(s_ct, t + 1)
                    wait_count(act, s_mm, t - 1)
                    nc.scalar.activation(cT[b][:, :], ps_c[b][:, 0:HID], ACT.Copy).then_inc(s_cT, 1)
                    if started(3, t):
                        hi(*ago(3, t, k, b))
                    if started(2, t):
                        normed(*ago(2, t, k, b))

                def normed(t, k, b):
                    act.wait_ge(norm.s_ready, t + 1)
                    wait_count(act, s_turn, t - 1)
                    nc.scalar.activation(h[b][:, :], x1[b][:, :], ACT.Relu, scale=norm.rstd[b][:, 0:1],
                                         bias=norm.shift[b][:, 0:1]).then_inc(s_h, 1)

                def hi(t, k, b):
                    act.wait_ge(s_turn, t + 1)
                    act.wait_ge(s_x1, t + 1)
                    nc.scalar.activation(slot_hi(t), ps_t[b][:, :], ACT.Copy, scale=SCALE_LN).then_inc(s_hi, 1)
                each_tile(act, NT, body)
                hi(*last(NT, 3)[0])
                normed(*last(NT, 2)[0])
                hi(*last(NT, 2)[0])
                normed(*last(NT, 1)[0])
                hi(*last(NT, 1)[0])

            @block.tensor
            def _(pe):
                pe.wait_ge(s_w, 48)

                def linear(t, k, b):
                    pe.wait_ge(s_cT, t + 1)
                    wait_count(pe, s_x1, t - 1)
                    nc.tensor.matmul(ps_x[b][:, :], cT[b][:, :], w[:, :], start=True, stop=True).then_inc(s_mm, 1)

                def turn(t, k, b):
                    pe.wait_ge(s_h, t + 1)
                    wait_count(pe, s_lo, t - 1)
                    transposes(pe, ps_t[b], h[b]).then_inc(s_turn, 1)

                def body(t, k, b):
                    pe.wait_ge(s_cv, t + 1)
                    wait_count(pe, s_cT, t - 1)
                    nc.tensor.transpose(ps_c[b][:, 0:P], cv[b][:, :], ident[:, :]).then_inc(s_ct, 1)
                    if started(3, t):
                        turn(*ago(3, t, k, b))
                    linear(t, k, b)
                each_tile(pe, NT, body)
                for tile in last(NT, 3):
                    turn(*tile)

    def edge_products(phase, source, gather, normed, mean, scale, unit, weight=None):
        with ExitStack() as ctx:
            if unit:
                w = sb(ctx, f"{phase}_w", [P, 2 * cols[unit]], F16)
            else:
                w = sb(ctx, f"{phase}_w", [P, C * D])
            m = [sb(ctx, f"{phase}_m{b}", [P, D]) for b in range(2)]
            sl = [sb(ctx, f"{phase}_sel{b}", [P, 2 * P]) for b in range(2)]
            aT = [sb(ctx, f"{phase}_aT{b}", [P, D]) for b in range(2)]
            tot = [sb(ctx, f"{phase}_tot{b}", [P, D]) for b in range(2)]
            f = sb(ctx, f"{phase}_f", [P, 1])
            ps_c = ps(ctx, f"{phase}_ps_c")
            ps_a = [ps(ctx, f"{phase}_ps_a{b}") for b in range(2)]
            ps_g = [ps(ctx, f"{phase}_ps_g{b}") for b in range(2)]
            s_w, s_f, s_row, s_carry, s_carried, s_sum, s_hi, s_lo, s_mm, s_tot = sems(
                phase, "w f row carry carried sum hi lo mm tot")
            m_in, sel_in, t_out = pair(phase, "min"), pair(phase, "selin"), pair(phase, "tout")
            norm = Norm(ctx, f"{phase}_norm") if normed else None
            aT16 = [a[:, :].bitcast(F16) for a in aT]
            block = ctx.enter_context(nc.Block())

            @block.sync
            def _(sp):
                if unit:
                    sp.dma_start(w[:, :], split_d[unit][:, :]).then_inc(s_w, 16)
                else:
                    sp.dma_start(w[:, :].rearrange("p (c n) -> p c n", c=C),
                                 weight.rearrange("(c p) n -> p c n", p=P)).then_inc(s_w, 16)

                def body(t, k, b):
                    wait_count(sp, s_sum, t - 1)
                    sp.dma_start(sl[b][:, :], sel_d[:, bass.ds(t * 2 * P, 2 * P)]).then_inc(sel_in[b], 16)
                    if not gather:
                        sp.dma_start(m[b][:, :], source[bass.ds(t * P, P), :]).then_inc(m_in[b], 16)
                each_tile(sp, ET, body)

            @block.gpsimd
            def _(pool):
                def scatter(t, k, b):
                    pool.wait_ge(s_tot, t + 1)
                    nc.gpsimd.indirect_dma_start(
                        agg_d[:, :], bass.IndirectOffsetOnAxis(ap=put_i[:, t:t + 1], axis=0), tot[b][:, :],
                        None, bounds_check=N - 1, oob_is_err=False).then_inc(t_out[b], 16)

                for t in range(ET):
                    b, k = t % 2, t // 2
                    if gather:
                        wait_count(pool, s_sum, t - 1)
                        nc.gpsimd.indirect_dma_start(
                            m[b][:, :], None, source[0:N, :],
                            bass.IndirectOffsetOnAxis(ap=src_i[:, t:t + 1], axis=0)).then_inc(m_in[b], 16)
                    if normed and t >= 1:
                        norm.on_pool(pool, t - 1, 1 - b, [(s_row, t - 2)])
                    if t >= 3:
                        scatter(*ago(3, t, k, b))
                if normed:
                    norm.on_pool(pool, ET - 1, (ET - 1) % 2, [(s_row, ET - 2)])
                for tile in last(ET, 3):
                    scatter(*tile)
                for b in range(2):
                    pool.wait_ge(t_out[b], 16 * (ET // 2))

            @block.vector
            def _(dve):
                if unit:
                    nc.vector.tensor_scalar(out=f[:, :], in0=down[:, unit_no[unit]:unit_no[unit] + 1],
                                            scalar1=1.0 / scale, scalar2=None, op0=MUL).then_inc(s_f, 1)
                else:
                    nc.vector.memset(f[:, :], 1.0).then_inc(s_f, 1)
                dve.wait_ge(s_f, 1)

                def carry(t, k, b):
                    if normed:
                        dve.wait_ge(s_row, t + 1)
                    else:
                        dve.wait_ge(m_in[b], 16 * (k + 1))
                    dve.wait_ge(s_carry, t)
                    nc.vector.tensor_copy(m[b][0:1, :], ps_c[0:1, :]).then_inc(s_carried, 1)

                def lo(t, k, b):
                    dve.wait_ge(s_hi, t + 1)
                    nc.vector.scalar_tensor_tensor(out=aT16[b][:, D:2 * D], in0=ps_a[b][:, :], scalar=scale,
                                                   in1=aT16[b][:, 0:D], op0=MUL, op1=SUB).then_inc(s_lo, 1)

                def totals(t, k, b):
                    dve.wait_ge(s_mm, t + 1)
                    wait_count(dve, t_out[b], 16 * k)
                    nc.vector.tensor_scalar(out=tot[b][:, :], in0=ps_g[b][:, :], scalar1=f[:, 0:1],
                                            scalar2=None, op0=MUL).then_inc(s_tot, 1)

                def rest(t, k, b):
                    if started(1, t):
                        carry(t, k, b)
                    if unit:
                        lo(t, k, b)

                def body(t, k, b):
                    if normed:
                        dve.wait_ge(m_in[b], 16 * (k + 1))
                        norm.on_vector(dve, m[b][:, :], t, b)
                    if started(1, t):
                        rest(*ago(1, t, k, b))
                    if started(2, t):
                        totals(*ago(2, t, k, b))
                each_tile(dve, ET, body)
                rest(*last(ET, 1)[0])
                for tile in last(ET, 2):
                    totals(*tile)

            @block.scalar
            def _(act):
                def hi(t, k, b):
                    act.wait_ge(s_sum, t + 1)
                    wait_count(act, s_mm, t - 1)
                    if unit:
                        nc.scalar.activation(aT16[b][:, 0:D], ps_a[b][:, :], ACT.Copy, scale=scale).then_inc(s_hi, 1)
                    else:
                        nc.scalar.activation(aT[b][:, :], ps_a[b][:, :], ACT.Copy).then_inc(s_hi, 1)

                def body(t, k, b):
                    if normed:
                        act.wait_ge(norm.s_ready, t + 1)
                        nc.scalar.activation(m[b][:, :], m[b][:, :], ACT.Relu, scale=norm.rstd[b][:, 0:1],
                                             bias=norm.shift[b][:, 0:1]).then_inc(s_row, 1)
                    if started(1, t):
                        hi(*ago(1, t, k, b))
                each_tile(act, ET, body)
                hi(*last(ET, 1)[0])

            @block.tensor
            def _(pe):
                pe.wait_ge(s_w, 16)

                def sums(t, k, b):
                    pe.wait_ge(sel_in[b], 16 * (k + 1))
                    if normed:
                        pe.wait_ge(s_row, t + 1)
                    else:
                        pe.wait_ge(m_in[b], 16 * (k + 1))
                    wait_count(pe, s_carried, t)
                    nc.tensor.matmul(ps_c[0:1, :], sl[b][:, P - 1:P], m[b][:, :], start=True,
                                     stop=True).then_inc(s_carry, 1)
                    wait_count(pe, s_lo if unit else s_hi, t - 1)
                    half = P if mean else 0
                    for c in range(C):
                        ins = nc.tensor.matmul(ps_a[b][:, c * P:(c + 1) * P], m[b][:, c * P:(c + 1) * P],
                                               sl[b][:, half:half + P], start=True, stop=True)
                    ins.then_inc(s_sum, 1)

                def mm(t, k, b):
                    pe.wait_ge(s_lo if unit else s_hi, t + 1)
                    wait_count(pe, s_tot, t - 1)
                    if unit:
                        product(pe, ps_g[b][:, :], lambda c: aT16[b][:, c * P:(c + 1) * P],
                                lambda c: aT16[b][:, D + c * P:D + (c + 1) * P], w, D).then_inc(s_mm, 1)
                    else:
                        for c in range(C):
                            ins = nc.tensor.matmul(ps_g[b][:, :], aT[b][:, c * P:(c + 1) * P],
                                                   w[:, c * D:(c + 1) * D], start=c == 0, stop=c == C - 1)
                        ins.then_inc(s_mm, 1)

                def body(t, k, b):
                    sums(t, k, b)
                    if started(1, t):
                        mm(*ago(1, t, k, b))
                each_tile(pe, ET, body)
                mm(*last(ET, 1)[0])

    def sage_layer(l):
        final = l == 2
        phase = f"s{l}"
        scale_in = SCALE_LN if l == 0 else SCALE_UNIT
        scale_out = SCALE_LN if final else SCALE_UNIT
        unit = f"self{l}"
        with ExitStack() as ctx:
            w = sb(ctx, f"{phase}_w", [P, 2 * cols[unit]], F16)
            bias = sb(ctx, f"{phase}_bias", [P, D])
            g = [sb(ctx, f"{phase}_g{b}", [P, D]) for b in range(4)]
            junk = sb(ctx, f"{phase}_junk", [P, D])
            h = [sb(ctx, f"{phase}_h{b}", [P, D]) for b in range(4)]
            en = [sb(ctx, f"{phase}_en{b}", [P, 1]) for b in range(2)]
            em = [sb(ctx, f"{phase}_em{b}", [P, 1]) for b in range(2)]
            rn = [sb(ctx, f"{phase}_rn{b}", [P, 1]) for b in range(2)]
            f = sb(ctx, f"{phase}_f", [P, 1])
            if final:
                x1 = [sb(ctx, f"{phase}_x1{b}", [P, D]) for b in range(4)]
                h3 = [sb(ctx, f"{phase}_h3{b}", [P, D]) for b in range(2)]
            ps_z = [ps(ctx, f"{phase}_ps_z{b}") for b in range(4)]
            ps_t = [ps(ctx, f"{phase}_ps_t{b}") for b in range(2)]
            s_w, s_f, s_mm, s_bias, s_r, s_en, s_em, s_rn, s_h, s_turn, s_hi, s_lo, s_x2, s_h3 = sems(
                phase, "w f mm bias r en em rn h turn hi lo x2 h3")
            g_in, h_out = pair(phase, "gin", 4), pair(phase, "hout", 4)
            x_in = pair(phase, "xin", 4) if final else None
            norm = Norm(ctx, f"{phase}_norm") if final else None
            turned, nturned = (h3, 2) if final else (h, 4)
            s_turned = s_h3 if final else s_h
            block = ctx.enter_context(nc.Block())

            @block.sync
            def _(sp):
                sp.dma_start(w[:, :], split_d[unit][:, :]).then_inc(s_w, 16)
                sp.dma_start(bias[:, :], wide(bsage[l])).then_inc(s_w, 16)

                def load(v):
                    b = v.buf(4)
                    wait_count(sp, s_h, v.t - 3)
                    sp.dma_start(g[b][0:rows_of(v.t), :], rows(agg_d, v.t)).then_inc(g_in[b], 16)

                def load_x(v):
                    b = v.buf(4)
                    stores, normed = 16 * v.uses(4), v.t - 3
                    wait_count(sp, h_out[b], stores)
                    wait_count(sp, s_h3, normed)
                    sp.dma_start(x1[b][0:rows_of(v.t), :], rows(x1_d, v.t)).then_inc(x_in[b], 16)

                def store(v):
                    b = v.buf(4)
                    if final:
                        sp.wait_ge(s_x2, v.t + 1)
                        sp.dma_start(rows(x2_d, v.t), x1[b][0:rows_of(v.t), :]).then_inc(h_out[b], 16)
                    else:
                        sp.wait_ge(s_h, v.t + 1)
                        sp.dma_start(rows(h_d, v.t), h[b][0:rows_of(v.t), :]).then_inc(h_out[b], 16)
                if final:
                    pipeline(sp, NT, (0, load), (4, store), (1, load_x))
                else:
                    pipeline(sp, NT, (0, load), (4, store))
                for b in range(4):
                    sp.wait_ge(h_out[b], 16 * ((NT + 3 - b) // 4))

            @block.gpsimd
            def _(pool):
                pool.wait_ge(s_w, 32)

                def add_bias(v):
                    b = v.buf(4)
                    pool.wait_ge(g_in[b], 16 * (v.uses(4) + 1))
                    nc.gpsimd.tensor_tensor(out=g[b][:, :], in0=g[b][:, :], in1=bias[:, :], op=ADD)\
                        .then_inc(s_bias, 1)

                def factor(v):
                    b = v.buf(2)
                    pool.wait_ge(s_em, v.t + 1)
                    wait_count(pool, s_h, v.t - 1)
                    nc.gpsimd.tensor_tensor(out=rn[b][:, :], in0=em[b][:, :], in1=minus_half[:, :],
                                            op=POW).then_inc(s_rn, 1)
                if final:
                    pipeline(pool, NT, (0, add_bias), (1, factor), (2, lambda v: norm.factors(pool, v, s_h3)))
                else:
                    pipeline(pool, NT, (0, add_bias), (1, factor))

            @block.vector
            def _(dve):
                nc.vector.tensor_scalar(out=f[:, :], in0=down[:, unit_no[unit]:unit_no[unit] + 1],
                                        scalar1=1.0 / scale_in, scalar2=None, op0=MUL).then_inc(s_f, 1)
                dve.wait_ge(s_f, 1)

                def z_sum(v):
                    b = v.buf(4)
                    dve.wait_ge(s_mm, v.t + 1)
                    dve.wait_ge(s_bias, v.t + 1)
                    nc.vector.scalar_tensor_tensor(out=g[b][:, :], in0=ps_z[b][:, :], scalar=f[:, 0:1],
                                                   in1=g[b][:, :], op0=MUL, op1=ADD).then_inc(s_r, 1)

                def length(v):
                    r, e = g[v.buf(4)], v.buf(2)
                    dve.wait_ge(s_r, v.t + 1)
                    wait_count(dve, s_em, v.t)
                    nc.vector.scalar_tensor_tensor(out=junk[:, :], in0=r[:, :], scalar=0.0, in1=r[:, :],
                                                   op0=MAX, op1=MUL, accum_out=en[e][:, 0:1]).then_inc(s_en, 1)

                def clamp(v):
                    e = v.buf(2)
                    dve.wait_ge(s_en, v.t + 1)
                    wait_count(dve, s_rn, v.t - 1)
                    nc.vector.tensor_scalar(out=em[e][:, :], in0=en[e][:, :], scalar1=NORM_EPS * NORM_EPS,
                                            scalar2=None, op0=MAX).then_inc(s_em, 1)

                def lo(v):
                    dve.wait_ge(s_hi, v.t + 1)
                    nc.vector.scalar_tensor_tensor(out=slot_lo(v.t), in0=ps_t[v.buf(2)][:, :], scalar=scale_out,
                                                   in1=slot_hi(v.t), op0=MUL, op1=SUB).then_inc(s_lo, 1)

                def residual(v):
                    b = v.buf(4)
                    dve.wait_ge(s_h, v.t + 1)
                    dve.wait_ge(x_in[b], 16 * (v.uses(4) + 1))
                    nc.vector.tensor_tensor(out=x1[b][:, :], in0=x1[b][:, :], in1=h[b][:, :], op=ADD)\
                        .then_inc(s_x2, 1)

                def stats(v):
                    dve.wait_ge(s_x2, v.t + 1)
                    norm.stats_of(dve, x1[v.buf(4)][:, :], v)
                if final:
                    pipeline(dve, NT, (0, z_sum), (2, residual), (0, length), (0, clamp), (2, stats), (5, lo))
                else:
                    pipeline(dve, NT, (0, z_sum), (0, length), (0, clamp), (3, lo))

            @block.scalar
            def _(act):
                def hi(v):
                    act.wait_ge(s_turn, v.t + 1)
                    nc.scalar.activation(slot_hi(v.t), ps_t[v.buf(2)][:, :], ACT.Copy,
                                         scale=scale_out).then_inc(s_hi, 1)

                def normed(v):
                    b = v.buf(2)
                    act.wait_ge(norm.s_ready, v.t + 1)
                    wait_count(act, s_turn, v.t - 1)
                    nc.scalar.activation(h3[b][:, :], x1[v.buf(4)][:, :], ACT.Relu, scale=norm.rstd[b][:, 0:1],
                                         bias=norm.shift[b][:, 0:1]).then_inc(s_h3, 1)

                def unit_rows(v):
                    b = v.buf(4)
                    act.wait_ge(s_rn, v.t + 1)
                    if final:
                        wait_count(act, s_x2, v.t - 3)
                    else:
                        wait_count(act, s_turn, v.t - 3)
                        wait_count(act, h_out[b], 16 * v.uses(4))
                    nc.scalar.activation(h[b][:, :], g[b][:, :], ACT.Relu,
                                         scale=rn[v.buf(2)][:, 0:1]).then_inc(s_h, 1)
                if final:
                    pipeline(act, NT, (5, hi), (3, normed), (1, unit_rows))
                else:
                    pipeline(act, NT, (3, hi), (1, unit_rows))

            @block.tensor
            def _(pe):
                pe.wait_ge(s_w, 32)

                def project(v):
                    wait_count(pe, s_r, v.t - 3)
                    product(pe, ps_z[v.buf(4)][:, :], lambda c: slots16[:, bass.ds(v.t * 2 * D + c * P, P)],
                            lambda c: slots16[:, bass.ds(v.t * 2 * D + D + c * P, P)], w, D).then_inc(s_mm, 1)

                def turn(v):
                    pe.wait_ge(s_turned, v.t + 1)
                    wait_count(pe, s_lo, v.t - 1)
                    transposes(pe, ps_t[v.buf(2)], turned[v.buf(nturned)]).then_inc(s_turn, 1)
                pipeline(pe, NT, (0, project), (4 if final else 2, turn))

    class Mish:

        def __init__(self, ctx, name):
            self.c = [sb(ctx, f"{name}_c{b}", [P, D]) for b in range(2)]
            self.e = sb(ctx, f"{name}_e", [P, D])
            self.s_c, self.s_e, self.s_w, self.s_l, self.s_q, self.s_rw, self.s_u = sems(
                name, "c e w l q rw u")

        def cap(self, dve, r, v, freed, count):
            wait_count(dve, freed, count)
            nc.vector.tensor_scalar(out=self.c[v.buf(2)][:, :], in0=r, scalar1=MISH_CAP, scalar2=None,
                                    op0=MIN).then_inc(self.s_c, 1)

        def exp(self, act, v):
            b = v.buf(2)
            act.wait_ge(self.s_c, v.t + 1)
            nc.scalar.activation(self.e[:, :], self.c[b][:, :], ACT.Exp).then_inc(self.s_e, 1)

        def poly(self, dve, v):
            b = v.buf(2)
            dve.wait_ge(self.s_e, v.t + 1)
            nc.vector.scalar_tensor_tensor(out=self.c[b][:, :], in0=self.e[:, :], scalar=2.0,
                                           in1=self.e[:, :], op0=ADD, op1=MUL).then_inc(self.s_w, 1)

        def inverse(self, act, v):
            b = v.buf(2)
            act.wait_ge(self.s_w, v.t + 1)
            nc.scalar.activation(self.e[:, :], self.c[b][:, :], ACT.Ln,
                                 bias=two_col[:, 0:1]).then_inc(self.s_l, 1)
            act.wait_ge(self.s_l, v.t + 1)
            nc.scalar.activation(self.e[:, :], self.e[:, :], ACT.Exp, scale=-1.0).then_inc(self.s_q, 1)

        def times(self, pool, r, v):
            b = v.buf(2)
            pool.wait_ge(self.s_w, v.t + 1)
            nc.gpsimd.tensor_tensor(out=r, in0=r, in1=self.c[b][:, :], op=MUL)\
                .then_inc(self.s_rw, 1)

        def result(self, dve, r, v):
            b = v.buf(2)
            dve.wait_ge(self.s_q, v.t + 1)
            dve.wait_ge(self.s_rw, v.t + 1)
            nc.vector.tensor_tensor(out=self.c[b][:, :], in0=r, in1=self.e[:, :],
                                    op=MUL).then_inc(self.s_u, 1)

    class OldMish:
        def __init__(self, ctx, name):
            self.c = sb(ctx, f"{name}_c", [P, D])
            self.e = sb(ctx, f"{name}_e", [P, D])
            self.w = sb(ctx, f"{name}_w", [P, D])
            self.q = self.e
            self.s_c, self.s_e, self.s_w, self.s_q, self.s_rq, self.s_rw, self.s_u = sems(
                name, "c e w q rq rw u")

        def on_vector(self, dve, r, out_ap, n):
            nc.vector.tensor_scalar(out=self.c[:, :], in0=r, scalar1=MISH_CAP, scalar2=None,
                                    op0=MIN).then_inc(self.s_c, 1)
            dve.wait_ge(self.s_e, n + 1)
            nc.vector.scalar_tensor_tensor(out=self.w[:, :], in0=self.e[:, :], scalar=2.0, in1=self.e[:, :],
                                           op0=ADD, op1=MUL).then_inc(self.s_w, 1)
            dve.wait_ge(self.s_w, n + 1)
            nc.vector.tensor_scalar(out=self.q[:, :], in0=self.w[:, :], scalar1=2.0, scalar2=None,
                                    op0=ADD).then_inc(self.s_q, 1)
            dve.wait_ge(self.s_q, n + 1)
            nc.vector.reciprocal(self.q[:, :], self.q[:, :]).then_inc(self.s_rq, 1)
            dve.wait_ge(self.s_rq, n + 1)
            dve.wait_ge(self.s_rw, n + 1)
            nc.vector.tensor_tensor(out=out_ap, in0=self.c[:, :], in1=self.q[:, :], op=MUL).then_inc(self.s_u, 1)

        def on_scalar(self, act, n):
            act.wait_ge(self.s_c, n + 1)
            nc.scalar.activation(self.e[:, :], self.c[:, :], ACT.Exp).then_inc(self.s_e, 1)

        def on_pool(self, pool, r, n):
            pool.wait_ge(self.s_w, n + 1)
            nc.gpsimd.tensor_tensor(out=self.c[:, :], in0=r, in1=self.w[:, :], op=MUL).then_inc(self.s_rw, 1)

    def edge_network():
        with ExitStack() as ctx:
            w1 = sb(ctx, "e_w1", [P, 2 * cols["edge"]], F16)
            w1c = sb(ctx, "e_w1c", [ED, D])
            w2 = sb(ctx, "e_w2", [P, C * D])
            bias1 = sb(ctx, "e_bias1", [P, D])
            bias2 = sb(ctx, "e_bias2", [P, D])
            m = [sb(ctx, f"e_m{s}", [P, D]) for s in range(2)]
            ea = sb(ctx, "e_ea", [P, ED])
            eaT = sb(ctx, "e_eaT", [ED, P])
            hT = [sb(ctx, f"e_hT{s}", [P, 2 * D], F16) for s in range(2)]
            r = sb(ctx, "e_r", [P, D])
            mT = hT[0][:, :].bitcast(F32)
            m1 = r
            f = sb(ctx, "e_f", [P, 1])
            ps_t = [ps(ctx, f"e_ps_t{s}") for s in range(2)]
            ps_e = ps(ctx, "e_ps_e")
            ps_1, ps_2, ps_m = ps(ctx, "e_ps_1"), ps(ctx, "e_ps_2"), ps(ctx, "e_ps_m")
            (s_w, s_f, s_wc, s_row, s_turn, s_hi, s_lo, s_et, s_eT, s_mm1, s_r, s_mt, s_mT, s_mm2,
             s_out, s_ea) = sems("e", "w f wc row turn hi lo et eT mm1 r mt mT mm2 out ea")
            m_in = pair("e", "min")
            norm = Norm(ctx, "e_norm")
            mish = OldMish(ctx, "e_mish")
            msg = mish.w
            u_edge = unit_no["edge"]
            block = ctx.enter_context(nc.Block())

            def first_no(t):
                return 0 if isinstance(t, int) and t == 0 else 2 * t - 1

            def next_of(t):
                return ET if isinstance(t, int) and t == ET - 1 else t + 2

            def second_no(t):
                return 2 * ET - 1 if isinstance(t, int) and t == ET - 1 else 2 * t + 2

            @block.sync
            def _(sp):
                sp.dma_start(w1[:, :], split_d["edge"][:, :]).then_inc(s_w, 16)
                sp.dma_start(w1c[:, :], W1[2 * D:2 * D + ED, :]).then_inc(s_w, 16)
                sp.dma_start(w2[:, :].rearrange("p (c n) -> p c n", c=C),
                             W2.rearrange("(c p) n -> p c n", p=P)).then_inc(s_w, 16)
                sp.dma_start(bias1[:, :], wide(b1)).then_inc(s_w, 16)
                sp.dma_start(bias2[:, :], wide(b2)).then_inc(s_w, 16)

                def body(t, k, b):
                    sp.wait_ge(mish.s_u, second_no(t) + 1)
                    sp.dma_start(msg_d[bass.ds(t * P, P), :], msg[:, :]).then_inc(s_out, 16)
                each_tile(sp, ET - 1, body)
                body(ET - 1, 0, 0)
                sp.wait_ge(s_out, 16 * ET)

            @block.gpsimd
            def _(pool):
                pool.wait_ge(s_w, 80)
                for t in range(ET):
                    for s, idx in enumerate((src_i, dst_i)):
                        wait_count(pool, s_turn, 2 * (t - 1) + s + 1)
                        nc.gpsimd.indirect_dma_start(
                            m[s][:, :], None, x2_d[0:N, :],
                            bass.IndirectOffsetOnAxis(ap=idx[:, t:t + 1], axis=0)).then_inc(m_in[s], 16)
                    wait_count(pool, s_et, t)
                    nc.gpsimd.indirect_dma_start(
                        ea[:, :], None, edge_attr[:, :],
                        bass.IndirectOffsetOnAxis(ap=edge_i[:, t:t + 1], axis=0)).then_inc(s_ea, 16)
                    for s in range(2):
                        v = 2 * t + s
                        norm.on_pool(pool, v, s, [(s_row, v - 1)])
                    mish.on_pool(pool, r[:, :], first_no(t))
                    if t >= 1:
                        mish.on_pool(pool, r[:, :], second_no(t - 1))
                mish.on_pool(pool, r[:, :], second_no(ET - 1))

            @block.vector
            def _(dve):
                dve.wait_ge(s_w, 80)
                nc.vector.tensor_scalar(out=f[:, :], in0=down[:, u_edge:u_edge + 1], scalar1=1.0 / SCALE_LN,
                                        scalar2=None, op0=MUL).then_inc(s_f, 1)
                nc.vector.tensor_scalar(out=w1c[:, :], in0=w1c[:, :], scalar1=up[0:ED, u_edge:u_edge + 1],
                                        scalar2=SCALE_LN, op0=MUL, op1=MUL).then_inc(s_wc, 1)
                dve.wait_ge(s_f, 1)

                def load_stage(t, k, b):
                    for s in range(2):
                        dve.wait_ge(m_in[s], 16 * (t + 1))
                        norm.on_vector(dve, m[s][:, :], 2 * t + s, s)

                def split(t, k, b):
                    dve.wait_ge(s_et, t + 1)
                    wait_count(dve, s_mm1, t)
                    nc.vector.tensor_copy(eaT[:, :], ps_e[0:ED, 0:P]).then_inc(s_eT, 1)
                    for s in range(2):
                        dve.wait_ge(s_hi, 2 * t + s + 1)
                        nc.vector.scalar_tensor_tensor(out=hT[s][:, D:2 * D], in0=ps_t[s][:, :],
                                                       scalar=SCALE_LN, in1=hT[s][:, 0:D], op0=MUL,
                                                       op1=SUB).then_inc(s_lo, 1)

                def first(t, k, b):
                    dve.wait_ge(s_mm1, t + 1)
                    if started(2, t):
                        dve.wait_ge(s_out, 16 * (t - 1))
                    nc.vector.scalar_tensor_tensor(out=r[:, :], in0=ps_1[:, :], scalar=f[:, 0:1],
                                                   in1=bias1[:, :], op0=MUL, op1=ADD).then_inc(s_r, 1)
                    dve.wait_ge(s_r, first_no(t) + 1)
                    mish.on_vector(dve, r[:, :], m1[:, :], first_no(t))

                def second(t, k, b):
                    dve.wait_ge(s_mm2, t + 1)
                    dve.wait_ge(s_mt, next_of(t))
                    nc.vector.tensor_tensor(out=r[:, :], in0=ps_2[:, :], in1=bias2[:, :], op=ADD).then_inc(s_r, 1)
                    dve.wait_ge(s_r, second_no(t) + 1)
                    mish.on_vector(dve, r[:, :], msg[:, :], second_no(t))

                def body(t, k, b):
                    load_stage(t, k, b)
                    split(t, k, b)
                    first(t, k, b)
                    if started(1, t):
                        second(*ago(1, t, k, b))
                each_tile(dve, ET, body)
                dve.wait_ge(s_out, 16 * (ET - 1))
                second(*last(ET, 1)[0])

            @block.scalar
            def _(act):
                def body(t, k, b):
                    for s in range(2):
                        act.wait_ge(norm.s_ready, 2 * t + s + 1)
                        nc.scalar.activation(m[s][:, :], m[s][:, :], ACT.Relu, scale=norm.rstd[s][:, 0:1],
                                             bias=norm.shift[s][:, 0:1]).then_inc(s_row, 1)
                    for s in range(2):
                        act.wait_ge(s_turn, 2 * t + s + 1)
                        wait_count(act, s_mm2, t)
                        nc.scalar.activation(hT[s][:, 0:D], ps_t[s][:, :], ACT.Copy, scale=SCALE_LN)\
                            .then_inc(s_hi, 1)
                    mish.on_scalar(act, first_no(t))
                    if started(1, t):
                        mish.on_scalar(act, second_no(ago(1, t, k, b)[0]))
                    act.wait_ge(s_mt, t + 1)
                    wait_count(act, s_mm2, t)
                    nc.scalar.activation(mT[:, :], ps_m[:, :], ACT.Copy).then_inc(s_mT, 1)
                each_tile(act, ET, body)
                mish.on_scalar(act, second_no(ET - 1))

            @block.tensor
            def _(pe):
                pe.wait_ge(s_w, 80)
                pe.wait_ge(s_wc, 1)

                def hidden(t, k, b):
                    pe.wait_ge(s_lo, 2 * t + 2)
                    pe.wait_ge(s_eT, t + 1)
                    wait_count(pe, s_r, first_no(t))
                    nc.tensor.matmul(ps_1[:, :], eaT[:, :], w1c[:, :], start=True, stop=False)
                    product(pe, ps_1[:, :], lambda c: hT[c // C][:, (c % C) * P:(c % C + 1) * P],
                            lambda c: hT[c // C][:, D + (c % C) * P:D + (c % C + 1) * P], w1, D,
                            nchunks=2 * C, first=False).then_inc(s_mm1, 1)

                def output(t, k, b):
                    pe.wait_ge(s_mT, t + 1)
                    if started(1, t):
                        pe.wait_ge(s_r, 2 * t + 1)
                    for c in range(C):
                        ins = nc.tensor.matmul(ps_2[:, :], mT[:, c * P:(c + 1) * P],
                                               w2[:, c * D:(c + 1) * D], start=c == 0, stop=c == C - 1)
                    ins.then_inc(s_mm2, 1)

                def body(t, k, b):
                    for s in range(2):
                        pe.wait_ge(s_row, 2 * t + s + 1)
                        wait_count(pe, s_lo, 2 * (t - 1) + s + 1)
                        transposes(pe, ps_t[s], m[s]).then_inc(s_turn, 1)
                    pe.wait_ge(s_ea, 16 * (t + 1))
                    wait_count(pe, s_eT, t)
                    nc.tensor.matmul(ps_e[0:ED, 0:P], ea[:, :], ident[:, :], start=True, stop=True)\
                        .then_inc(s_et, 1)
                    hidden(t, k, b)
                    pe.wait_ge(mish.s_u, first_no(t) + 1)
                    wait_count(pe, s_mT, t)
                    transposes(pe, ps_m, m1).then_inc(s_mt, 1)
                    output(t, k, b)
                each_tile(pe, ET, body)

    def node_update():
        with ExitStack() as ctx:
            w3 = sb(ctx, "u_w3", [P, 2 * cols["update"]], F16)
            w4 = sb(ctx, "u_w4", [P, C * D])
            bias3, gam, bet = (sb(ctx, f"u_{n}", [P, D]) for n in ("bias3", "gam", "bet"))
            b4_rows = sb(ctx, "u_b4_rows", [3, D], BF16)
            ones3 = sb(ctx, "u_ones3", [3, P], BF16)
            g = [sb(ctx, f"u_g{b}", [P, D]) for b in range(2)]
            x2 = [sb(ctx, f"u_x2{b}", [P, D]) for b in range(4)]
            uT, yn, h4 = (sb(ctx, f"u_{n}", [P, D]) for n in ("uT", "yn", "h4"))
            b4_row = x2[0][0:1, :]
            b4_part = [x2[m + 1][0:1, 0:D // 2].bitcast(BF16) for m in range(3)]
            f = sb(ctx, "u_f", [P, 1])
            ps_z = [ps(ctx, f"u_ps_z{b}") for b in range(2)]
            ps_u = ps(ctx, "u_ps_u")
            ps_o = [ps(ctx, f"u_ps_o{b}") for b in range(2)]
            ps_t = [ps(ctx, f"u_ps_t{b}") for b in range(2)]
            (s_w, s_f, s_b4, s_ones, s_mm, s_bias, s_r, s_ut, s_uT, s_mm4, s_yn, s_xb, s_yg, s_x3,
             s_h4, s_turn, s_hi, s_lo) = sems(
                "u", "w f b4 ones mm bias r ut uT mm4 yn xb yg x3 h4 turn hi lo")
            g_in, x_in, x_out = pair("u", "gin"), pair("u", "xin", 4), pair("u", "xout", 4)
            normy, norm3 = Norm(ctx, "u_ny"), Norm(ctx, "u_n3")
            mish = Mish(ctx, "u_mish")
            u_no = unit_no["update"]
            block = ctx.enter_context(nc.Block())

            @block.sync
            def _(sp):
                sp.dma_start(b4_row, b4.rearrange("(o d) -> o d", o=1)).then_inc(s_b4, 16)
                sp.dma_start(w3[:, :], split_d["update"][:, :]).then_inc(s_w, 16)
                sp.dma_start(w4[:, :].rearrange("p (c n) -> p c n", c=C),
                             W4.rearrange("(c p) n -> p c n", p=P)).then_inc(s_w, 16)
                for tile, vec in ((bias3, b3), (gam, gamma2), (bet, beta2)):
                    sp.dma_start(tile[:, :], wide(vec)).then_inc(s_w, 16)
                sp.wait_ge(s_f, 6)
                for m in range(3):
                    sp.dma_start(b4_rows[m:m + 1, :], b4_part[m]).then_inc(s_w, 16)

                def load(v):
                    b = v.buf(2)
                    wait_count(sp, mish.s_u, v.t - 1)
                    sp.dma_start(g[b][0:rows_of(v.t), :], rows(agg_d, v.t)).then_inc(g_in[b], 16)

                def load_x(v):
                    b = v.buf(4)
                    wait_count(sp, x_out[b], 16 * v.uses(4))
                    sp.dma_start(x2[b][0:rows_of(v.t), :], rows(x2_d, v.t)).then_inc(x_in[b], 16)

                sp.wait_ge(s_w, 128)
                pipeline(sp, NT, (0, load), (1, load_x))

            @block.gpsimd
            def _(pool):
                nc.gpsimd.memset(ones3[:, :], 1.0).then_inc(s_ones, 1)
                pool.wait_ge(s_w, 128)

                def add_bias(v):
                    b = v.buf(2)
                    pool.wait_ge(g_in[b], 16 * (v.uses(2) + 1))
                    nc.gpsimd.tensor_tensor(out=g[b][:, :], in0=g[b][:, :], in1=bias3[:, :], op=ADD)\
                        .then_inc(s_bias, 1)

                def add_beta(v):
                    b = v.buf(4)
                    pool.wait_ge(x_in[b], 16 * (v.uses(4) + 1))
                    nc.gpsimd.tensor_tensor(out=x2[b][:, :], in0=x2[b][:, :], in1=bet[:, :], op=ADD)\
                        .then_inc(s_xb, 1)

                def times_gamma(v):
                    pool.wait_ge(s_yn, v.t + 1)
                    nc.gpsimd.tensor_tensor(out=yn[:, :], in0=yn[:, :], in1=gam[:, :], op=MUL)\
                        .then_inc(s_yg, 1)
                pipeline(pool, NT, (0, add_bias), (3, lambda v: normy.factors(pool, v, s_yn)),
                         (4, lambda v: norm3.factors(pool, v, s_h4)), (3, add_beta), (3, times_gamma),
                         (0, lambda v: mish.times(pool, g[v.buf(2)][:, :], v)))

            @block.vector
            def _(dve):
                nc.vector.tensor_scalar(out=f[:, :], in0=down[:, u_no:u_no + 1], scalar1=1.0 / SCALE_LN,
                                        scalar2=None, op0=MUL).then_inc(s_f, 1)
                dve.wait_ge(s_b4, 16)
                for m in range(3):
                    if m:
                        nc.vector.tensor_tensor(out=b4_row, in0=b4_row, in1=b4_part[m - 1], op=SUB).then_inc(s_f, 1)
                        dve.wait_ge(s_f, 2 * m + 1)
                    nc.vector.tensor_copy(b4_part[m], b4_row).then_inc(s_f, 1)
                    dve.wait_ge(s_f, 2 * m + 2)

                def z_sum(v):
                    b = v.buf(2)
                    dve.wait_ge(s_mm, v.t + 1)
                    dve.wait_ge(s_bias, v.t + 1)
                    nc.vector.scalar_tensor_tensor(out=g[b][:, :], in0=ps_z[b][:, :], scalar=f[:, 0:1],
                                                   in1=g[b][:, :], op0=MUL, op1=ADD).then_inc(s_r, 1)

                def cap(v):
                    dve.wait_ge(s_r, v.t + 1)
                    mish.cap(dve, g[v.buf(2)][:, :], v, s_ut, v.t - 1)

                def y_stats(v):
                    dve.wait_ge(s_mm4, v.t + 1)
                    normy.stats_of(dve, ps_o[v.buf(2)][:, :], v)

                def residual(v):
                    b = v.buf(4)
                    dve.wait_ge(s_yg, v.t + 1)
                    dve.wait_ge(s_xb, v.t + 1)
                    nc.vector.tensor_tensor(out=x2[b][:, :], in0=x2[b][:, :], in1=yn[:, :], op=ADD)\
                        .then_inc(s_x3, 1)

                def x3_stats(v):
                    dve.wait_ge(s_x3, v.t + 1)
                    norm3.stats_of(dve, x2[v.buf(4)][:, :], v)

                def lo(v):
                    dve.wait_ge(s_hi, v.t + 1)
                    nc.vector.scalar_tensor_tensor(out=slot_lo(v.t), in0=ps_t[v.buf(2)][:, :], scalar=SCALE_LN,
                                                   in1=slot_hi(v.t), op0=MUL, op1=SUB).then_inc(s_lo, 1)
                pipeline(dve, NT, (0, z_sum), (0, cap), (5, lo), (0, lambda v: mish.poly(dve, v)), (2, y_stats),
                         (3, residual), (0, lambda v: mish.result(dve, g[v.buf(2)][:, :], v)),
                         (3, x3_stats))

            @block.scalar
            def _(act):
                def u_parts(v):
                    act.wait_ge(s_ut, v.t + 1)
                    wait_count(act, s_mm4, v.t)
                    nc.scalar.activation(uT[:, :], ps_u[:, :], ACT.Copy).then_inc(s_uT, 1)

                def y_normed(v):
                    b = v.buf(2)
                    act.wait_ge(normy.s_ready, v.t + 1)
                    wait_count(act, s_x3, v.t)
                    nc.scalar.activation(yn[:, :], ps_o[b][:, :], ACT.Identity, scale=normy.rstd[b][:, 0:1],
                                         bias=normy.shift[b][:, 0:1]).then_inc(s_yn, 1)

                def next_rows(v):
                    b = v.buf(2)
                    act.wait_ge(norm3.s_ready, v.t + 1)
                    wait_count(act, s_turn, v.t)
                    nc.scalar.activation(h4[:, :], x2[v.buf(4)][:, :], ACT.Relu,
                                         scale=norm3.rstd[b][:, 0:1],
                                         bias=norm3.shift[b][:, 0:1]).then_inc(s_h4, 1)

                def hi(v):
                    act.wait_ge(s_turn, v.t + 1)
                    nc.scalar.activation(slot_hi(v.t), ps_t[v.buf(2)][:, :], ACT.Copy,
                                         scale=SCALE_LN).then_inc(s_hi, 1)

                def store(v):
                    b = v.buf(4)
                    act.wait_ge(s_h4, v.t + 1)
                    act.dma_start(rows(x3_d, v.t), x2[b][0:rows_of(v.t), :]).then_inc(x_out[b], 16)
                pipeline(act, NT, (5, store), (5, hi), (3, y_normed), (0, lambda v: mish.exp(act, v)), (4, next_rows),
                         (0, lambda v: mish.inverse(act, v)), (1, u_parts))
                for b in range(4):
                    act.wait_ge(x_out[b], 16 * ((NT + 3 - b) // 4))

            @block.tensor
            def _(pe):
                pe.wait_ge(s_ones, 1)
                pe.wait_ge(s_w, 128)

                def update(v):
                    wait_count(pe, s_r, v.t - 1)
                    product(pe, ps_z[v.buf(2)][:, :], lambda c: slots16[:, bass.ds(v.t * 2 * D + c * P, P)],
                            lambda c: slots16[:, bass.ds(v.t * 2 * D + D + c * P, P)], w3, D).then_inc(s_mm, 1)

                def turn_u(v):
                    pe.wait_ge(mish.s_u, v.t + 1)
                    wait_count(pe, s_uT, v.t)
                    transposes(pe, ps_u, mish.c[v.buf(2)]).then_inc(s_ut, 1)

                def second(v):
                    b = v.buf(2)
                    wait_count(pe, s_yn, v.t - 1)
                    nc.tensor.matmul(ps_o[b][:, :], ones3[:, :], b4_rows[:, :], start=True, stop=False)
                    for part in range(2):
                        for c in range(C):
                            nc.tensor.matmul(ps_o[b][:, c * P:(c + 1) * P],
                                             slots16[:, bass.ds(v.t * 2 * D + part * D + c * P, P)],
                                             unscale[:, :], start=False, stop=False)
                    pe.wait_ge(s_uT, v.t + 1)
                    for c in range(C):
                        ins = nc.tensor.matmul(ps_o[b][:, :], uT[:, c * P:(c + 1) * P],
                                               w4[:, c * D:(c + 1) * D], start=False, stop=c == C - 1)
                    ins.then_inc(s_mm4, 1)

                def turn(v):
                    pe.wait_ge(s_h4, v.t + 1)
                    wait_count(pe, s_lo, v.t - 1)
                    transposes(pe, ps_t[v.buf(2)], h4).then_inc(s_turn, 1)
                pipeline(pe, NT, (0, update), (2, second), (1, turn_u), (4, turn))

    def batch_rows(pilot, shiftb, sum1, sum2):
        phase = "zp" if pilot else "z"
        with ExitStack() as ctx:
            w = sb(ctx, f"{phase}_w", [P, 2 * cols["root"]], F16)
            g = [sb(ctx, f"{phase}_g{b}", [P, D]) for b in range(2)]
            sq = [sb(ctx, f"{phase}_sq{b}", [P, D]) for b in range(2)]
            ones = sb(ctx, f"{phase}_ones", [P, P])
            f = sb(ctx, f"{phase}_f", [P, 1])
            ps_z = [ps(ctx, f"{phase}_ps_z{b}") for b in range(2)]
            ps_m = ps(ctx, f"{phase}_ps_m")
            s_w, s_f, s_mm, s_bias, s_z, s_sq, s_s1, s_s2, s_mean = sems(
                phase, "w f mm bias z sq s1 s2 mean")
            g_in = pair(phase, "gin")
            nt = 1 if pilot else NT
            u_no = unit_no["root"]
            zrow = (lambda t: sq[0][:, :]) if pilot else slot
            block = ctx.enter_context(nc.Block())

            @block.sync
            def _(sp):
                sp.dma_start(w[:, :], split_d["root"][:, :]).then_inc(s_w, 16)
                if pilot:
                    sp.dma_start(shiftb[:, :], wide(bl)).then_inc(s_w, 16)
                    sp.dma_start(g[0][:, :], rows(agg_d, 0)).then_inc(g_in[0], 16)
                    return

                def body(t, k, b):
                    wait_count(sp, s_z, t - 1)
                    sp.dma_start(g[b][0:rows_of(t), :], rows(agg_d, t)).then_inc(g_in[b], 16)
                each_tile(sp, NT, body)

            @block.gpsimd
            def _(pool):
                if pilot:
                    nc.gpsimd.memset(ones[:, :], 1.0 / P).then_inc(s_mean, 1)
                    pool.wait_ge(s_w, 32)
                    pool.wait_ge(g_in[0], 16)
                    nc.gpsimd.tensor_tensor(out=g[0][:, :], in0=g[0][:, :], in1=shiftb[:, :], op=ADD)\
                        .then_inc(s_bias, 1)
                    return

                def body(t, k, b):
                    pool.wait_ge(g_in[b], 16 * (k + 1))
                    nc.gpsimd.tensor_tensor(out=g[b][:, :], in0=g[b][:, :], in1=shiftb[:, :], op=ADD)\
                        .then_inc(s_bias, 1)
                each_tile(pool, NT, body)

            @block.vector
            def _(dve):
                nc.vector.tensor_scalar(out=f[:, :], in0=down[:, u_no:u_no + 1], scalar1=1.0 / SCALE_LN,
                                        scalar2=None, op0=MUL).then_inc(s_f, 1)
                dve.wait_ge(s_f, 1)

                def z_of(t, k, b):
                    dve.wait_ge(s_mm, t + 1)
                    dve.wait_ge(s_bias, t + 1)
                    nc.vector.scalar_tensor_tensor(out=zrow(t), in0=ps_z[b][:, :], scalar=f[:, 0:1],
                                                   in1=g[b][:, :], op0=MUL, op1=ADD).then_inc(s_z, 1)
                if pilot:
                    z_of(0, 0, 0)
                    dve.wait_ge(s_mean, 2)
                    nc.vector.tensor_tensor(out=shiftb[:, :], in0=shiftb[:, :], in1=ps_m[:, :], op=SUB)\
                        .then_inc(s_s1, 1)
                    dve.wait_ge(s_s1, 1)
                    return
                nc.vector.memset(sum1[:, :], 0.0)
                nc.vector.memset(sum2[:, :], 0.0).then_inc(s_f, 1)
                dve.wait_ge(s_f, 2)

                def squares(t, k, b):
                    n = rows_of(t)
                    dve.wait_ge(s_sq, t + 1)
                    wait_count(dve, s_s2, t)
                    nc.vector.tensor_tensor(out=sum2[0:n, :], in0=sum2[0:n, :], in1=sq[b][0:n, :], op=ADD)\
                        .then_inc(s_s2, 1)

                def body(t, k, b):
                    n = rows_of(t)
                    z_of(t, k, b)
                    if started(1, t):
                        squares(*ago(1, t, k, b))
                    dve.wait_ge(s_z, t + 1)
                    wait_count(dve, s_s1, t)
                    nc.vector.tensor_tensor(out=sum1[0:n, :], in0=sum1[0:n, :], in1=slot(t)[0:n, :], op=ADD)\
                        .then_inc(s_s1, 1)
                each_tile(dve, NT, body)
                squares(*last(NT, 1)[0])

            @block.scalar
            def _(act):
                if pilot:
                    return

                def body(t, k, b):
                    act.wait_ge(s_z, t + 1)
                    wait_count(act, s_s2, t - 1)
                    nc.scalar.activation(sq[b][:, :], slot(t), ACT.Square).then_inc(s_sq, 1)
                each_tile(act, NT, body)

            @block.tensor
            def _(pe):
                pe.wait_ge(s_w, 32 if pilot else 16)

                def body(t, k, b):
                    wait_count(pe, s_z, t - 1)
                    product(pe, ps_z[b][:, :], lambda c: slots16[:, bass.ds(t * 2 * D + c * P, P)],
                            lambda c: slots16[:, bass.ds(t * 2 * D + D + c * P, P)], w, D).then_inc(s_mm, 1)
                if pilot:
                    body(0, 0, 0)
                    pe.wait_ge(s_z, 1)
                    pe.wait_ge(s_mean, 1)
                    nc.tensor.matmul(ps_m[:, :], ones[:, :], sq[0][:, :], start=True, stop=True).then_inc(s_mean, 1)
                else:
                    each_tile(pe, NT, body)

    def finish(sum1, sum2):
        with ExitStack() as ctx:
            ones = sb(ctx, "f_ones", [P, P])
            gam, bet, mean, var, a_row, b_row, half = (
                sb(ctx, f"f_{n}", [P, D]) for n in ("gam", "bet", "mean", "var", "a", "b", "half"))
            x3 = [sb(ctx, f"f_x{b}", [P, D]) for b in range(4)]
            ps_1, ps_2 = ps(ctx, "f_ps_1"), ps(ctx, "f_ps_2")
            s_w, s_mm, s_v, s_p, s_coef, s_za, s_zb, s_o, s_mem = sems("f", "w mm v p coef za zb o mem")
            x_in = [sem(f"f_in{b}") for b in range(4)]
            o_out = [sem(f"f_out{b}") for b in range(4)]
            block = ctx.enter_context(nc.Block())
            whole = NT // 4 * 4

            def by_four(eng, body):
                for t in range(4):
                    body(t, 0, t)
                with eng.Fori(1, NT // 4) as i:
                    for b in range(4):
                        body(4 * i + b, i, b)
                for t in range(whole, NT):
                    body(t, t // 4, t % 4)

            @block.sync
            def _(sp):
                sp.dma_start(gam[:, :], wide(gamma3)).then_inc(s_w, 16)
                sp.dma_start(bet[:, :], wide(beta3)).then_inc(s_w, 16)

                def body(t, k, b):
                    wait_count(sp, o_out[b], 16 * k)
                    sp.dma_start(x3[b][0:rows_of(t), :], rows(x3_d, t)).then_inc(x_in[b], 16)
                by_four(sp, body)

            @block.scalar
            def _(act):
                def body(t, k, b):
                    act.wait_ge(s_o, t + 1)
                    act.dma_start(rows(out, t), x3[b][0:rows_of(t), :]).then_inc(o_out[b], 16)
                by_four(act, body)
                for b in range(4):
                    act.wait_ge(o_out[b], 16 * ((NT - b + 3) // 4))

            @block.tensor
            def _(pe):
                pe.wait_ge(s_mem, 2)
                nc.tensor.matmul(ps_1[:, :], ones[:, :], sum1[:, :], start=True, stop=True)
                nc.tensor.matmul(ps_2[:, :], ones[:, :], sum2[:, :], start=True, stop=True).then_inc(s_mm, 1)

            @block.gpsimd
            def _(pool):
                nc.gpsimd.memset(ones[:, :], 1.0).then_inc(s_mem, 1)
                nc.gpsimd.memset(half[:, :], -0.5).then_inc(s_mem, 1)
                pool.wait_ge(s_mem, 2)
                pool.wait_ge(s_v, 4)
                nc.gpsimd.tensor_tensor(out=a_row[:, :], in0=var[:, :], in1=half[:, :], op=POW).then_inc(s_p, 1)
                pool.wait_ge(s_coef, 2)

                def body(t, k, b):
                    nc.gpsimd.tensor_tensor(out=slot(t), in0=slot(t), in1=a_row[:, :], op=MUL).then_inc(s_za, 1)
                by_four(pool, body)

            @block.vector
            def _(dve):
                dve.wait_ge(s_mm, 1)
                dve.wait_ge(s_w, 32)
                nc.vector.tensor_scalar(out=mean[:, :], in0=ps_1[:, :], scalar1=1.0 / N, scalar2=None,
                                        op0=MUL).then_inc(s_v, 1)
                dve.wait_ge(s_v, 1)
                nc.vector.tensor_tensor(out=b_row[:, :], in0=mean[:, :], in1=mean[:, :], op=MUL).then_inc(s_v, 1)
                dve.wait_ge(s_v, 2)
                nc.vector.scalar_tensor_tensor(out=var[:, :], in0=ps_2[:, :], scalar=1.0 / N, in1=b_row[:, :],
                                               op0=MUL, op1=SUB).then_inc(s_v, 1)
                dve.wait_ge(s_v, 3)
                nc.vector.tensor_scalar(out=var[:, :], in0=var[:, :], scalar1=0.0, scalar2=BN_EPS,
                                        op0=MAX, op1=ADD).then_inc(s_v, 1)
                dve.wait_ge(s_p, 1)
                nc.vector.tensor_tensor(out=a_row[:, :], in0=a_row[:, :], in1=gam[:, :], op=MUL).then_inc(s_coef, 1)
                dve.wait_ge(s_coef, 1)
                nc.vector.tensor_tensor(out=b_row[:, :], in0=mean[:, :], in1=a_row[:, :], op=MUL).then_inc(s_v, 1)
                dve.wait_ge(s_v, 5)
                nc.vector.tensor_tensor(out=b_row[:, :], in0=bet[:, :], in1=b_row[:, :], op=SUB).then_inc(s_coef, 1)
                dve.wait_ge(s_coef, 2)

                def body(t, k, b):
                    dve.wait_ge(s_za, t + 1)
                    nc.vector.tensor_tensor(out=slot(t), in0=slot(t), in1=b_row[:, :], op=ADD).then_inc(s_zb, 1)
                    dve.wait_ge(s_zb, t + 1)
                    dve.wait_ge(x_in[b], 16 * (k + 1))
                    nc.vector.scalar_tensor_tensor(out=x3[b][:, :], in0=slot(t), scalar=0.0, in1=x3[b][:, :],
                                                   op0=MAX, op1=ADD).then_inc(s_o, 1)
                by_four(dve, body)

    prepare_weights()
    prepare_graph()
    gcn_project()
    edge_sums_gcn()
    gcn_finish()
    recycle_semaphores()
    edge_products("a0", x1_d, True, True, True, SCALE_LN, "neigh0")
    sage_layer(0)
    edge_products("a1", h_d, True, False, True, SCALE_UNIT, "neigh1")
    sage_layer(1)
    edge_products("a2", h_d, True, False, True, SCALE_UNIT, "neigh2")
    sage_layer(2)
    recycle_semaphores()
    edge_network()
    edge_products("a3", msg_d, False, False, False, None, None, W3[D:2 * D, :])
    node_update()
    recycle_semaphores()
    edge_products("a4", x3_d, True, True, True, SCALE_LN, "aggr")
    shiftb, sum1, sum2 = (sb(top, n, [P, D]) for n in ("shiftb", "sum1", "sum2"))
    batch_rows(True, shiftb, sum1, sum2)
    batch_rows(False, shiftb, sum1, sum2)
    finish(sum1, sum2)
    top.close()


_INS = ["x", "src", "dst", "edge_attr_64", "L0_gnn_W_conv", "L0_gnn_b_conv", "L0_gnn_W_lin", "L0_gnn_b_lin",
        "L1_gnn_W_self", "L1_gnn_W_neigh", "L1_gnn_b", "L2_gnn_W1", "L2_gnn_b1", "L2_gnn_W2", "L2_gnn_b2",
        "L2_gnn_W3", "L2_gnn_b3", "L2_gnn_W4", "L2_gnn_b4", "L2_gnn_gamma", "L2_gnn_beta",
        "L3_gnn_W_l", "L3_gnn_b_l", "L3_gnn_W_r", "L3_gnn_gamma", "L3_gnn_beta"]


def kernel(**inputs):
    import numpy as _np
    import concourse.bacc as _bacc
    from concourse import mybir as _mybir
    from concourse.bass_utils import run_bass_kernel_spmd as _run

    nc = _bacc.Bacc("TRN2", target_bir_lowering=False, num_devices=1)
    arrays, args = {}, []
    for name in _INS:
        a = _np.asarray(inputs[name])
        if name in ("L3_gnn_W_l", "L3_gnn_W_r"):
            a = a.T
        a = _np.ascontiguousarray(a)
        arrays[f"in_{name}"] = a
        args.append(nc.dram_tensor(f"in_{name}", a.shape, _mybir.dt.from_np(a.dtype), kind="ExternalInput").ap())
    out = nc.dram_tensor("out_rows", (N, D), F32, kind="ExternalOutput").ap()
    gnn_program(nc, *args, out)
    r = _run(nc, [arrays], core_ids=[0])
    return r.results[0]["out_rows"]
```

```python
from contextlib import ExitStack

import concourse.bass as bass
from concourse import mybir

P = 128
F32 = mybir.dt.float32
F16 = mybir.dt.float16
BF16 = mybir.dt.bfloat16
I32 = mybir.dt.int32
ALU = mybir.AluOpType
ACT = mybir.ActivationFunctionType
AX = mybir.AxisListType
ADD, SUB, MUL, MAX, MIN, POW = ALU.add, ALU.subtract, ALU.mult, ALU.max, ALU.min, ALU.pow

N, D, E, ED, HID = 10000, 512, 2500, 64, 128
C = D // P
NT = -(-N // P)
TAIL = N - (NT - 1) * P
NPAD = NT * P
EPT = P - 1
ET = -(-E // EPT)
EQ = 20
EP = E // EQ
assert EP * EQ == E and EP <= P
NOWHERE = 2 * N
LN_EPS, NORM_EPS, BN_EPS = 1e-5, 1e-12, 1e-5
PEEL = 6
SCALE_LN = 2.0 ** 11
SCALE_UNIT = 2.0 ** 15
MISH_CAP = 10.0


def wait_count(eng, sem, n):
    if not isinstance(n, int) or n > 0:
        eng.wait_ge(sem, n)


def each_tile(eng, n, body):
    for t in range(PEEL):
        body(t, t // 2, t % 2)
    with eng.Fori(PEEL // 2, n // 2) as i:
        body(2 * i, i, 0)
        body(2 * i + 1, i, 1)
    if n % 2:
        body(n - 1, n // 2, 0)


def ago(n, t, k, b):
    for _ in range(n):
        t, k, b = t - 1, (k if b else k - 1), 1 - b
    return t, k, b


def started(n, t):
    return not isinstance(t, int) or t >= n


def last(n, lag):
    return [(t, t // 2, t % 2) for t in range(n - lag, n)]


class Tile:

    def __init__(self, i, j):
        self.i, self.j = (i + j // 4 if j // 4 else i), j % 4
        self.t = 4 * self.i + self.j

    def buf(self, n):
        return self.j % n

    def uses(self, n):
        if n == 1:
            return self.t
        return self.i if n == 4 else 2 * self.i + self.j // 2

    def later(self, n):
        return Tile(self.i, self.j + n)


def pipeline(eng, n, *stages, peel=12):
    def step(t):
        for lag, stage in stages:
            tile = t.later(-lag)
            if not isinstance(tile.i, int) or 0 <= tile.t < n:
                stage(tile)

    for t in range(min(peel, n)):
        step(Tile(t // 4, t % 4))
    whole = max(n // 4 * 4, peel)
    if whole > peel:
        with eng.Fori(peel // 4, whole // 4) as i:
            for j in range(4):
                step(Tile(i, j))
    for t in range(min(whole, n) if n < peel else whole, n + max(lag for lag, _ in stages)):
        step(Tile(t // 4, t % 4))


def gnn_program(nc, x, src, dst, edge_attr, Wc, bc, Wlin, blin, Wself, Wneigh, bsage, W1, b1, W2, b2,
                W3, b3, W4, b4, gamma2, beta2, WlT, bl, WrT, gamma3, beta3, out):
    top = ExitStack()

    def dram(name, shape, dt=F32):
        return nc.dram_tensor(name, shape, dt, kind="Internal").ap()

    hw_d = dram("hw_rows", [NPAD, HID])
    gcn_d = dram("gcn_sums", [NPAD, HID])
    agg_d = dram("neighbour_rows", [NPAD, D])
    x1_d = dram("x1_rows", [NPAD, D])
    x2_d = dram("x2_rows", [NPAD, D])
    x3_d = dram("x3_rows", [NPAD, D])
    h_d = dram("sage_rows", [NPAD, D])
    hid_d = dram("hidden_rows_turned", [P, ET * D])
    rec_d = dram("edge_records", [ET * P, 8])
    cnt_d = dram("in_degree", [NPAD, 1])
    sel_d = dram("selections", [P, ET * 2 * P])

    units = {"conv": (Wc, 1), **{f"self{l}": (Wself[l], 1) for l in range(3)},
             **{f"neigh{l}": (Wneigh[l], 1) for l in range(3)},
             "edge": (W1[0:2 * D, :], 2), "update": (W3[0:D, :], 1), "aggr": (WlT, 1), "root": (WrT, 1)}
    unit_no = {name: n for n, name in enumerate(units)}
    cols = {name: w.shape[0] // P * w.shape[1] for name, (w, _) in units.items()}
    split_d = {name: dram(f"split_{name}", [P, 2 * cols[name]], F16) for name in units}
    NU = len(units)

    def sb(ctx, name, shape, dt=F32):
        return ctx.enter_context(nc.sbuf_tensor(name, shape, dt))

    def ps(ctx, name, shape=(P, D)):
        return ctx.enter_context(nc.psum_tensor(name, list(shape), F32))

    taken = []

    def sem(name):
        taken.append(nc.alloc_semaphore(name))
        return taken[-1]

    def sems(phase, names):
        return [sem(f"{phase}_{n}") for n in names.split()]

    def pair(phase, name, n=2):
        return [sem(f"{phase}_{name}{b}") for b in range(n)]

    def recycle_semaphores():
        nc.clear_and_free_semaphores(taken)
        taken.clear()
        nc.all_engine_barrier()

    slots = sb(top, "slots", [P, NT * D])
    ident = sb(top, "ident", [P, P])
    dis = sb(top, "dis", [P, NT])
    src_i = sb(top, "src_i", [P, ET], I32)
    dst_i = sb(top, "dst_i", [P, ET], I32)
    put_i = sb(top, "put_i", [P, ET], I32)
    edge_i = sb(top, "edge_i", [P, ET], I32)
    up = sb(top, "up", [P, NU])
    down = sb(top, "down", [P, NU])
    eps_col = sb(top, "eps_col", [P, 1])
    minus_half = sb(top, "minus_half", [P, 1])
    minus_one = sb(top, "minus_one", [P, 1])
    two_col = sb(top, "two_col", [P, 1])
    unscale = sb(top, "unscale", [P, P], F16)
    slots16 = slots[:, :].bitcast(F16)

    def slot(t):
        return slots[:, bass.ds(t * D, D)]

    def slot_hi(t):
        return slots16[:, bass.ds(t * 2 * D, D)]

    def slot_lo(t):
        return slots16[:, bass.ds(t * 2 * D + D, D)]

    def rows_of(t):
        return TAIL if isinstance(t, int) and t == NT - 1 else P

    def rows(ap, t):
        return ap[bass.ds(t * P, rows_of(t)), :]

    def wide(vec):
        return vec.rearrange("(o d) -> o d", o=1).to_broadcast([P, vec.shape[0]])

    def product(pe, out_ap, hi, lo, w, n, nchunks=C, first=True, stop=True):
        size = nchunks * n
        ins = None
        for c in range(nchunks):
            for m, (a, part) in enumerate(((hi, 0), (hi, 1), (lo, 0))):
                ins = nc.tensor.matmul(out_ap, a(c), w[:, part * size + c * n:part * size + (c + 1) * n],
                                       start=first and c == 0 and m == 0,
                                       stop=stop and c == nchunks - 1 and m == 2)
        return ins

    def transposes(pe, out_ap, in_ap):
        for c in range(C):
            ins = nc.tensor.transpose(out_ap[:, c * P:(c + 1) * P], in_ap[:, c * P:(c + 1) * P], ident[:, :])
        return ins

    def prepare():
        with ExitStack() as ctx:
            mx = sb(ctx, "w_mx", [P, NU])
            mxa = sb(ctx, "w_mxa", [P, NU])
            ex = sb(ctx, "w_ex", [P, NU], I32)
            fld = sb(ctx, "w_fld", [P, NU], I32)
            inv = sb(ctx, "w_inv", [P, NU], I32)
            JOB = C * D
            jobs = [(n, name, c0, min(JOB, cols[name])) for n, name in enumerate(units)
                    for c0 in range(0, cols[name], JOB)]
            parts_all = sb(ctx, "w_parts", [P, 4 * 2 * JOB], F16)
            parts = [parts_all[:, b * 2 * JOB:(b + 1) * 2 * JOB] for b in range(4)]
            LQ = 9
            base, at = {}, 0
            for name in units:
                base[name] = at
                at += cols[name]
            ZW = NT * D // 16
            row_i = parts_all[:, 0:2 * E].bitcast(I32)
            row_f = slots[:, at:at + E]
            key = slots[:, at + E:at + 2 * E]
            junk = slots[:, at + 2 * E:at + 3 * E].bitcast(BF16)
            junk_v, junk_s = junk[:, 0:E], junk[:, E:2 * E]
            sel_at = at + 3 * E
            sel = slots[:, sel_at:sel_at + ET * 2 * P]
            zeros_at = sel_at + ET * 2 * P
            zeros = slots[:, zeros_at:zeros_at + ZW]
            assert zeros_at + ZW <= (NT - 1) * D
            col_i = sb(ctx, "g_col_i", [P, EQ], I32)
            scol_i = sb(ctx, "g_scol_i", [P, EQ], I32)
            (col_f, neg_f, neg_key, mine, base_key, sign, equal, less, before, rank, put_f, is_last) = (
                sb(ctx, f"g_{n}", [P, EQ]) for n in ("col_f", "neg_f", "neg_key", "mine", "base_key", "sign", "equal",
                                                     "less", "before", "rank", "put_f", "is_last"))
            whole = [sb(ctx, f"g_whole{b}", [P, EQ]) for b in range(2)]
            put_u = sb(ctx, "g_put_u", [P, EQ], I32)
            pos_u = sb(ctx, "g_pos_u", [P, EQ], I32)
            rec = sb(ctx, "g_rec", [P, EQ, 8])
            blank = sb(ctx, "g_blank", [P, ET, 8])
            recs = sb(ctx, "g_recs", [P, ET, 8])
            offs = sb(ctx, "g_offs", [P, ET])
            first_j = sb(ctx, "g_first_j", [P, ET])
            jrow = sb(ctx, "g_jrow", [P, P])
            tri = sb(ctx, "g_tri", [P, P])
            selT = [sb(ctx, f"g_selT{b}", [P, 2 * P]) for b in range(2)]
            cnt = sb(ctx, "g_cnt", [P, P])
            deg = sb(ctx, "g_deg", [P, NT])
            half = sb(ctx, "g_half", [P, NT])
            ps_sel = [ps(ctx, f"g_ps_sel{b}") for b in range(2)]
            ps_cnt = ps(ctx, "g_ps_cnt")
            zid, made, s_max, s_all, s_exp, s_up, s_hi, s_lo = sems("w", "zid made max all exp up hi lo")
            loaded = [sem(f"w_in{n}") for n in range(NU)]
            stored = pair("w", "out", 4)
            (s_in, s_zero, s_made, s_cast, s_key, s_sign, s_col, s_ready, s_blank, s_rec, s_cntin,
             s_recs, s_link, s_selT, s_turn, s_sel, s_selout, s_cload, s_cT, s_deg, s_dis) = sems(
                "g", "in zero made cast key sign col ready blank rec cntin recs link selT turn sel "
                "selout cload cT deg dis")
            block = ctx.enter_context(nc.Block())

            def raw(name):
                return slots[:, base[name]:base[name] + cols[name]]

            @block.sync
            def _(sp):
                sp.dma_start(col_i[0:EP, :], dst.rearrange("(p q) -> p q", q=EQ)).then_inc(s_in, 16)
                sp.dma_start(scol_i[0:EP, :], src.rearrange("(p q) -> p q", q=EQ)).then_inc(s_in, 16)
                sp.dma_start(row_i, wide(dst)).then_inc(s_in, 16)
                for n, (name, (w, _)) in enumerate(units.items()):
                    sp.dma_start(raw(name).rearrange("p (c m) -> p c m", m=w.shape[1]),
                                 w.rearrange("(c p) m -> p c m", p=P)).then_inc(loaded[n], 16)
                sp.wait_ge(s_made, 1)
                sp.dma_start(cnt_d.rearrange("(p a) o -> p (a o)", p=P), zeros[:, 0:NT]).then_inc(s_blank, 16)
                sp.dma_start(rec_d.rearrange("(p a) f -> p a f", p=P), blank[:, :, :]).then_inc(s_blank, 16)
                agg_v = agg_d.rearrange("(p a) d -> p (a d)", p=P)
                gcn_v = gcn_d.rearrange("(p a) d -> p (a d)", p=P)
                for q in range(4):
                    sp.dma_start(gcn_v[:, q * ZW:(q + 1) * ZW], zeros).then_inc(s_zero, 16)
                for q in range(16):
                    sp.dma_start(agg_v[:, q * ZW:(q + 1) * ZW], zeros).then_inc(s_zero, 16)
                sp.wait_ge(s_rec, 16 * EQ)
                sp.dma_start(recs[:, :, :], rec_d.rearrange("(t p) f -> p t f", p=P)).then_inc(s_recs, 16)
                for k, (n, name, c0, m) in enumerate(jobs):
                    sp.wait_ge(s_lo, k + 1)
                    sp.dma_start(split_d[name].rearrange("p (two m) -> p two m", two=2)[:, :, c0:c0 + m],
                                 parts[k % 4][:, 0:2 * m].rearrange("p (two m) -> p two m", two=2)).then_inc(
                        stored[k % 4], 16)
                sp.wait_ge(s_sel, ET)
                sp.dma_start(sel_d[:, :], sel).then_inc(s_selout, 16)
                sp.wait_ge(s_selout, 16)
                for b in range(4):
                    sp.wait_ge(stored[b], 16 * ((len(jobs) + 3 - b) // 4))
                sp.wait_ge(s_zero, 320)

            @block.gpsimd
            def _(pool):
                nc.gpsimd.iota(key, pattern=[[1, E]], base=-(N * E // 2), channel_multiplier=0,
                               allow_small_or_imprecise_dtypes=True).then_inc(s_col, 1)
                nc.gpsimd.iota(mine[:, :], pattern=[[1, EQ]], base=0, channel_multiplier=EQ,
                               allow_small_or_imprecise_dtypes=True).then_inc(s_col, 1)
                nc.gpsimd.iota(base_key[:, :], pattern=[[1, EQ]], base=-(N * E // 2), channel_multiplier=EQ,
                               allow_small_or_imprecise_dtypes=True).then_inc(s_col, 1)
                nc.gpsimd.iota(offs[:, :], pattern=[[EPT, ET]], base=-1, channel_multiplier=0,
                               allow_small_or_imprecise_dtypes=True).then_inc(s_col, 1)
                nc.gpsimd.iota(jrow[:, :], pattern=[[1, P]], base=0, channel_multiplier=0,
                               allow_small_or_imprecise_dtypes=True).then_inc(s_col, 1)
                nc.gpsimd.memset(tri[:, :], 1.0).then_inc(s_col, 1)
                nc.gpsimd.memset(half[:, :], -0.5).then_inc(s_col, 1)
                nc.gpsimd.memset(ident[:, :], 0.0).then_inc(zid, 1)
                nc.gpsimd.memset(unscale[:, :], 0.0).then_inc(zid, 1)
                nc.gpsimd.memset(eps_col[:, :], LN_EPS)
                nc.gpsimd.memset(minus_half[:, :], -0.5)
                nc.gpsimd.memset(minus_one[:, :], -1.0)
                nc.gpsimd.memset(two_col[:, :], 2.0)
                pool.wait_ge(zid, 2)
                nc.gpsimd.affine_select(out=ident[:, :], in_=ident[:, :], compare_op=ALU.not_equal, fill=1.0,
                                        base=0, pattern=[[-1, P]], channel_multiplier=1).then_inc(made, 1)
                nc.gpsimd.affine_select(out=unscale[:, :], in_=unscale[:, :], compare_op=ALU.not_equal,
                                        fill=1.0 / SCALE_LN, base=0, pattern=[[-1, P]],
                                        channel_multiplier=1).then_inc(made, 1)
                pool.wait_ge(s_col, 7)
                nc.gpsimd.affine_select(out=tri[:, :], in_=tri[:, :], compare_op=ALU.is_ge, fill=0.0, base=0,
                                        pattern=[[-1, P]], channel_multiplier=1).then_inc(s_col, 1)
                pool.wait_ge(s_blank, 32)
                pool.wait_ge(s_ready, 1)
                for q in range(EQ):
                    nc.gpsimd.indirect_dma_start(
                        rec_d[:, :], bass.IndirectOffsetOnAxis(ap=pos_u[0:EP, q:q + 1], axis=0),
                        rec[0:EP, q, :], None).then_inc(s_rec, 16)
                pool.wait_ge(s_max, NU)
                nc.gpsimd.partition_all_reduce(mxa[:, :], mx[:, :], P, bass.bass_isa.ReduceOp.max)\
                    .then_inc(s_all, 1)
                for q in range(EQ):
                    nc.gpsimd.indirect_dma_start(
                        cnt_d[:, :], bass.IndirectOffsetOnAxis(ap=put_u[0:EP, q:q + 1], axis=0),
                        equal[0:EP, q:q + 1], None, bounds_check=N - 1, oob_is_err=False).then_inc(s_cntin, 16)
                pool.wait_ge(s_cntin, 16 * EQ)
                nc.gpsimd.dma_start(cnt[0:NT, :], cnt_d.rearrange("(t p) o -> t (p o)", p=P)).then_inc(s_cload, 16)
                pool.wait_ge(made, 2)
                pool.wait_ge(s_deg, 1)
                nc.gpsimd.tensor_tensor(out=dis[:, :], in0=deg[:, :], in1=half[:, :], op=POW).then_inc(s_dis, 1)
                pool.wait_ge(s_dis, 1)

            @block.scalar
            def _(act):
                act.wait_ge(s_key, 2)
                for q in range(EQ):
                    nc.scalar.activation(junk_s[0:EP, :], key[0:EP, :], ACT.Sign, bias=neg_key[0:EP, q:q + 1],
                                         accum_out=sign[0:EP, q:q + 1]).then_inc(s_sign, 1)
                    act.wait_ge(s_sign, q + 1)
                for n, q in enumerate(range(LQ, EQ)):
                    nc.scalar.activation(junk_s[0:EP, :], row_f[0:EP, :], ACT.Sign, bias=neg_f[0:EP, q:q + 1],
                                         accum_out=less[0:EP, q:q + 1]).then_inc(s_sign, 1)
                    act.wait_ge(s_sign, EQ + n + 1)
                act.wait_ge(s_up, 2)
                for k, (n, name, c0, m) in enumerate(jobs):
                    wait_count(act, stored[k % 4], 16 * (k // 4))
                    nc.scalar.activation(parts[k % 4][:, 0:m], raw(name)[:, c0:c0 + m], ACT.Copy,
                                         scale=up[:, n:n + 1]).then_inc(s_hi, 1)
                for t in range(ET):
                    act.wait_ge(s_turn, t + 1)
                    nc.scalar.activation(sel[:, t * 2 * P:(t + 1) * 2 * P], ps_sel[t % 2][:, 0:2 * P],
                                         ACT.Copy).then_inc(s_sel, 1)

            @block.vector
            def _(dve):
                links = [0]

                def link(ins):
                    links[0] += 1
                    ins.then_inc(s_link, 1)
                    dve.wait_ge(s_link, links[0])

                nc.vector.memset(slot(NT - 1), 0.0)
                link(nc.vector.memset(blank[:, :, :], 0.0))
                nc.vector.memset(blank[:, :, 2], float(NOWHERE))
                nc.vector.memset(blank[:, :, 3], 1e6)
                nc.vector.memset(cnt[:, :], 0.0)
                link(nc.vector.memset(rec[:, :, :], 0.0))
                nc.vector.memset(zeros, 0.0).then_inc(s_made, 1)
                dve.wait_ge(s_in, 48)
                nc.vector.tensor_copy(row_f, row_i).then_inc(s_cast, 1)
                nc.vector.tensor_copy(col_f[0:EP, :], col_i[0:EP, :]).then_inc(s_cast, 1)
                nc.vector.tensor_copy(rec[0:EP, :, 0], scol_i[0:EP, :]).then_inc(s_cast, 1)
                dve.wait_ge(s_cast, 3)
                dve.wait_ge(s_col, 3)
                nc.vector.scalar_tensor_tensor(out=key[0:EP, :], in0=row_f[0:EP, :], scalar=float(E),
                                               in1=key[0:EP, :], op0=MUL, op1=ADD).then_inc(s_key, 1)
                link(nc.vector.scalar_tensor_tensor(out=base_key[0:EP, :], in0=col_f[0:EP, :], scalar=float(E),
                                                    in1=base_key[0:EP, :], op0=MUL, op1=ADD))
                nc.vector.tensor_scalar(out=neg_f[0:EP, :], in0=col_f[0:EP, :], scalar1=-1.0,
                                        scalar2=None, op0=MUL)
                nc.vector.tensor_scalar(out=neg_key[0:EP, :], in0=base_key[0:EP, :], scalar1=-1.0,
                                        scalar2=None, op0=MUL).then_inc(s_key, 1)
                for q in range(EQ):
                    link(nc.vector.tensor_scalar(out=junk_v[0:EP, :], in0=row_f[0:EP, :],
                                                 scalar1=col_f[0:EP, q:q + 1], scalar2=0.0, op0=ALU.is_equal,
                                                 op1=ADD, accum_out=equal[0:EP, q:q + 1]))
                    if q < LQ:
                        link(nc.vector.tensor_scalar(out=junk_v[0:EP, :], in0=row_f[0:EP, :],
                                                     scalar1=col_f[0:EP, q:q + 1], scalar2=0.0, op0=ALU.is_lt,
                                                     op1=ADD, accum_out=less[0:EP, q:q + 1]))
                dve.wait_ge(s_sign, EQ + EQ - LQ)
                a = slice(0, EP)
                link(nc.vector.tensor_tensor(out=less[a, LQ:EQ], in0=less[a, LQ:EQ], in1=equal[a, LQ:EQ], op=ADD))
                link(nc.vector.tensor_scalar(out=less[a, LQ:EQ], in0=less[a, LQ:EQ], scalar1=-0.5,
                                             scalar2=0.5 * E, op0=MUL, op1=ADD))
                link(nc.vector.tensor_scalar(out=rank[a, :], in0=sign[a, :], scalar1=-0.5,
                                             scalar2=0.5 * (E - 1), op0=MUL, op1=ADD))
                link(nc.vector.tensor_tensor(out=before[a, :], in0=rank[a, :], in1=less[a, :], op=SUB))
                link(nc.vector.tensor_scalar(out=whole[0][a, :], in0=rank[a, :], scalar1=1.0, scalar2=None, op0=ADD))
                for n in range(1, ET):
                    link(nc.vector.scalar_tensor_tensor(out=whole[n % 2][a, :], in0=rank[a, :],
                                                        scalar=float(n * EPT), in1=whole[(n - 1) % 2][a, :],
                                                        op0=ALU.is_ge, op1=ADD))
                link(nc.vector.tensor_copy(pos_u[a, :], whole[(ET - 1) % 2][a, :]))
                link(nc.vector.tensor_tensor(out=is_last[a, :], in0=equal[a, :], in1=before[a, :], op=SUB))
                link(nc.vector.tensor_scalar(out=is_last[a, :], in0=is_last[a, :], scalar1=1.0, scalar2=None,
                                             op0=ALU.is_equal))
                link(nc.vector.scalar_tensor_tensor(out=put_f[a, :], in0=col_f[a, :], scalar=-float(NOWHERE),
                                                    in1=is_last[a, :], op0=ADD, op1=MUL))
                link(nc.vector.tensor_scalar(out=rec[a, :, 2], in0=put_f[a, :], scalar1=float(NOWHERE),
                                             scalar2=None, op0=ADD))
                link(nc.vector.tensor_copy(put_u[a, :], rec[a, :, 2]))
                link(nc.vector.tensor_copy(rec[a, :, 1], col_f[a, :]))
                link(nc.vector.tensor_copy(rec[a, :, 3], less[a, :]))
                link(nc.vector.reciprocal(rec[a, :, 4], equal[a, :]))
                nc.vector.tensor_copy(rec[a, :, 5], mine[a, :]).then_inc(s_ready, 1)
                for n, name in enumerate(units):
                    dve.wait_ge(loaded[n], 16)
                    nc.vector.tensor_reduce(out=mx[:, n:n + 1], in_=raw(name), op=MAX, axis=AX.X,
                                            apply_absolute_value=True).then_inc(s_max, 1)
                dve.wait_ge(s_all, 1)
                nc.vector.tensor_scalar(out=ex[:, :], in0=mxa[:, :].bitcast(I32), scalar1=23, scalar2=None,
                                        op0=ALU.logical_shift_right).then_inc(s_exp, 1)
                dve.wait_ge(s_exp, 1)
                nc.vector.tensor_scalar(out=fld[:, :], in0=ex[:, :], scalar1=-1.0, scalar2=268.0,
                                        op0=MUL, op1=ADD).then_inc(s_exp, 1)
                dve.wait_ge(s_exp, 2)
                nc.vector.tensor_scalar(out=ex[:, :], in0=fld[:, :], scalar1=253.0, scalar2=1.0,
                                        op0=MIN, op1=MAX).then_inc(s_exp, 1)
                dve.wait_ge(s_exp, 3)
                nc.vector.tensor_scalar(out=inv[:, :], in0=ex[:, :], scalar1=-1.0, scalar2=254.0,
                                        op0=MUL, op1=ADD).then_inc(s_exp, 1)
                nc.vector.tensor_scalar(out=up[:, :].bitcast(I32), in0=ex[:, :], scalar1=23, scalar2=None,
                                        op0=ALU.logical_shift_left).then_inc(s_up, 1)
                dve.wait_ge(s_exp, 4)
                nc.vector.tensor_scalar(out=down[:, :].bitcast(I32), in0=inv[:, :], scalar1=23, scalar2=None,
                                        op0=ALU.logical_shift_left).then_inc(s_up, 1)
                dve.wait_ge(s_up, 2)
                for k, (n, name, c0, m) in enumerate(jobs):
                    dve.wait_ge(s_hi, k + 1)
                    nc.vector.scalar_tensor_tensor(out=parts[k % 4][:, m:2 * m], in0=raw(name)[:, c0:c0 + m],
                                                   scalar=up[:, n:n + 1], in1=parts[k % 4][:, 0:m],
                                                   op0=MUL, op1=SUB).then_inc(s_lo, 1)
                dve.wait_ge(s_cT, 1)
                nc.vector.tensor_scalar(out=deg[:, :], in0=ps_cnt[:, 0:NT], scalar1=1.0, scalar2=None,
                                        op0=ADD).then_inc(s_deg, 1)
                dve.wait_ge(s_recs, 16)
                nc.vector.tensor_copy(src_i[:, :], recs[:, :, 0])
                nc.vector.tensor_copy(dst_i[:, :], recs[:, :, 1])
                nc.vector.tensor_copy(put_i[:, :], recs[:, :, 2])
                nc.vector.tensor_copy(edge_i[:, :], recs[:, :, 5])
                dve.wait_ge(s_col, 8)
                link(nc.vector.tensor_tensor(out=first_j[:, :], in0=recs[:, :, 3], in1=offs[:, :], op=SUB))
                for t in range(ET):
                    wait_count(dve, s_turn, t - 1)
                    link(nc.vector.scalar_tensor_tensor(out=selT[t % 2][:, 0:P], in0=jrow[:, :],
                                                        scalar=first_j[:, t:t + 1], in1=tri[:, :],
                                                        op0=ALU.is_ge, op1=MUL))
                    nc.vector.tensor_scalar(out=selT[t % 2][:, P:2 * P], in0=selT[t % 2][:, 0:P],
                                            scalar1=recs[:, t, 4:5], scalar2=None, op0=MUL).then_inc(s_selT, 1)

            @block.tensor
            def _(pe):
                pe.wait_ge(made, 1)
                pe.wait_ge(s_cload, 16)
                nc.tensor.transpose(ps_cnt[:, 0:P], cnt[:, :], ident[:, :]).then_inc(s_cT, 1)
                for t in range(ET):
                    pe.wait_ge(s_selT, t + 1)
                    wait_count(pe, s_sel, t - 1)
                    nc.tensor.transpose(ps_sel[t % 2][:, 0:P], selT[t % 2][:, 0:P], ident[:, :])
                    nc.tensor.transpose(ps_sel[t % 2][:, P:2 * P], selT[t % 2][:, P:2 * P],
                                        ident[:, :]).then_inc(s_turn, 1)

    class Norm:
        def __init__(self, ctx, name, n=4):
            self.n = n
            self.stats, self.mv, self.ve, self.rstd, self.shift, self.nm = (
                [sb(ctx, f"{name}_{part}{b}", [P, size]) for b in range(n)]
                for part, size in (("st", 6), ("mv", 2), ("ve", 1), ("rs", 1), ("sh", 1), ("nm", 1)))
            self.pause = sb(ctx, f"{name}_pause", [P, 1])
            self.s_stats, self.s_mv, self.s_ve, self.s_rstd, self.s_ready = sems(
                name, "stats mv ve rstd ready")

        def moments(self, dve, in_ap, v):
            nc.vector.bn_stats(self.stats[v.buf(self.n)][:, :], in_ap).then_inc(self.s_stats, 1)

        def aggregate(self, dve, v):
            b = v.buf(self.n)
            dve.wait_ge(self.s_stats, v.t + 1)
            wait_count(dve, self.s_ready, v.t + 1 - self.n)
            nc.vector.memset(self.pause[:, :], 0.0)
            nc.vector.bn_aggr(self.mv[b][:, :], self.stats[b][:, :]).then_inc(self.s_mv, 1)

        def factors(self, pool, v, s_used):
            b = v.buf(self.n)
            pool.wait_ge(self.s_mv, v.t + 1)
            nc.gpsimd.tensor_tensor(out=self.nm[b][:, :], in0=self.mv[b][:, 0:1], in1=minus_one[:, :], op=MUL)
            nc.gpsimd.tensor_tensor(out=self.ve[b][:, :], in0=self.mv[b][:, 1:2], in1=eps_col[:, :],
                                    op=ADD).then_inc(self.s_ve, 1)
            pool.wait_ge(self.s_ve, v.t + 1)
            wait_count(pool, s_used, v.t + 1 - self.n)
            nc.gpsimd.tensor_tensor(out=self.rstd[b][:, :], in0=self.ve[b][:, :], in1=minus_half[:, :],
                                    op=POW).then_inc(self.s_rstd, 1)
            pool.wait_ge(self.s_rstd, v.t + 1)
            nc.gpsimd.tensor_tensor(out=self.shift[b][:, :], in0=self.nm[b][:, :], in1=self.rstd[b][:, :],
                                    op=MUL).then_inc(self.s_ready, 1)

        def apply(self, out_ap, in_ap, v, func=ACT.Relu):
            b = v.buf(self.n)
            return nc.scalar.activation(out_ap, in_ap, func, scale=self.rstd[b][:, 0:1],
                                        bias=self.shift[b][:, 0:1])

    def gcn_project():
        with ExitStack() as ctx:
            w = sb(ctx, "p_w", [P, 2 * cols["conv"]], F16)
            h = [sb(ctx, f"p_h{b}", [P, D]) for b in range(2)]
            hT = [sb(ctx, f"p_hT{b}", [P, 2 * D], F16) for b in range(2)]
            hw = [sb(ctx, f"p_hw{b}", [P, HID]) for b in range(4)]
            f = sb(ctx, "p_f", [P, 1])
            dis_f = sb(ctx, "p_dis_f", [P, NT])
            dcol = [sb(ctx, f"p_dcol{b}", [P, 1]) for b in range(2)]
            ps_t = [ps(ctx, f"p_ps_t{b}") for b in range(2)]
            ps_h = [ps(ctx, f"p_ps_h{b}") for b in range(2)]
            s_w, s_f, s_h, s_turn, s_hi, s_lo, s_mm, s_dcol, s_hw = sems(
                "p", "w f h turn hi lo mm dcol hw")
            x_in, hw_out = pair("p", "xin", 4), pair("p", "hwout", 4)
            norm = Norm(ctx, "p_norm")
            block = ctx.enter_context(nc.Block())

            @block.sync
            def _(sp):
                sp.dma_start(w[:, :], split_d["conv"][:, :]).then_inc(s_w, 16)

                def load(v):
                    wait_count(sp, norm.s_stats, v.t - 3)
                    sp.dma_start(slot(v.t)[0:rows_of(v.t), :], rows(x, v.t)).then_inc(x_in[v.buf(4)], 16)

                def store(v):
                    b = v.buf(4)
                    sp.wait_ge(s_hw, v.t + 1)
                    sp.dma_start(rows(hw_d, v.t), hw[b][0:rows_of(v.t), :]).then_inc(hw_out[b], 16)
                pipeline(sp, NT, (0, load), (8, store))
                for b in range(4):
                    sp.wait_ge(hw_out[b], 16 * ((NT + 3 - b) // 4))

            @block.vector
            def _(dve):
                nc.vector.tensor_scalar(out=f[:, :], in0=down[:, unit_no["conv"]:unit_no["conv"] + 1],
                                        scalar1=1.0 / SCALE_LN, scalar2=None, op0=MUL).then_inc(s_f, 1)
                dve.wait_ge(s_f, 1)
                nc.vector.tensor_scalar(out=dis_f[:, :], in0=dis[:, :], scalar1=f[:, 0:1], scalar2=None,
                                        op0=MUL).then_inc(s_f, 1)
                dve.wait_ge(s_f, 2)

                def moments(v):
                    dve.wait_ge(x_in[v.buf(4)], 16 * (v.uses(4) + 1))
                    norm.moments(dve, slot(v.t), v)

                def lo(v):
                    b = v.buf(2)
                    dve.wait_ge(s_hi, v.t + 1)
                    wait_count(dve, s_mm, v.t - 1)
                    nc.vector.scalar_tensor_tensor(out=hT[b][:, D:2 * D], in0=ps_t[b][:, :], scalar=SCALE_LN,
                                                   in1=hT[b][:, 0:D], op0=MUL, op1=SUB).then_inc(s_lo, 1)

                def degree(v):
                    wait_count(dve, s_hw, v.t - 1)
                    nc.vector.tensor_copy(dcol[v.buf(2)][:, :], dis_f[:, bass.ds(v.t, 1)]).then_inc(s_dcol, 1)
                pipeline(dve, NT, (6, degree), (0, moments), (4, lo), (0, lambda v: norm.aggregate(dve, v)))

            @block.gpsimd
            def _(pool):
                pipeline(pool, NT, (0, lambda v: norm.factors(pool, v, s_h)))

            @block.scalar
            def _(act):
                def hi(v):
                    b = v.buf(2)
                    act.wait_ge(s_turn, v.t + 1)
                    wait_count(act, s_mm, v.t - 1)
                    nc.scalar.activation(hT[b][:, 0:D], ps_t[b][:, :], ACT.Copy, scale=SCALE_LN).then_inc(s_hi, 1)

                def normed(v):
                    act.wait_ge(norm.s_ready, v.t + 1)
                    wait_count(act, s_turn, v.t - 1)
                    norm.apply(h[v.buf(2)][:, :], slot(v.t), v).then_inc(s_h, 1)

                def scaled(v):
                    b = v.buf(4)
                    act.wait_ge(s_dcol, v.t + 1)
                    act.wait_ge(s_mm, v.t + 1)
                    wait_count(act, hw_out[b], 16 * v.uses(4))
                    nc.scalar.activation(hw[b][:, :], ps_h[v.buf(2)][:, 0:HID], ACT.Copy,
                                         scale=dcol[v.buf(2)][:, 0:1]).then_inc(s_hw, 1)
                pipeline(act, NT, (4, hi), (2, normed), (6, scaled))

            @block.tensor
            def _(pe):
                pe.wait_ge(s_w, 16)

                def turn(v):
                    b = v.buf(2)
                    pe.wait_ge(s_h, v.t + 1)
                    wait_count(pe, s_lo, v.t - 1)
                    transposes(pe, ps_t[b], h[b]).then_inc(s_turn, 1)

                def project(v):
                    b = v.buf(2)
                    pe.wait_ge(s_lo, v.t + 1)
                    wait_count(pe, s_hw, v.t - 1)
                    product(pe, ps_h[b][:, 0:HID], lambda c: hT[b][:, c * P:(c + 1) * P],
                            lambda c: hT[b][:, D + c * P:D + (c + 1) * P], w, HID).then_inc(s_mm, 1)
                pipeline(pe, NT, (3, turn), (5, project))

    def edge_sums_gcn():
        with ExitStack() as ctx:
            m = [sb(ctx, f"q_m{b}", [P, HID]) for b in range(4)]
            sl = [sb(ctx, f"q_sel{b}", [P, P]) for b in range(4)]
            tot = [sb(ctx, f"q_tot{b}", [P, HID]) for b in range(4)]
            ps_c = ps(ctx, "q_ps_c")
            ps_s = [ps(ctx, f"q_ps_s{b}") for b in range(2)]
            s_carry, s_carried, s_sum, s_tot = sems("q", "carry carried sum tot")
            m_in, sel_in, t_out = pair("q", "min", 4), pair("q", "selin", 4), pair("q", "tout", 4)
            block = ctx.enter_context(nc.Block())

            @block.sync
            def _(sp):
                def load(v):
                    b = v.buf(4)
                    wait_count(sp, s_sum, v.t - 3)
                    sp.dma_start(sl[b][:, :], sel_d[:, bass.ds(v.t * 2 * P, P)]).then_inc(sel_in[b], 16)
                pipeline(sp, ET, (0, load), peel=8)

            @block.gpsimd
            def _(pool):
                def gather(v):
                    b = v.buf(4)
                    wait_count(pool, s_sum, v.t - 3)
                    nc.gpsimd.indirect_dma_start(
                        m[b][:, :], None, hw_d[0:N, :],
                        bass.IndirectOffsetOnAxis(ap=src_i[:, v.t:v.t + 1], axis=0)).then_inc(m_in[b], 16)

                def scatter(v):
                    b = v.buf(4)
                    pool.wait_ge(s_tot, v.t + 1)
                    nc.gpsimd.indirect_dma_start(
                        gcn_d[:, :], bass.IndirectOffsetOnAxis(ap=put_i[:, v.t:v.t + 1], axis=0),
                        tot[b][:, :], None, bounds_check=N - 1, oob_is_err=False).then_inc(t_out[b], 16)
                pipeline(pool, ET, (0, gather), (3, scatter), peel=ET)
                for b in range(4):
                    pool.wait_ge(t_out[b], 16 * (ET // 4))

            @block.vector
            def _(dve):
                def carry(v):
                    b = v.buf(4)
                    if isinstance(v.t, int) and v.t == 0:
                        return
                    dve.wait_ge(m_in[b], 16 * (v.uses(4) + 1))
                    dve.wait_ge(s_carry, v.t)
                    nc.vector.tensor_copy(m[b][0:1, :], ps_c[0:1, 0:HID]).then_inc(s_carried, 1)

                def totals(v):
                    b = v.buf(4)
                    dve.wait_ge(s_sum, v.t + 1)
                    wait_count(dve, t_out[b], 16 * v.uses(4))
                    nc.vector.tensor_copy(tot[b][:, :], ps_s[v.buf(2)][:, 0:HID]).then_inc(s_tot, 1)
                pipeline(dve, ET, (0, carry), (1, totals), peel=8)

            @block.tensor
            def _(pe):
                def sums(v):
                    b, p = v.buf(4), v.buf(2)
                    pe.wait_ge(sel_in[b], 16 * (v.uses(4) + 1))
                    pe.wait_ge(m_in[b], 16 * (v.uses(4) + 1))
                    wait_count(pe, s_carried, v.t)
                    nc.tensor.matmul(ps_c[0:1, 0:HID], sl[b][:, P - 1:P], m[b][:, :], start=True,
                                     stop=True).then_inc(s_carry, 1)
                    wait_count(pe, s_tot, v.t - 1)
                    nc.tensor.matmul(ps_s[p][:, 0:HID], sl[b][:, :], m[b][:, :], start=True,
                                     stop=True).then_inc(s_sum, 1)
                pipeline(pe, ET, (0, sums), peel=8)

    def gcn_finish():
        with ExitStack() as ctx:
            w = sb(ctx, "r_w", [P, D])
            bias_c = sb(ctx, "r_bias_c", [HID, 1])
            bias_l = sb(ctx, "r_bias_l", [P, D])
            hw = [sb(ctx, f"r_hw{b}", [P, HID]) for b in range(4)]
            gs = [sb(ctx, f"r_gs{b}", [P, HID]) for b in range(4)]
            diag = [sb(ctx, f"r_diag{b}", [P, P]) for b in range(2)]
            cT = [sb(ctx, f"r_cT{b}", [P, HID]) for b in range(2)]
            x1 = [sb(ctx, f"r_x1{b}", [P, D]) for b in range(4)]
            xb = [sb(ctx, f"r_xb{b}", [P, D]) for b in range(4)]
            h = [sb(ctx, f"r_h{b}", [P, D]) for b in range(2)]
            dcol = [sb(ctx, f"r_dcol{b}", [P, 1]) for b in range(2)]
            ps_c = [ps(ctx, f"r_ps_c{b}") for b in range(2)]
            ps_x = [ps(ctx, f"r_ps_x{b}") for b in range(2)]
            ps_t = [ps(ctx, f"r_ps_t{b}") for b in range(2)]
            s_w, s_dcol, s_diag, s_ct, s_cT, s_mm, s_xb, s_x1, s_h, s_turn, s_hi, s_lo = sems(
                "r", "w dcol diag ct cT mm xb x1 h turn hi lo")
            g_in, x_out = pair("r", "gin", 4), pair("r", "xout", 4)
            norm = Norm(ctx, "r_norm")
            block = ctx.enter_context(nc.Block())

            @block.sync
            def _(sp):
                sp.dma_start(w[:, :], Wlin[:, :]).then_inc(s_w, 16)
                sp.dma_start(bias_c[:, :], bc.rearrange("(p o) -> p o", o=1)).then_inc(s_w, 16)
                sp.dma_start(bias_l[:, :], wide(blin)).then_inc(s_w, 16)

                def load(v):
                    b, n = v.buf(4), rows_of(v.t)
                    wait_count(sp, s_ct, v.t - 3)
                    sp.dma_start(hw[b][0:n, :], rows(hw_d, v.t)).then_inc(g_in[b], 16)
                    sp.dma_start(gs[b][0:n, :], rows(gcn_d, v.t)).then_inc(g_in[b], 16)

                def store(v):
                    b = v.buf(4)
                    sp.wait_ge(s_x1, v.t + 1)
                    sp.dma_start(rows(x1_d, v.t), x1[b][0:rows_of(v.t), :]).then_inc(x_out[b], 16)
                pipeline(sp, NT, (0, load), (6, store))
                for b in range(4):
                    sp.wait_ge(x_out[b], 16 * ((NT + 3 - b) // 4))

            @block.gpsimd
            def _(pool):
                pool.wait_ge(s_w, 48)

                def add_bias(v):
                    b = v.buf(4)
                    wait_count(pool, s_x1, v.t - 3)
                    nc.gpsimd.tensor_tensor(out=xb[b][:, :], in0=slot(v.t), in1=bias_l[:, :], op=ADD)\
                        .then_inc(s_xb, 1)
                pipeline(pool, NT, (0, add_bias), (3, lambda v: norm.factors(pool, v, s_h)))

            @block.vector
            def _(dve):
                dve.wait_ge(s_w, 48)

                def degree(v):
                    wait_count(dve, s_diag, v.t - 1)
                    nc.vector.tensor_copy(dcol[v.buf(2)][:, :], dis[:, bass.ds(v.t, 1)]).then_inc(s_dcol, 1)

                def diagonal(v):
                    b = v.buf(2)
                    dve.wait_ge(s_dcol, v.t + 1)
                    wait_count(dve, s_ct, v.t - 1)
                    nc.vector.tensor_scalar(out=diag[b][:, :], in0=ident[:, :], scalar1=dcol[b][:, 0:1],
                                            scalar2=None, op0=MUL).then_inc(s_diag, 1)

                def residual(v):
                    b = v.buf(4)
                    dve.wait_ge(s_mm, v.t + 1)
                    dve.wait_ge(s_xb, v.t + 1)
                    wait_count(dve, x_out[b], 16 * v.uses(4))
                    wait_count(dve, s_h, v.t - 3)
                    nc.vector.tensor_tensor(out=x1[b][:, :], in0=ps_x[v.buf(2)][:, :], in1=xb[b][:, :], op=ADD)\
                        .then_inc(s_x1, 1)

                def moments(v):
                    dve.wait_ge(s_x1, v.t + 1)
                    norm.moments(dve, x1[v.buf(4)][:, :], v)

                def lo(v):
                    dve.wait_ge(s_hi, v.t + 1)
                    nc.vector.scalar_tensor_tensor(out=slot_lo(v.t), in0=ps_t[v.buf(2)][:, :], scalar=SCALE_LN,
                                                   in1=slot_hi(v.t), op0=MUL, op1=SUB).then_inc(s_lo, 1)
                pipeline(dve, NT, (0, degree), (3, residual), (0, diagonal), (3, moments), (7, lo),
                         (3, lambda v: norm.aggregate(dve, v)))

            @block.scalar
            def _(act):
                act.wait_ge(s_w, 48)

                def copy_c(v):
                    b = v.buf(2)
                    act.wait_ge(s_ct, v.t + 1)
                    wait_count(act, s_mm, v.t - 1)
                    nc.scalar.activation(cT[b][:, :], ps_c[b][:, 0:HID], ACT.Identity,
                                         bias=bias_c[:, 0:1]).then_inc(s_cT, 1)

                def normed(v):
                    act.wait_ge(norm.s_ready, v.t + 1)
                    wait_count(act, s_turn, v.t - 1)
                    norm.apply(h[v.buf(2)][:, :], x1[v.buf(4)][:, :], v).then_inc(s_h, 1)

                def hi(v):
                    act.wait_ge(s_turn, v.t + 1)
                    act.wait_ge(s_x1, v.t + 1)
                    nc.scalar.activation(slot_hi(v.t), ps_t[v.buf(2)][:, :], ACT.Copy,
                                         scale=SCALE_LN).then_inc(s_hi, 1)
                pipeline(act, NT, (1, copy_c), (6, hi), (5, normed))

            @block.tensor
            def _(pe):
                pe.wait_ge(s_w, 48)

                def convolve(v):
                    b = v.buf(2)
                    pe.wait_ge(s_diag, v.t + 1)
                    pe.wait_ge(g_in[v.buf(4)], 32 * (v.uses(4) + 1))
                    wait_count(pe, s_cT, v.t - 1)
                    nc.tensor.matmul(ps_c[b][:, 0:P], hw[v.buf(4)][:, :], diag[b][:, :], start=True, stop=False)
                    nc.tensor.matmul(ps_c[b][:, 0:P], gs[v.buf(4)][:, :], diag[b][:, :], start=False,
                                     stop=True).then_inc(s_ct, 1)

                def linear(v):
                    b = v.buf(2)
                    pe.wait_ge(s_cT, v.t + 1)
                    wait_count(pe, s_x1, v.t - 1)
                    nc.tensor.matmul(ps_x[b][:, :], cT[b][:, :], w[:, :], start=True, stop=True).then_inc(s_mm, 1)

                def turn(v):
                    b = v.buf(2)
                    pe.wait_ge(s_h, v.t + 1)
                    wait_count(pe, s_lo, v.t - 1)
                    transposes(pe, ps_t[b], h[b]).then_inc(s_turn, 1)
                pipeline(pe, NT, (1, convolve), (2, linear), (6, turn))

    def edge_products(phase, source, normed, scale, unit, ahead):
        with ExitStack() as ctx:
            w = sb(ctx, f"{phase}_w", [P, 2 * cols[unit]], F16)
            m = [sb(ctx, f"{phase}_m{b}", [P, D]) for b in range(4)]
            sl = [sb(ctx, f"{phase}_sel{b}", [P, 2 * P]) for b in range(4)]
            aT = [sb(ctx, f"{phase}_aT{b}", [P, 2 * D], F16) for b in range(2)]
            tot = [sb(ctx, f"{phase}_tot{b}", [P, D]) for b in range(4)]
            f = sb(ctx, f"{phase}_f", [P, 1])
            ps_c = ps(ctx, f"{phase}_ps_c")
            ps_a = [ps(ctx, f"{phase}_ps_a{b}") for b in range(2)]
            ps_g = [ps(ctx, f"{phase}_ps_g{b}") for b in range(2)]
            s_w, s_f, s_row, s_carry, s_carried, s_sum, s_hi, s_lo, s_mm, s_tot = sems(
                phase, "w f row carry carried sum hi lo mm tot")
            m_in, sel_in, t_out = pair(phase, "min", 4), pair(phase, "selin", 4), pair(phase, "tout", 4)
            s_ahead = sem(f"{phase}_ahead")
            norm = Norm(ctx, f"{phase}_norm") if normed else None
            block = ctx.enter_context(nc.Block())

            def rows_there(eng, v):
                if normed:
                    eng.wait_ge(s_row, v.t + 1)
                else:
                    eng.wait_ge(m_in[v.buf(4)], 16 * (v.uses(4) + 1))

            @block.sync
            def _(sp):
                def load(v):
                    b = v.buf(4)
                    wait_count(sp, s_sum, v.t - 3)
                    sp.dma_start(sl[b][:, :], sel_d[:, bass.ds(v.t * 2 * P, 2 * P)]).then_inc(sel_in[b], 16)
                load(Tile(0, 0))
                sp.dma_start(w[:, :], split_d[unit][:, :]).then_inc(s_w, 16)
                for t in range(1, ET):
                    load(Tile(0, t))
                for tile, rows_ahead in ahead:
                    sp.dma_start(tile, rows_ahead).then_inc(s_ahead, 16)
                sp.wait_ge(s_ahead, 16 * len(ahead))

            @block.gpsimd
            def _(pool):
                def gather(v):
                    b = v.buf(4)
                    wait_count(pool, s_sum, v.t - 3)
                    nc.gpsimd.indirect_dma_start(
                        m[b][:, :], None, source[0:N, :],
                        bass.IndirectOffsetOnAxis(ap=src_i[:, v.t:v.t + 1], axis=0)).then_inc(m_in[b], 16)

                def scatter(v):
                    b = v.buf(4)
                    pool.wait_ge(s_tot, v.t + 1)
                    nc.gpsimd.indirect_dma_start(
                        agg_d[:, :], bass.IndirectOffsetOnAxis(ap=put_i[:, v.t:v.t + 1], axis=0),
                        tot[b][:, :], None, bounds_check=N - 1, oob_is_err=False).then_inc(t_out[b], 16)
                if normed:
                    pipeline(pool, ET, (0, gather), (2, lambda v: norm.factors(pool, v, s_row)), (6, scatter),
                             peel=ET)
                else:
                    pipeline(pool, ET, (0, gather), (6, scatter), peel=ET)
                for b in range(4):
                    pool.wait_ge(t_out[b], 16 * (ET // 4))

            @block.vector
            def _(dve):
                nc.vector.tensor_scalar(out=f[:, :], in0=down[:, unit_no[unit]:unit_no[unit] + 1],
                                        scalar1=1.0 / scale, scalar2=None, op0=MUL).then_inc(s_f, 1)
                dve.wait_ge(s_f, 1)

                def moments(v):
                    dve.wait_ge(m_in[v.buf(4)], 16 * (v.uses(4) + 1))
                    norm.moments(dve, m[v.buf(4)][:, :], v)

                def carry(v):
                    if isinstance(v.t, int) and v.t == 0:
                        return
                    rows_there(dve, v)
                    dve.wait_ge(s_carry, v.t)
                    nc.vector.tensor_copy(m[v.buf(4)][0:1, :], ps_c[0:1, :]).then_inc(s_carried, 1)

                def lo(v):
                    b = v.buf(2)
                    dve.wait_ge(s_hi, v.t + 1)
                    nc.vector.scalar_tensor_tensor(out=aT[b][:, D:2 * D], in0=ps_a[b][:, :], scalar=scale,
                                                   in1=aT[b][:, 0:D], op0=MUL, op1=SUB).then_inc(s_lo, 1)

                def totals(v):
                    b = v.buf(4)
                    dve.wait_ge(s_mm, v.t + 1)
                    wait_count(dve, t_out[b], 16 * v.uses(4))
                    nc.vector.tensor_scalar(out=tot[b][:, :], in0=ps_g[v.buf(2)][:, :], scalar1=f[:, 0:1],
                                            scalar2=None, op0=MUL).then_inc(s_tot, 1)
                if normed:
                    pipeline(dve, ET, (1, carry), (0, moments), (0, lambda v: norm.aggregate(dve, v)), (1, lo),
                             (3, totals), peel=8)
                else:
                    pipeline(dve, ET, (1, carry), (1, lo), (3, totals), peel=8)

            @block.scalar
            def _(act):
                def normed_rows(v):
                    act.wait_ge(norm.s_ready, v.t + 1)
                    b = v.buf(4)
                    norm.apply(m[b][:, :], m[b][:, :], v).then_inc(s_row, 1)

                def hi(v):
                    b = v.buf(2)
                    act.wait_ge(s_sum, v.t + 1)
                    wait_count(act, s_mm, v.t - 1)
                    nc.scalar.activation(aT[b][:, 0:D], ps_a[b][:, :], ACT.Copy, scale=scale).then_inc(s_hi, 1)
                if normed:
                    pipeline(act, ET, (1, hi), (0, normed_rows), peel=8)
                else:
                    pipeline(act, ET, (1, hi), peel=8)

            @block.tensor
            def _(pe):
                def sums(v):
                    b = v.buf(4)
                    pe.wait_ge(sel_in[b], 16 * (v.uses(4) + 1))
                    rows_there(pe, v)
                    wait_count(pe, s_carried, v.t)
                    nc.tensor.matmul(ps_c[0:1, :], sl[b][:, P - 1:P], m[b][:, :], start=True,
                                     stop=True).then_inc(s_carry, 1)
                    a = v.buf(2)
                    wait_count(pe, s_lo, v.t - 1)
                    for c in range(C):
                        ins = nc.tensor.matmul(ps_a[a][:, c * P:(c + 1) * P], m[b][:, c * P:(c + 1) * P],
                                               sl[b][:, P:2 * P], start=True, stop=True)
                    ins.then_inc(s_sum, 1)

                def project(v):
                    b = v.buf(2)
                    if isinstance(v.t, int) and v.t == 0:
                        pe.wait_ge(s_w, 16)
                    pe.wait_ge(s_lo, v.t + 1)
                    wait_count(pe, s_tot, v.t - 1)
                    product(pe, ps_g[b][:, :], lambda c: aT[b][:, c * P:(c + 1) * P],
                            lambda c: aT[b][:, D + c * P:D + (c + 1) * P], w, D).then_inc(s_mm, 1)
                pipeline(pe, ET, (1, sums), (2, project), peel=8)

    def sage_layer(l, w, bias):
        final = l == 2
        phase = f"s{l}"
        scale_in = SCALE_LN if l == 0 else SCALE_UNIT
        scale_out = SCALE_LN if final else SCALE_UNIT
        unit = f"self{l}"
        with ExitStack() as ctx:
            g = [sb(ctx, f"{phase}_g{b}", [P, D]) for b in range(4)]
            junk = sb(ctx, f"{phase}_junk", [P, D])
            h = [sb(ctx, f"{phase}_h{b}", [P, D]) for b in range(4)]
            en = [sb(ctx, f"{phase}_en{b}", [P, 1]) for b in range(2)]
            em = [sb(ctx, f"{phase}_em{b}", [P, 1]) for b in range(2)]
            rn = [sb(ctx, f"{phase}_rn{b}", [P, 1]) for b in range(2)]
            f = sb(ctx, f"{phase}_f", [P, 1])
            if final:
                x1 = [sb(ctx, f"{phase}_x1{b}", [P, D]) for b in range(4)]
                h3 = [sb(ctx, f"{phase}_h3{b}", [P, D]) for b in range(2)]
            ps_z = [ps(ctx, f"{phase}_ps_z{b}") for b in range(4)]
            ps_t = [ps(ctx, f"{phase}_ps_t{b}") for b in range(2)]
            s_f, s_mm, s_bias, s_r, s_en, s_em, s_rn, s_h, s_turn, s_hi, s_lo, s_x2, s_h3 = sems(
                phase, "f mm bias r en em rn h turn hi lo x2 h3")
            g_in, h_out = pair(phase, "gin", 4), pair(phase, "hout", 4)
            x_in = pair(phase, "xin", 4) if final else None
            norm = Norm(ctx, f"{phase}_norm") if final else None
            turned, nturned = (h3, 2) if final else (h, 4)
            s_turned = s_h3 if final else s_h
            block = ctx.enter_context(nc.Block())

            @block.sync
            def _(sp):
                def load(v):
                    b = v.buf(4)
                    wait_count(sp, s_h, v.t - 3)
                    sp.dma_start(g[b][0:rows_of(v.t), :], rows(agg_d, v.t)).then_inc(g_in[b], 16)

                def load_x(v):
                    b = v.buf(4)
                    stores, normed = 16 * v.uses(4), v.t - 3
                    wait_count(sp, h_out[b], stores)
                    wait_count(sp, s_h3, normed)
                    sp.dma_start(x1[b][0:rows_of(v.t), :], rows(x1_d, v.t)).then_inc(x_in[b], 16)

                def store(v):
                    b = v.buf(4)
                    if final:
                        sp.wait_ge(s_x2, v.t + 1)
                        sp.dma_start(rows(x2_d, v.t), x1[b][0:rows_of(v.t), :]).then_inc(h_out[b], 16)
                    else:
                        sp.wait_ge(s_h, v.t + 1)
                        sp.dma_start(rows(h_d, v.t), h[b][0:rows_of(v.t), :]).then_inc(h_out[b], 16)
                if final:
                    pipeline(sp, NT, (0, load), (4, store), (1, load_x))
                else:
                    pipeline(sp, NT, (0, load), (4, store))
                for b in range(4):
                    sp.wait_ge(h_out[b], 16 * ((NT + 3 - b) // 4))

            @block.gpsimd
            def _(pool):
                def add_bias(v):
                    b = v.buf(4)
                    pool.wait_ge(g_in[b], 16 * (v.uses(4) + 1))
                    nc.gpsimd.tensor_tensor(out=g[b][:, :], in0=g[b][:, :], in1=bias[:, :], op=ADD)\
                        .then_inc(s_bias, 1)

                def factor(v):
                    b = v.buf(2)
                    pool.wait_ge(s_em, v.t + 1)
                    wait_count(pool, s_h, v.t - 1)
                    nc.gpsimd.tensor_tensor(out=rn[b][:, :], in0=em[b][:, :], in1=minus_half[:, :],
                                            op=POW).then_inc(s_rn, 1)
                if final:
                    pipeline(pool, NT, (0, add_bias), (2, factor), (3, lambda v: norm.factors(pool, v, s_h3)))
                else:
                    pipeline(pool, NT, (0, add_bias), (2, factor))

            @block.vector
            def _(dve):
                nc.vector.tensor_scalar(out=f[:, :], in0=down[:, unit_no[unit]:unit_no[unit] + 1],
                                        scalar1=1.0 / scale_in, scalar2=None, op0=MUL).then_inc(s_f, 1)
                dve.wait_ge(s_f, 1)

                def z_sum(v):
                    b = v.buf(4)
                    dve.wait_ge(s_mm, v.t + 1)
                    dve.wait_ge(s_bias, v.t + 1)
                    nc.vector.scalar_tensor_tensor(out=g[b][:, :], in0=ps_z[b][:, :], scalar=f[:, 0:1],
                                                   in1=g[b][:, :], op0=MUL, op1=ADD).then_inc(s_r, 1)

                def length(v):
                    r, e = g[v.buf(4)], v.buf(2)
                    dve.wait_ge(s_r, v.t + 1)
                    wait_count(dve, s_em, v.t)
                    nc.vector.scalar_tensor_tensor(out=junk[:, :], in0=r[:, :], scalar=0.0, in1=r[:, :],
                                                   op0=MAX, op1=MUL, accum_out=en[e][:, 0:1]).then_inc(s_en, 1)

                def clamp(v):
                    e = v.buf(2)
                    dve.wait_ge(s_en, v.t + 1)
                    wait_count(dve, s_rn, v.t - 1)
                    nc.vector.tensor_scalar(out=em[e][:, :], in0=en[e][:, :], scalar1=NORM_EPS * NORM_EPS,
                                            scalar2=None, op0=MAX).then_inc(s_em, 1)

                def lo(v):
                    dve.wait_ge(s_hi, v.t + 1)
                    nc.vector.scalar_tensor_tensor(out=slot_lo(v.t), in0=ps_t[v.buf(2)][:, :], scalar=scale_out,
                                                   in1=slot_hi(v.t), op0=MUL, op1=SUB).then_inc(s_lo, 1)

                def residual(v):
                    b = v.buf(4)
                    dve.wait_ge(s_h, v.t + 1)
                    dve.wait_ge(x_in[b], 16 * (v.uses(4) + 1))
                    nc.vector.tensor_tensor(out=x1[b][:, :], in0=x1[b][:, :], in1=h[b][:, :], op=ADD)\
                        .then_inc(s_x2, 1)

                def stats(v):
                    dve.wait_ge(s_x2, v.t + 1)
                    norm.moments(dve, x1[v.buf(4)][:, :], v)
                if final:
                    pipeline(dve, NT, (0, z_sum), (2, residual), (0, length), (2, stats), (0, clamp), (5, lo),
                             (2, lambda v: norm.aggregate(dve, v)))
                else:
                    pipeline(dve, NT, (0, z_sum), (0, length), (0, clamp), (3, lo))

            @block.scalar
            def _(act):
                def hi(v):
                    act.wait_ge(s_turn, v.t + 1)
                    nc.scalar.activation(slot_hi(v.t), ps_t[v.buf(2)][:, :], ACT.Copy,
                                         scale=scale_out).then_inc(s_hi, 1)

                def normed(v):
                    b = v.buf(2)
                    act.wait_ge(norm.s_ready, v.t + 1)
                    wait_count(act, s_turn, v.t - 1)
                    norm.apply(h3[b][:, :], x1[v.buf(4)][:, :], v).then_inc(s_h3, 1)

                def unit_rows(v):
                    b = v.buf(4)
                    act.wait_ge(s_rn, v.t + 1)
                    if final:
                        wait_count(act, s_x2, v.t - 3)
                    else:
                        wait_count(act, s_turn, v.t - 3)
                        wait_count(act, h_out[b], 16 * v.uses(4))
                    nc.scalar.activation(h[b][:, :], g[b][:, :], ACT.Relu,
                                         scale=rn[v.buf(2)][:, 0:1]).then_inc(s_h, 1)
                if final:
                    pipeline(act, NT, (5, hi), (3, normed), (1, unit_rows))
                else:
                    pipeline(act, NT, (3, hi), (1, unit_rows))

            @block.tensor
            def _(pe):
                def project(v):
                    wait_count(pe, s_r, v.t - 3)
                    product(pe, ps_z[v.buf(4)][:, :], lambda c: slots16[:, bass.ds(v.t * 2 * D + c * P, P)],
                            lambda c: slots16[:, bass.ds(v.t * 2 * D + D + c * P, P)], w, D).then_inc(s_mm, 1)

                def turn(v):
                    pe.wait_ge(s_turned, v.t + 1)
                    wait_count(pe, s_lo, v.t - 1)
                    transposes(pe, ps_t[v.buf(2)], turned[v.buf(nturned)]).then_inc(s_turn, 1)
                pipeline(pe, NT, (0, project), (4 if final else 2, turn))

    class Mish:

        def __init__(self, ctx, name):
            self.c = [sb(ctx, f"{name}_c{b}", [P, D]) for b in range(2)]
            self.e = sb(ctx, f"{name}_e", [P, D])
            self.s_c, self.s_e, self.s_w, self.s_l, self.s_q, self.s_rw, self.s_u = sems(
                name, "c e w l q rw u")

        def cap(self, dve, r, v, freed, count):
            wait_count(dve, freed, count)
            nc.vector.tensor_scalar(out=self.c[v.buf(2)][:, :], in0=r, scalar1=MISH_CAP, scalar2=None,
                                    op0=MIN).then_inc(self.s_c, 1)

        def exp(self, act, v):
            b = v.buf(2)
            act.wait_ge(self.s_c, v.t + 1)
            nc.scalar.activation(self.e[:, :], self.c[b][:, :], ACT.Exp).then_inc(self.s_e, 1)

        def poly(self, dve, v):
            b = v.buf(2)
            dve.wait_ge(self.s_e, v.t + 1)
            nc.vector.scalar_tensor_tensor(out=self.c[b][:, :], in0=self.e[:, :], scalar=2.0,
                                           in1=self.e[:, :], op0=ADD, op1=MUL).then_inc(self.s_w, 1)

        def inverse(self, act, v):
            b = v.buf(2)
            act.wait_ge(self.s_w, v.t + 1)
            nc.scalar.activation(self.e[:, :], self.c[b][:, :], ACT.Ln,
                                 bias=two_col[:, 0:1]).then_inc(self.s_l, 1)
            act.wait_ge(self.s_l, v.t + 1)
            nc.scalar.activation(self.e[:, :], self.e[:, :], ACT.Exp, scale=-1.0).then_inc(self.s_q, 1)

        def times(self, pool, r, v):
            b = v.buf(2)
            pool.wait_ge(self.s_w, v.t + 1)
            nc.gpsimd.tensor_tensor(out=r, in0=r, in1=self.c[b][:, :], op=MUL)\
                .then_inc(self.s_rw, 1)

        def result(self, dve, r, v):
            b = v.buf(2)
            dve.wait_ge(self.s_q, v.t + 1)
            dve.wait_ge(self.s_rw, v.t + 1)
            nc.vector.tensor_tensor(out=self.c[b][:, :], in0=r, in1=self.e[:, :],
                                    op=MUL).then_inc(self.s_u, 1)

    def edge_hidden():
        with ExitStack() as ctx:
            w1 = sb(ctx, "e_w1", [P, 2 * cols["edge"]], F16)
            w1c = sb(ctx, "e_w1c", [ED, D])
            bias1 = sb(ctx, "e_bias1", [P, D])
            m = [[sb(ctx, f"e_m{s}{b}", [P, D]) for b in range(2)] for s in range(2)]
            hT = [[sb(ctx, f"e_hT{s}{b}", [P, 2 * D], F16) for b in range(2)] for s in range(2)]
            ea = [sb(ctx, f"e_ea{b}", [P, ED]) for b in range(2)]
            eaT = sb(ctx, "e_eaT", [ED, P])
            r = sb(ctx, "e_r", [P, D])
            mT = sb(ctx, "e_mT", [P, D])
            f = sb(ctx, "e_f", [P, 1])
            ps_t = [ps(ctx, f"e_ps_t{s}") for s in range(2)]
            ps_e, ps_m = ps(ctx, "e_ps_e"), ps(ctx, "e_ps_m")
            ps_1 = [ps(ctx, f"e_ps_1{b}") for b in range(2)]
            s_w, s_f, s_wc, s_et, s_eT, s_mm, s_r, s_mt, s_mT = sems("e", "w f wc et eT mm r mt mT")
            s_row, s_turn, s_hi, s_lo = pair("e", "row"), pair("e", "turn"), pair("e", "hi"), pair("e", "lo")
            m_in, ea_in = [pair("e", f"min{s}") for s in range(2)], pair("e", "ein")
            s_out = sem("e_out")
            norms = [Norm(ctx, f"e_norm{s}", 2) for s in range(2)]
            mish = Mish(ctx, "e_mish")
            u_edge = unit_no["edge"]
            block = ctx.enter_context(nc.Block())

            @block.sync
            def _(sp):
                sp.dma_start(w1c[:, :], W1[2 * D:2 * D + ED, :]).then_inc(s_w, 16)
                sp.dma_start(w1[:, :], split_d["edge"][:, :]).then_inc(s_w, 16)
                sp.dma_start(bias1[:, :], wide(b1)).then_inc(s_w, 16)

                def store(v):
                    sp.wait_ge(s_mT, v.t + 1)
                    sp.dma_start(hid_d[:, bass.ds(v.t * D, D)], mT[:, :]).then_inc(s_out, 16)
                pipeline(sp, ET, (0, store), peel=8)
                sp.wait_ge(s_out, 16 * ET)

            @block.gpsimd
            def _(pool):
                def gather(v):
                    b = v.buf(2)
                    for s, idx in enumerate((src_i, dst_i)):
                        wait_count(pool, s_turn[s], v.t - 1)
                        nc.gpsimd.indirect_dma_start(
                            m[s][b][:, :], None, x2_d[0:N, :],
                            bass.IndirectOffsetOnAxis(ap=idx[:, v.t:v.t + 1], axis=0)).then_inc(m_in[s][b], 16)
                    wait_count(pool, s_et, v.t - 1)
                    nc.gpsimd.indirect_dma_start(
                        ea[b][:, :], None, edge_attr[:, :],
                        bass.IndirectOffsetOnAxis(ap=edge_i[:, v.t:v.t + 1], axis=0)).then_inc(ea_in[b], 16)
                pipeline(pool, ET, (0, gather), (4, lambda v: mish.times(pool, r[:, :], v)),
                         (1, lambda v: norms[0].factors(pool, v, s_row[0])),
                         (1, lambda v: norms[1].factors(pool, v, s_row[1])), peel=ET)

            @block.vector
            def _(dve):
                dve.wait_ge(s_w, 48)
                nc.vector.tensor_scalar(out=f[:, :], in0=down[:, u_edge:u_edge + 1], scalar1=1.0 / SCALE_LN,
                                        scalar2=None, op0=MUL).then_inc(s_f, 1)
                nc.vector.tensor_scalar(out=w1c[:, :], in0=w1c[:, :], scalar1=up[0:ED, u_edge:u_edge + 1],
                                        scalar2=SCALE_LN, op0=MUL, op1=MUL).then_inc(s_wc, 1)
                dve.wait_ge(s_f, 1)

                def moments(v):
                    for s in range(2):
                        dve.wait_ge(m_in[s][v.buf(2)], 16 * (v.uses(2) + 1))
                        norms[s].moments(dve, m[s][v.buf(2)][:, :], v)
                    for s in range(2):
                        norms[s].aggregate(dve, v)

                def split(v):
                    b = v.buf(2)
                    for s in range(2):
                        dve.wait_ge(s_hi[s], v.t + 1)
                        nc.vector.scalar_tensor_tensor(out=hT[s][b][:, D:2 * D], in0=ps_t[s][:, :],
                                                       scalar=SCALE_LN, in1=hT[s][b][:, 0:D], op0=MUL,
                                                       op1=SUB).then_inc(s_lo[s], 1)

                def attributes(v):
                    dve.wait_ge(s_et, v.t + 1)
                    wait_count(dve, s_mm, v.t)
                    nc.vector.tensor_copy(eaT[:, :], ps_e[0:ED, 0:P]).then_inc(s_eT, 1)

                def z_sum(v):
                    dve.wait_ge(s_mm, v.t + 1)
                    wait_count(dve, mish.s_u, v.t)
                    nc.vector.scalar_tensor_tensor(out=r[:, :], in0=ps_1[v.buf(2)][:, :], scalar=f[:, 0:1],
                                                   in1=bias1[:, :], op0=MUL, op1=ADD).then_inc(s_r, 1)

                def cap(v):
                    dve.wait_ge(s_r, v.t + 1)
                    mish.cap(dve, r[:, :], v, s_mt, v.t - 1)
                pipeline(dve, ET, (3, z_sum), (3, cap), (1, split), (3, lambda v: mish.poly(dve, v)),
                         (0, moments), (3, lambda v: mish.result(dve, r[:, :], v)), (1, attributes), peel=8)

            @block.scalar
            def _(act):
                def normed(v):
                    b = v.buf(2)
                    for s in range(2):
                        act.wait_ge(norms[s].s_ready, v.t + 1)
                        norms[s].apply(m[s][b][:, :], m[s][b][:, :], v).then_inc(s_row[s], 1)

                def hi(v):
                    for s in range(2):
                        act.wait_ge(s_turn[s], v.t + 1)
                        wait_count(act, s_mm, v.t - 1)
                        nc.scalar.activation(hT[s][v.buf(2)][:, 0:D], ps_t[s][:, :], ACT.Copy, scale=SCALE_LN)\
                            .then_inc(s_hi[s], 1)

                def copy_m(v):
                    act.wait_ge(s_mt, v.t + 1)
                    wait_count(act, s_out, 16 * v.t)
                    nc.scalar.activation(mT[:, :], ps_m[:, :], ACT.Copy).then_inc(s_mT, 1)
                pipeline(act, ET, (3, lambda v: mish.exp(act, v)), (1, hi), (3, lambda v: mish.inverse(act, v)),
                         (0, normed), (4, copy_m), peel=8)

            @block.tensor
            def _(pe):
                pe.wait_ge(s_w, 48)
                pe.wait_ge(s_wc, 1)

                def turn(v):
                    b = v.buf(2)
                    for s in range(2):
                        pe.wait_ge(s_row[s], v.t + 1)
                        wait_count(pe, s_lo[s], v.t)
                        transposes(pe, ps_t[s], m[s][b]).then_inc(s_turn[s], 1)
                    pe.wait_ge(ea_in[b], 16 * (v.uses(2) + 1))
                    wait_count(pe, s_eT, v.t)
                    nc.tensor.matmul(ps_e[0:ED, 0:P], ea[b][:, :], ident[:, :], start=True, stop=True)\
                        .then_inc(s_et, 1)

                def hidden(v):
                    b = v.buf(2)
                    pe.wait_ge(s_lo[0], v.t + 1)
                    pe.wait_ge(s_lo[1], v.t + 1)
                    pe.wait_ge(s_eT, v.t + 1)
                    wait_count(pe, s_r, v.t - 1)
                    nc.tensor.matmul(ps_1[b][:, :], eaT[:, :], w1c[:, :], start=True, stop=False)
                    product(pe, ps_1[b][:, :], lambda c: hT[c // C][b][:, (c % C) * P:(c % C + 1) * P],
                            lambda c: hT[c // C][b][:, D + (c % C) * P:D + (c % C + 1) * P], w1, D,
                            nchunks=2 * C, first=False).then_inc(s_mm, 1)

                def turn_m(v):
                    pe.wait_ge(mish.s_u, v.t + 1)
                    wait_count(pe, s_mT, v.t)
                    transposes(pe, ps_m, mish.c[v.buf(2)]).then_inc(s_mt, 1)
                pipeline(pe, ET, (1, turn), (2, hidden), (4, turn_m), peel=8)

    def edge_messages():
        with ExitStack() as ctx:
            w2 = sb(ctx, "n_w2", [P, C * D])
            w3 = sb(ctx, "n_w3", [P, C * D])
            bias2 = sb(ctx, "n_bias2", [P, D])
            mT = [sb(ctx, f"n_mT{b}", [P, D]) for b in range(2)]
            sl = [sb(ctx, f"n_sel{b}", [P, 2 * P]) for b in range(2)]
            r = sb(ctx, "n_r", [P, D])
            aT = [sb(ctx, f"n_aT{b}", [P, D]) for b in range(2)]
            tot = [sb(ctx, f"n_tot{b}", [P, D]) for b in range(2)]
            ps_2 = [ps(ctx, f"n_ps_2{b}") for b in range(2)]
            ps_c = ps(ctx, "n_ps_c")
            ps_a = [ps(ctx, f"n_ps_a{b}") for b in range(2)]
            ps_g = [ps(ctx, f"n_ps_g{b}") for b in range(2)]
            s_w, s_mm, s_r, s_carry, s_carried, s_sum, s_aT, s_mm3, s_tot = sems(
                "n", "w mm r carry carried sum aT mm3 tot")
            m_in, sel_in, t_out = pair("n", "min"), pair("n", "selin"), pair("n", "tout")
            mish = Mish(ctx, "n_mish")
            block = ctx.enter_context(nc.Block())

            @block.sync
            def _(sp):
                sp.dma_start(w2[:, :].rearrange("p (c n) -> p c n", c=C),
                             W2.rearrange("(c p) n -> p c n", p=P)).then_inc(s_w, 16)
                sp.dma_start(bias2[:, :], wide(b2)).then_inc(s_w, 16)
                sp.dma_start(w3[:, :].rearrange("p (c n) -> p c n", c=C),
                             W3[D:2 * D, :].rearrange("(c p) n -> p c n", p=P)).then_inc(s_w, 16)

                def load(v):
                    b = v.buf(2)
                    wait_count(sp, s_mm, v.t - 1)
                    sp.dma_start(mT[b][:, :], hid_d[:, bass.ds(v.t * D, D)]).then_inc(m_in[b], 16)

                def load_sel(v):
                    b = v.buf(2)
                    wait_count(sp, s_sum, v.t - 1)
                    sp.dma_start(sl[b][:, :], sel_d[:, bass.ds(v.t * 2 * P, 2 * P)]).then_inc(sel_in[b], 16)
                pipeline(sp, ET, (0, load), (1, load_sel), peel=8)

            @block.gpsimd
            def _(pool):
                def scatter(v):
                    b = v.buf(2)
                    pool.wait_ge(s_tot, v.t + 1)
                    nc.gpsimd.indirect_dma_start(
                        agg_d[:, :], bass.IndirectOffsetOnAxis(ap=put_i[:, v.t:v.t + 1], axis=0),
                        tot[b][:, :], None, bounds_check=N - 1, oob_is_err=False).then_inc(t_out[b], 16)
                pipeline(pool, ET, (0, lambda v: mish.times(pool, r[:, :], v)), (4, scatter), peel=ET)
                for b in range(2):
                    pool.wait_ge(t_out[b], 16 * (ET // 2))

            @block.vector
            def _(dve):
                dve.wait_ge(s_w, 48)

                def z_sum(v):
                    dve.wait_ge(s_mm, v.t + 1)
                    wait_count(dve, mish.s_u, v.t)
                    nc.vector.tensor_tensor(out=r[:, :], in0=ps_2[v.buf(2)][:, :], in1=bias2[:, :], op=ADD)\
                        .then_inc(s_r, 1)

                def cap(v):
                    dve.wait_ge(s_r, v.t + 1)
                    mish.cap(dve, r[:, :], v, s_sum, v.t - 1)

                def carry(v):
                    if isinstance(v.t, int) and v.t == 0:
                        return
                    dve.wait_ge(mish.s_u, v.t + 1)
                    dve.wait_ge(s_carry, v.t)
                    nc.vector.tensor_copy(mish.c[v.buf(2)][0:1, :], ps_c[0:1, :]).then_inc(s_carried, 1)

                def totals(v):
                    b = v.buf(2)
                    dve.wait_ge(s_mm3, v.t + 1)
                    wait_count(dve, t_out[b], 16 * v.uses(2))
                    nc.vector.tensor_copy(tot[b][:, :], ps_g[b][:, :]).then_inc(s_tot, 1)
                pipeline(dve, ET, (0, z_sum), (0, cap), (0, lambda v: mish.poly(dve, v)), (3, totals),
                         (0, lambda v: mish.result(dve, r[:, :], v)), (0, carry), peel=8)

            @block.scalar
            def _(act):
                def copy_sums(v):
                    b = v.buf(2)
                    act.wait_ge(s_sum, v.t + 1)
                    wait_count(act, s_mm3, v.t - 1)
                    nc.scalar.activation(aT[b][:, :], ps_a[b][:, :], ACT.Copy).then_inc(s_aT, 1)
                pipeline(act, ET, (0, lambda v: mish.exp(act, v)), (0, lambda v: mish.inverse(act, v)),
                         (1, copy_sums), peel=8)

            @block.tensor
            def _(pe):
                pe.wait_ge(s_w, 48)

                def float_product(out, a, w):
                    for c in range(C):
                        ins = nc.tensor.matmul(out[:, :], a[:, c * P:(c + 1) * P], w[:, c * D:(c + 1) * D],
                                               start=c == 0, stop=c == C - 1)
                    return ins

                def message(v):
                    b = v.buf(2)
                    pe.wait_ge(m_in[b], 16 * (v.uses(2) + 1))
                    wait_count(pe, s_r, v.t - 1)
                    float_product(ps_2[b], mT[b], w2).then_inc(s_mm, 1)

                def sums(v):
                    b = v.buf(2)
                    pe.wait_ge(sel_in[b], 16 * (v.uses(2) + 1))
                    pe.wait_ge(mish.s_u, v.t + 1)
                    wait_count(pe, s_carried, v.t)
                    nc.tensor.matmul(ps_c[0:1, :], sl[b][:, P - 1:P], mish.c[b][:, :], start=True,
                                     stop=True).then_inc(s_carry, 1)
                    wait_count(pe, s_aT, v.t - 1)
                    for c in range(C):
                        ins = nc.tensor.matmul(ps_a[b][:, c * P:(c + 1) * P], mish.c[b][:, c * P:(c + 1) * P],
                                               sl[b][:, 0:P], start=True, stop=True)
                    ins.then_inc(s_sum, 1)

                def project(v):
                    b = v.buf(2)
                    pe.wait_ge(s_aT, v.t + 1)
                    wait_count(pe, s_tot, v.t - 1)
                    float_product(ps_g[b], aT[b], w3).then_inc(s_mm3, 1)
                pipeline(pe, ET, (0, message), (2, project), (1, sums), peel=8)

    def node_update():
        with ExitStack() as ctx:
            w3 = sb(ctx, "u_w3", [P, 2 * cols["update"]], F16)
            w4 = sb(ctx, "u_w4", [P, C * D])
            bias3, gam, bet = (sb(ctx, f"u_{n}", [P, D]) for n in ("bias3", "gam", "bet"))
            b4_rows = sb(ctx, "u_b4_rows", [3, D], BF16)
            ones3 = sb(ctx, "u_ones3", [3, P], BF16)
            g = [sb(ctx, f"u_g{b}", [P, D]) for b in range(2)]
            x2 = [sb(ctx, f"u_x2{b}", [P, D]) for b in range(4)]
            uT, yn, h4 = (sb(ctx, f"u_{n}", [P, D]) for n in ("uT", "yn", "h4"))
            b4_row = x2[0][0:1, :]
            b4_part = [x2[m + 1][0:1, 0:D // 2].bitcast(BF16) for m in range(3)]
            f = sb(ctx, "u_f", [P, 1])
            ps_z = [ps(ctx, f"u_ps_z{b}") for b in range(2)]
            ps_u = ps(ctx, "u_ps_u")
            ps_o = [ps(ctx, f"u_ps_o{b}") for b in range(2)]
            ps_t = [ps(ctx, f"u_ps_t{b}") for b in range(2)]
            (s_w, s_f, s_b4, s_ones, s_mm, s_bias, s_r, s_ut, s_uT, s_mm4, s_yn, s_xb, s_yg, s_x3,
             s_h4, s_turn, s_hi, s_lo) = sems(
                "u", "w f b4 ones mm bias r ut uT mm4 yn xb yg x3 h4 turn hi lo")
            g_in, x_in, x_out = pair("u", "gin"), pair("u", "xin", 4), pair("u", "xout", 4)
            normy, norm3 = Norm(ctx, "u_ny", 2), Norm(ctx, "u_n3", 2)
            mish = Mish(ctx, "u_mish")
            u_no = unit_no["update"]
            block = ctx.enter_context(nc.Block())

            @block.sync
            def _(sp):
                sp.dma_start(b4_row, b4.rearrange("(o d) -> o d", o=1)).then_inc(s_b4, 16)
                sp.dma_start(w3[:, :], split_d["update"][:, :]).then_inc(s_w, 16)
                sp.dma_start(w4[:, :].rearrange("p (c n) -> p c n", c=C),
                             W4.rearrange("(c p) n -> p c n", p=P)).then_inc(s_w, 16)
                for tile, vec in ((bias3, b3), (gam, gamma2), (bet, beta2)):
                    sp.dma_start(tile[:, :], wide(vec)).then_inc(s_w, 16)
                sp.wait_ge(s_f, 6)
                for m in range(3):
                    sp.dma_start(b4_rows[m:m + 1, :], b4_part[m]).then_inc(s_w, 16)

                def load(v):
                    b = v.buf(2)
                    wait_count(sp, mish.s_u, v.t - 1)
                    sp.dma_start(g[b][0:rows_of(v.t), :], rows(agg_d, v.t)).then_inc(g_in[b], 16)

                def load_x(v):
                    b = v.buf(4)
                    wait_count(sp, x_out[b], 16 * v.uses(4))
                    sp.dma_start(x2[b][0:rows_of(v.t), :], rows(x2_d, v.t)).then_inc(x_in[b], 16)

                sp.wait_ge(s_w, 128)
                pipeline(sp, NT, (0, load), (1, load_x))

            @block.gpsimd
            def _(pool):
                nc.gpsimd.memset(ones3[:, :], 1.0).then_inc(s_ones, 1)
                pool.wait_ge(s_w, 128)

                def add_bias(v):
                    b = v.buf(2)
                    pool.wait_ge(g_in[b], 16 * (v.uses(2) + 1))
                    nc.gpsimd.tensor_tensor(out=g[b][:, :], in0=g[b][:, :], in1=bias3[:, :], op=ADD)\
                        .then_inc(s_bias, 1)

                def add_beta(v):
                    b = v.buf(4)
                    pool.wait_ge(x_in[b], 16 * (v.uses(4) + 1))
                    nc.gpsimd.tensor_tensor(out=x2[b][:, :], in0=x2[b][:, :], in1=bet[:, :], op=ADD)\
                        .then_inc(s_xb, 1)

                def times_gamma(v):
                    pool.wait_ge(s_yn, v.t + 1)
                    nc.gpsimd.tensor_tensor(out=yn[:, :], in0=yn[:, :], in1=gam[:, :], op=MUL)\
                        .then_inc(s_yg, 1)
                pipeline(pool, NT, (0, add_bias), (3, lambda v: normy.factors(pool, v, s_yn)),
                         (4, lambda v: norm3.factors(pool, v, s_h4)), (3, add_beta), (3, times_gamma),
                         (0, lambda v: mish.times(pool, g[v.buf(2)][:, :], v)))

            @block.vector
            def _(dve):
                nc.vector.tensor_scalar(out=f[:, :], in0=down[:, u_no:u_no + 1], scalar1=1.0 / SCALE_LN,
                                        scalar2=None, op0=MUL).then_inc(s_f, 1)
                dve.wait_ge(s_b4, 16)
                for m in range(3):
                    if m:
                        nc.vector.tensor_tensor(out=b4_row, in0=b4_row, in1=b4_part[m - 1], op=SUB).then_inc(s_f, 1)
                        dve.wait_ge(s_f, 2 * m + 1)
                    nc.vector.tensor_copy(b4_part[m], b4_row).then_inc(s_f, 1)
                    dve.wait_ge(s_f, 2 * m + 2)

                def z_sum(v):
                    b = v.buf(2)
                    dve.wait_ge(s_mm, v.t + 1)
                    dve.wait_ge(s_bias, v.t + 1)
                    nc.vector.scalar_tensor_tensor(out=g[b][:, :], in0=ps_z[b][:, :], scalar=f[:, 0:1],
                                                   in1=g[b][:, :], op0=MUL, op1=ADD).then_inc(s_r, 1)

                def cap(v):
                    dve.wait_ge(s_r, v.t + 1)
                    mish.cap(dve, g[v.buf(2)][:, :], v, s_ut, v.t - 1)

                def y_stats(v):
                    dve.wait_ge(s_mm4, v.t + 1)
                    normy.moments(dve, ps_o[v.buf(2)][:, :], v)

                def residual(v):
                    b = v.buf(4)
                    dve.wait_ge(s_yg, v.t + 1)
                    dve.wait_ge(s_xb, v.t + 1)
                    nc.vector.tensor_tensor(out=x2[b][:, :], in0=x2[b][:, :], in1=yn[:, :], op=ADD)\
                        .then_inc(s_x3, 1)

                def x3_stats(v):
                    dve.wait_ge(s_x3, v.t + 1)
                    norm3.moments(dve, x2[v.buf(4)][:, :], v)

                def lo(v):
                    dve.wait_ge(s_hi, v.t + 1)
                    nc.vector.scalar_tensor_tensor(out=slot_lo(v.t), in0=ps_t[v.buf(2)][:, :], scalar=SCALE_LN,
                                                   in1=slot_hi(v.t), op0=MUL, op1=SUB).then_inc(s_lo, 1)
                pipeline(dve, NT, (0, z_sum), (0, cap), (5, lo), (0, lambda v: mish.poly(dve, v)), (2, y_stats),
                         (3, residual), (2, lambda v: normy.aggregate(dve, v)), (3, x3_stats),
                         (0, lambda v: mish.result(dve, g[v.buf(2)][:, :], v)),
                         (3, lambda v: norm3.aggregate(dve, v)))

            @block.scalar
            def _(act):
                def u_parts(v):
                    act.wait_ge(s_ut, v.t + 1)
                    wait_count(act, s_mm4, v.t)
                    nc.scalar.activation(uT[:, :], ps_u[:, :], ACT.Copy).then_inc(s_uT, 1)

                def y_normed(v):
                    b = v.buf(2)
                    act.wait_ge(normy.s_ready, v.t + 1)
                    wait_count(act, s_x3, v.t)
                    normy.apply(yn[:, :], ps_o[b][:, :], v, ACT.Identity).then_inc(s_yn, 1)

                def next_rows(v):
                    b = v.buf(2)
                    act.wait_ge(norm3.s_ready, v.t + 1)
                    wait_count(act, s_turn, v.t)
                    norm3.apply(h4[:, :], x2[v.buf(4)][:, :], v).then_inc(s_h4, 1)

                def hi(v):
                    act.wait_ge(s_turn, v.t + 1)
                    nc.scalar.activation(slot_hi(v.t), ps_t[v.buf(2)][:, :], ACT.Copy,
                                         scale=SCALE_LN).then_inc(s_hi, 1)

                def store(v):
                    b = v.buf(4)
                    act.wait_ge(s_h4, v.t + 1)
                    act.dma_start(rows(x3_d, v.t), x2[b][0:rows_of(v.t), :]).then_inc(x_out[b], 16)
                pipeline(act, NT, (5, store), (5, hi), (3, y_normed), (0, lambda v: mish.exp(act, v)), (4, next_rows),
                         (0, lambda v: mish.inverse(act, v)), (1, u_parts))
                for b in range(4):
                    act.wait_ge(x_out[b], 16 * ((NT + 3 - b) // 4))

            @block.tensor
            def _(pe):
                pe.wait_ge(s_ones, 1)
                pe.wait_ge(s_w, 128)

                def update(v):
                    wait_count(pe, s_r, v.t - 1)
                    product(pe, ps_z[v.buf(2)][:, :], lambda c: slots16[:, bass.ds(v.t * 2 * D + c * P, P)],
                            lambda c: slots16[:, bass.ds(v.t * 2 * D + D + c * P, P)], w3, D).then_inc(s_mm, 1)

                def turn_u(v):
                    pe.wait_ge(mish.s_u, v.t + 1)
                    wait_count(pe, s_uT, v.t)
                    transposes(pe, ps_u, mish.c[v.buf(2)]).then_inc(s_ut, 1)

                def second(v):
                    b = v.buf(2)
                    wait_count(pe, s_yn, v.t - 1)
                    nc.tensor.matmul(ps_o[b][:, :], ones3[:, :], b4_rows[:, :], start=True, stop=False)
                    for part in range(2):
                        for c in range(C):
                            nc.tensor.matmul(ps_o[b][:, c * P:(c + 1) * P],
                                             slots16[:, bass.ds(v.t * 2 * D + part * D + c * P, P)],
                                             unscale[:, :], start=False, stop=False)
                    pe.wait_ge(s_uT, v.t + 1)
                    for c in range(C):
                        ins = nc.tensor.matmul(ps_o[b][:, :], uT[:, c * P:(c + 1) * P],
                                               w4[:, c * D:(c + 1) * D], start=False, stop=c == C - 1)
                    ins.then_inc(s_mm4, 1)

                def turn(v):
                    pe.wait_ge(s_h4, v.t + 1)
                    wait_count(pe, s_lo, v.t - 1)
                    transposes(pe, ps_t[v.buf(2)], h4).then_inc(s_turn, 1)
                pipeline(pe, NT, (0, update), (2, second), (1, turn_u), (4, turn))

    def batch_rows(pilot, w, shiftb, sum1, sum2):
        phase = "zp" if pilot else "z"
        with ExitStack() as ctx:
            g = [sb(ctx, f"{phase}_g{b}", [P, D]) for b in range(2)]
            sq = [sb(ctx, f"{phase}_sq{b}", [P, D]) for b in range(2)]
            ones = sb(ctx, f"{phase}_ones", [P, P])
            f = sb(ctx, f"{phase}_f", [P, 1])
            ps_z = [ps(ctx, f"{phase}_ps_z{b}") for b in range(2)]
            ps_m = ps(ctx, f"{phase}_ps_m")
            s_f, s_mm, s_bias, s_z, s_sq, s_s1, s_s2, s_mean = sems(
                phase, "f mm bias z sq s1 s2 mean")
            g_in = pair(phase, "gin")
            nt = 1 if pilot else NT
            u_no = unit_no["root"]
            zrow = (lambda t: sq[0][:, :]) if pilot else slot
            block = ctx.enter_context(nc.Block())

            @block.sync
            def _(sp):
                if pilot:
                    sp.dma_start(g[0][:, :], rows(agg_d, 0)).then_inc(g_in[0], 16)
                    return

                def body(t, k, b):
                    wait_count(sp, s_z, t - 1)
                    sp.dma_start(g[b][0:rows_of(t), :], rows(agg_d, t)).then_inc(g_in[b], 16)
                each_tile(sp, NT, body)

            @block.gpsimd
            def _(pool):
                if pilot:
                    nc.gpsimd.memset(ones[:, :], 1.0 / P).then_inc(s_mean, 1)
                    pool.wait_ge(g_in[0], 16)
                    nc.gpsimd.tensor_tensor(out=g[0][:, :], in0=g[0][:, :], in1=shiftb[:, :], op=ADD)\
                        .then_inc(s_bias, 1)
                    return

                def body(t, k, b):
                    pool.wait_ge(g_in[b], 16 * (k + 1))
                    nc.gpsimd.tensor_tensor(out=g[b][:, :], in0=g[b][:, :], in1=shiftb[:, :], op=ADD)\
                        .then_inc(s_bias, 1)
                each_tile(pool, NT, body)

            @block.vector
            def _(dve):
                nc.vector.tensor_scalar(out=f[:, :], in0=down[:, u_no:u_no + 1], scalar1=1.0 / SCALE_LN,
                                        scalar2=None, op0=MUL).then_inc(s_f, 1)
                dve.wait_ge(s_f, 1)

                def z_of(t, k, b):
                    dve.wait_ge(s_mm, t + 1)
                    dve.wait_ge(s_bias, t + 1)
                    nc.vector.scalar_tensor_tensor(out=zrow(t), in0=ps_z[b][:, :], scalar=f[:, 0:1],
                                                   in1=g[b][:, :], op0=MUL, op1=ADD).then_inc(s_z, 1)
                if pilot:
                    z_of(0, 0, 0)
                    dve.wait_ge(s_mean, 2)
                    nc.vector.tensor_tensor(out=shiftb[:, :], in0=shiftb[:, :], in1=ps_m[:, :], op=SUB)\
                        .then_inc(s_s1, 1)
                    dve.wait_ge(s_s1, 1)
                    return
                nc.vector.memset(sum1[:, :], 0.0)
                nc.vector.memset(sum2[:, :], 0.0).then_inc(s_f, 1)
                dve.wait_ge(s_f, 2)

                def squares(t, k, b):
                    n = rows_of(t)
                    dve.wait_ge(s_sq, t + 1)
                    wait_count(dve, s_s2, t)
                    nc.vector.tensor_tensor(out=sum2[0:n, :], in0=sum2[0:n, :], in1=sq[b][0:n, :], op=ADD)\
                        .then_inc(s_s2, 1)

                def body(t, k, b):
                    n = rows_of(t)
                    z_of(t, k, b)
                    if started(1, t):
                        squares(*ago(1, t, k, b))
                    dve.wait_ge(s_z, t + 1)
                    wait_count(dve, s_s1, t)
                    nc.vector.tensor_tensor(out=sum1[0:n, :], in0=sum1[0:n, :], in1=slot(t)[0:n, :], op=ADD)\
                        .then_inc(s_s1, 1)
                each_tile(dve, NT, body)
                squares(*last(NT, 1)[0])

            @block.scalar
            def _(act):
                if pilot:
                    return

                def body(t, k, b):
                    act.wait_ge(s_z, t + 1)
                    wait_count(act, s_s2, t - 1)
                    nc.scalar.activation(sq[b][:, :], slot(t), ACT.Square).then_inc(s_sq, 1)
                each_tile(act, NT, body)

            @block.tensor
            def _(pe):
                def body(t, k, b):
                    wait_count(pe, s_z, t - 1)
                    product(pe, ps_z[b][:, :], lambda c: slots16[:, bass.ds(t * 2 * D + c * P, P)],
                            lambda c: slots16[:, bass.ds(t * 2 * D + D + c * P, P)], w, D).then_inc(s_mm, 1)
                if pilot:
                    body(0, 0, 0)
                    pe.wait_ge(s_z, 1)
                    pe.wait_ge(s_mean, 1)
                    nc.tensor.matmul(ps_m[:, :], ones[:, :], sq[0][:, :], start=True, stop=True).then_inc(s_mean, 1)
                else:
                    each_tile(pe, NT, body)

    def finish(sum1, sum2):
        with ExitStack() as ctx:
            ones = sb(ctx, "f_ones", [P, P])
            gam, bet, mean, var, a_row, b_row, step = (
                sb(ctx, f"f_{n}", [P, D]) for n in ("gam", "bet", "mean", "var", "a", "b", "step"))
            x3 = [sb(ctx, f"f_x{b}", [P, D]) for b in range(4)]
            rows_out = [sb(ctx, f"f_o{b}", [P, D]) for b in range(4)]
            ps_1, ps_2 = ps(ctx, "f_ps_1"), ps(ctx, "f_ps_2")
            s_w, s_mm, s_v, s_p, s_n, s_coef, s_za, s_zb, s_o, s_mem = sems("f", "w mm v p n coef za zb o mem")
            x_in = [sem(f"f_in{b}") for b in range(4)]
            o_out = [sem(f"f_out{b}") for b in range(4)]
            block = ctx.enter_context(nc.Block())

            @block.sync
            def _(sp):
                def load(v):
                    b = v.buf(4)
                    wait_count(sp, s_o, v.t - 3)
                    sp.dma_start(x3[b][0:rows_of(v.t), :], rows(x3_d, v.t)).then_inc(x_in[b], 16)
                sp.dma_start(gam[:, :], wide(gamma3)).then_inc(s_w, 16)
                sp.dma_start(bet[:, :], wide(beta3)).then_inc(s_w, 16)
                pipeline(sp, NT, (0, load))

            @block.scalar
            def _(act):
                act.wait_ge(s_v, 4)
                nc.scalar.activation(a_row[:, :], var[:, :], ACT.Ln).then_inc(s_p, 1)
                act.wait_ge(s_p, 1)
                nc.scalar.activation(a_row[:, :], a_row[:, :], ACT.Exp, scale=-0.5).then_inc(s_p, 1)

                def store(v):
                    b = v.buf(4)
                    act.wait_ge(s_o, v.t + 1)
                    act.dma_start(rows(out, v.t), rows_out[b][0:rows_of(v.t), :]).then_inc(o_out[b], 16)
                pipeline(act, NT, (0, store))
                for b in range(4):
                    act.wait_ge(o_out[b], 16 * ((NT - b + 3) // 4))

            @block.tensor
            def _(pe):
                pe.wait_ge(s_mem, 1)
                nc.tensor.matmul(ps_1[:, :], ones[:, :], sum1[:, :], start=True, stop=True)
                nc.tensor.matmul(ps_2[:, :], ones[:, :], sum2[:, :], start=True, stop=True).then_inc(s_mm, 1)

            @block.gpsimd
            def _(pool):
                nc.gpsimd.memset(ones[:, :], 1.0).then_inc(s_mem, 1)
                pool.wait_ge(s_coef, 2)

                def times_a(v):
                    nc.gpsimd.tensor_tensor(out=slot(v.t), in0=slot(v.t), in1=a_row[:, :], op=MUL)\
                        .then_inc(s_za, 1)
                pipeline(pool, NT, (0, times_a))

            @block.vector
            def _(dve):
                dve.wait_ge(s_mm, 1)
                dve.wait_ge(s_w, 32)
                nc.vector.tensor_scalar(out=mean[:, :], in0=ps_1[:, :], scalar1=1.0 / N, scalar2=None,
                                        op0=MUL).then_inc(s_v, 1)
                dve.wait_ge(s_v, 1)
                nc.vector.tensor_tensor(out=b_row[:, :], in0=mean[:, :], in1=mean[:, :], op=MUL).then_inc(s_v, 1)
                dve.wait_ge(s_v, 2)
                nc.vector.scalar_tensor_tensor(out=var[:, :], in0=ps_2[:, :], scalar=1.0 / N, in1=b_row[:, :],
                                               op0=MUL, op1=SUB).then_inc(s_v, 1)
                dve.wait_ge(s_v, 3)
                nc.vector.tensor_scalar(out=var[:, :], in0=var[:, :], scalar1=0.0, scalar2=BN_EPS,
                                        op0=MAX, op1=ADD).then_inc(s_v, 1)
                dve.wait_ge(s_p, 2)
                nc.vector.tensor_tensor(out=step[:, :], in0=a_row[:, :], in1=a_row[:, :], op=MUL).then_inc(s_n, 1)
                dve.wait_ge(s_n, 1)
                nc.vector.tensor_tensor(out=step[:, :], in0=step[:, :], in1=var[:, :], op=MUL).then_inc(s_n, 1)
                dve.wait_ge(s_n, 2)
                nc.vector.tensor_scalar(out=step[:, :], in0=step[:, :], scalar1=-0.5, scalar2=1.5,
                                        op0=MUL, op1=ADD).then_inc(s_n, 1)
                dve.wait_ge(s_n, 3)
                nc.vector.tensor_tensor(out=a_row[:, :], in0=a_row[:, :], in1=step[:, :], op=MUL).then_inc(s_n, 1)
                dve.wait_ge(s_n, 4)
                nc.vector.tensor_tensor(out=a_row[:, :], in0=a_row[:, :], in1=gam[:, :], op=MUL).then_inc(s_coef, 1)
                dve.wait_ge(s_coef, 1)
                nc.vector.tensor_tensor(out=b_row[:, :], in0=mean[:, :], in1=a_row[:, :], op=MUL).then_inc(s_v, 1)
                dve.wait_ge(s_v, 5)
                nc.vector.tensor_tensor(out=b_row[:, :], in0=bet[:, :], in1=b_row[:, :], op=SUB).then_inc(s_coef, 1)
                dve.wait_ge(s_coef, 2)

                def plus_b(v):
                    dve.wait_ge(s_za, v.t + 1)
                    nc.vector.tensor_tensor(out=slot(v.t), in0=slot(v.t), in1=b_row[:, :], op=ADD).then_inc(s_zb, 1)

                def add_up(v):
                    b = v.buf(4)
                    dve.wait_ge(s_zb, v.t + 1)
                    dve.wait_ge(x_in[b], 16 * (v.uses(4) + 1))
                    wait_count(dve, o_out[b], 16 * v.uses(4))
                    nc.vector.scalar_tensor_tensor(out=rows_out[b][:, :], in0=slot(v.t), scalar=0.0,
                                                   in1=x3[b][:, :], op0=MAX, op1=ADD).then_inc(s_o, 1)
                pipeline(dve, NT, (0, plus_b), (1, add_up))

    prepare()
    gcn_project()
    edge_sums_gcn()
    gcn_finish()
    recycle_semaphores()
    for l, source in enumerate((x1_d, h_d, h_d)):
        with ExitStack() as layer:
            w_self = sb(layer, f"w_self{l}", [P, 2 * cols[f"self{l}"]], F16)
            b_self = sb(layer, f"b_self{l}", [P, D])
            edge_products(f"a{l}", source, l == 0, SCALE_UNIT if l else SCALE_LN, f"neigh{l}",
                          [(w_self[:, :], split_d[f"self{l}"][:, :]), (b_self[:, :], wide(bsage[l]))])
            sage_layer(l, w_self, b_self)
    recycle_semaphores()
    edge_hidden()
    edge_messages()
    node_update()
    recycle_semaphores()
    shiftb, sum1, sum2 = (sb(top, n, [P, D]) for n in ("shiftb", "sum1", "sum2"))
    with ExitStack() as layer:
        w_root = sb(layer, "w_root", [P, 2 * cols["root"]], F16)
        edge_products("a4", x3_d, True, SCALE_LN, "aggr",
                      [(w_root[:, :], split_d["root"][:, :]), (shiftb[:, :], wide(bl))])
        batch_rows(True, w_root, shiftb, sum1, sum2)
        batch_rows(False, w_root, shiftb, sum1, sum2)
    finish(sum1, sum2)
    top.close()


_INS = ["x", "src", "dst", "edge_attr_64", "L0_gnn_W_conv", "L0_gnn_b_conv", "L0_gnn_W_lin", "L0_gnn_b_lin",
        "L1_gnn_W_self", "L1_gnn_W_neigh", "L1_gnn_b", "L2_gnn_W1", "L2_gnn_b1", "L2_gnn_W2", "L2_gnn_b2",
        "L2_gnn_W3", "L2_gnn_b3", "L2_gnn_W4", "L2_gnn_b4", "L2_gnn_gamma", "L2_gnn_beta",
        "L3_gnn_W_l", "L3_gnn_b_l", "L3_gnn_W_r", "L3_gnn_gamma", "L3_gnn_beta"]


def kernel(**inputs):
    import numpy as _np
    import concourse.bacc as _bacc
    from concourse import mybir as _mybir
    from concourse.bass_utils import run_bass_kernel_spmd as _run

    nc = _bacc.Bacc("TRN2", target_bir_lowering=False, num_devices=1)
    arrays, args = {}, []
    for name in _INS:
        a = _np.asarray(inputs[name])
        if name in ("L3_gnn_W_l", "L3_gnn_W_r"):
            a = a.T
        a = _np.ascontiguousarray(a)
        arrays[f"in_{name}"] = a
        args.append(nc.dram_tensor(f"in_{name}", a.shape, _mybir.dt.from_np(a.dtype), kind="ExternalInput").ap())
    out = nc.dram_tensor("out_rows", (N, D), F32, kind="ExternalOutput").ap()
    gnn_program(nc, *args, out)
    r = _run(nc, [arrays], core_ids=[0])
    return r.results[0]["out_rows"]
```
